# Optimizing a Trainium2 kernel written in Bass

```python
import numpy as np
import jax
import jax.numpy as jnp

def _softmax(x, axis=-1):
    return jax.nn.softmax(x, axis=axis)

def _gelu(x):
    return jax.nn.gelu(x, approximate=True)

def _silu(x):
    return jax.nn.silu(x)

def _sigmoid(x):
    return jax.nn.sigmoid(x)

def _layernorm(x, axis=-1, eps=1e-05):
    m = jnp.mean(x, axis=axis, keepdims=True)
    v = jnp.var(x, axis=axis, keepdims=True)
    return (x - m) / jnp.sqrt(v + eps)

def _scatter_add(tgt, idx, src, axis=0):
    return tgt.at[idx].add(src)

def _segment_sum(src, seg, n):
    return jax.ops.segment_sum(src, seg, n)
kernel_name = 'mk_prb_d2_jaxref_r8_dec247'

def setup_inputs(seed: int=0):
    np.random.seed(seed)
    _w = jnp.asarray

    def _L0_attn_setup():
        import jax, jax.numpy as jnp
        import numpy as np
        E2M1_GRID = jnp.array([0.0, 0.5, 1.0, 1.5, 2.0, 3.0, 4.0, 6.0], dtype=jnp.float32)
        E2M1_MIDS = (E2M1_GRID[1:] + E2M1_GRID[:-1]) / 2.0
        FP4_MAX = 6.0
        FP8_E4M3_MAX = 448.0

        def nvfp4_quant_dequant(w):
            O, I = w.shape
            w16 = w.reshape(O, I // 128, 8, 16)
            amax128 = jnp.max(jnp.abs(w16), axis=(-2, -1))
            outer = amax128 / (FP4_MAX * FP8_E4M3_MAX)
            outer = jnp.where(outer > 0, outer, 1.0)
            amax16 = jnp.max(jnp.abs(w16), axis=-1)
            inner = amax16 / FP4_MAX / outer[..., None]
            inner = inner.astype(jnp.float8_e4m3fn).astype(jnp.float32)
            scale = outer[..., None] * inner
            safe = jnp.where(scale > 0, scale, 1.0)[..., None]
            code = w16 / safe
            a = jnp.abs(code)
            idx = jnp.searchsorted(E2M1_MIDS, a)
            q = E2M1_GRID[idx] * jnp.sign(code)
            return (q * scale[..., None]).reshape(O, I)
        key = jax.random.key(seed)
        k0, k1, k2 = jax.random.split(key, 3)
        B, S, H = (2, 256, 256)
        hidden_states = jax.random.normal(k0, (B, S, H), dtype=jnp.float32)
        w_qkv = jax.random.normal(k1, (3 * H, H), dtype=jnp.float32) * 0.023
        w_o = jax.random.normal(k2, (H, H), dtype=jnp.float32) * 0.023
        w_qkv = nvfp4_quant_dequant(w_qkv)
        w_o = nvfp4_quant_dequant(w_o)
        return {'hidden_states': hidden_states, 'w_qkv': w_qkv, 'w_o': w_o}
    _L0_attn_in = _L0_attn_setup()

    def _L0_ffn_setup():
        import jax, jax.numpy as jnp
        import numpy as np
        TOP_K = 2
        key = jax.random.key(seed)
        k0, k1, k2, k3 = jax.random.split(key, 4)
        B, S, D, E, H = (4, 128, 256, 16, 128)
        x = jax.random.normal(k0, (B, S, D), jnp.float32) * 0.02
        Wg = jax.random.normal(k1, (E, D), jnp.float32) * 0.02
        balance_bias = jnp.zeros((E,), jnp.float32)
        W1 = jax.random.normal(k2, (E, D, H), jnp.float32) * 0.02
        W2 = jax.random.normal(k3, (E, H, D), jnp.float32) * 0.02
        return {'x': x, 'Wg': Wg, 'balance_bias': balance_bias, 'W1': W1, 'W2': W2}
    _L0_ffn_in = _L0_ffn_setup()

    def _L1_attn_setup():
        import jax, jax.numpy as jnp
        import numpy as np
        D_MODEL = 256
        key = jax.random.key(seed)
        kx, kw, kb = jax.random.split(key, 3)
        B, T, D = (4, 512, D_MODEL)
        x = jax.random.normal(kx, (B, T, D), dtype=jnp.float32)
        scale = 1.0 / np.sqrt(D)
        W = jax.random.uniform(kw, (D, 3 * D), dtype=jnp.float32, minval=-scale, maxval=scale)
        b = jax.random.uniform(kb, (3 * D,), dtype=jnp.float32, minval=-scale, maxval=scale)
        return {'x': x, 'W': W, 'b': b}
    _L1_attn_in = _L1_attn_setup()

    def _L1_ffn_setup():
        import jax, jax.numpy as jnp
        import numpy as np
        TOP_K = 4
        key = jax.random.key(seed)
        ks = jax.random.split(key, 8)
        B, S, D, E, H, HS = (2, 256, 256, 16, 128, 512)
        scaled = lambda k, shape, fan: jax.random.normal(k, shape, jnp.float32) * fan ** (-0.5)
        return {'x': jax.random.normal(ks[0], (B, S, D), jnp.float32), 'w_router': scaled(ks[1], (D, E), D), 'we1': scaled(ks[2], (E, D, H), D), 'we3': scaled(ks[3], (E, D, H), D), 'we2': scaled(ks[4], (E, H, D), H), 'ws1': scaled(ks[5], (D, HS), D), 'ws3': scaled(ks[6], (D, HS), D), 'ws2': scaled(ks[7], (HS, D), HS)}
    _L1_ffn_in = _L1_ffn_setup()
    _d = {'L0_attn_hidden_states': _L0_attn_in['hidden_states'], 'L0_attn_w_qkv': _L0_attn_in['w_qkv'], 'L0_attn_w_o': _L0_attn_in['w_o'], 'L0_ffn_Wg': _L0_ffn_in['Wg'], 'L0_ffn_balance_bias': _L0_ffn_in['balance_bias'], 'L0_ffn_W1': _L0_ffn_in['W1'], 'L0_ffn_W2': _L0_ffn_in['W2'], 'L1_attn_W': _L1_attn_in['W'], 'L1_attn_b': _L1_attn_in['b'], 'L1_ffn_w_router': _L1_ffn_in['w_router'], 'L1_ffn_we1': _L1_ffn_in['we1'], 'L1_ffn_we3': _L1_ffn_in['we3'], 'L1_ffn_we2': _L1_ffn_in['we2'], 'L1_ffn_ws1': _L1_ffn_in['ws1'], 'L1_ffn_ws3': _L1_ffn_in['ws3'], 'L1_ffn_ws2': _L1_ffn_in['ws2']}
    _x0 = _d['L0_attn_hidden_states']
    _d['L0_attn_hidden_states'] = jax.random.normal(jax.random.fold_in(jax.random.key(seed), 1), (1, 2048, 256), dtype=_x0.dtype)
    del _x0
    return _d

def reference(L0_attn_hidden_states, L0_attn_w_qkv, L0_attn_w_o, L0_ffn_Wg, L0_ffn_balance_bias, L0_ffn_W1, L0_ffn_W2, L1_attn_W, L1_attn_b, L1_ffn_w_router, L1_ffn_we1, L1_ffn_we3, L1_ffn_we2, L1_ffn_ws1, L1_ffn_ws3, L1_ffn_ws2):

    def _L0_attn_ref(hidden_states, w_qkv, w_o):
        import jax, jax.numpy as jnp
        import numpy as np
        E2M1_GRID = jnp.array([0.0, 0.5, 1.0, 1.5, 2.0, 3.0, 4.0, 6.0], dtype=jnp.float32)
        E2M1_MIDS = (E2M1_GRID[1:] + E2M1_GRID[:-1]) / 2.0
        FP4_MAX = 6.0
        FP8_E4M3_MAX = 448.0

        def nvfp4_quant_dequant(w):
            O, I = w.shape
            w16 = w.reshape(O, I // 128, 8, 16)
            amax128 = jnp.max(jnp.abs(w16), axis=(-2, -1))
            outer = amax128 / (FP4_MAX * FP8_E4M3_MAX)
            outer = jnp.where(outer > 0, outer, 1.0)
            amax16 = jnp.max(jnp.abs(w16), axis=-1)
            inner = amax16 / FP4_MAX / outer[..., None]
            inner = inner.astype(jnp.float8_e4m3fn).astype(jnp.float32)
            scale = outer[..., None] * inner
            safe = jnp.where(scale > 0, scale, 1.0)[..., None]
            code = w16 / safe
            a = jnp.abs(code)
            idx = jnp.searchsorted(E2M1_MIDS, a)
            q = E2M1_GRID[idx] * jnp.sign(code)
            return (q * scale[..., None]).reshape(O, I)
        B, S, H = hidden_states.shape
        num_heads = 16
        head_dim = H // num_heads
        qkv = jnp.einsum('bsh,oh->bso', hidden_states, w_qkv)
        qkv = qkv.reshape(B, S, 3, num_heads, head_dim)
        qkv = jnp.transpose(qkv, (2, 0, 3, 1, 4))
        q, k, v = (qkv[0], qkv[1], qkv[2])
        scale = 1.0 / jnp.sqrt(jnp.float32(head_dim))
        scores = jnp.einsum('bhqd,bhkd->bhqk', q, k) * scale
        causal = jnp.tril(jnp.ones((S, S), dtype=bool))
        scores = jnp.where(causal, scores, jnp.finfo(scores.dtype).min)
        probs = jax.nn.softmax(scores, axis=-1)
        attn = jnp.einsum('bhqk,bhkd->bhqd', probs, v)
        attn = jnp.transpose(attn, (0, 2, 1, 3)).reshape(B, S, H)
        return jnp.einsum('bsh,oh->bso', attn, w_o)

    def _L0_ffn_ref(x, Wg, balance_bias, W1, W2):
        import jax, jax.numpy as jnp
        import numpy as np
        TOP_K = 2
        B, S, D = x.shape
        E = Wg.shape[0]
        xf = x.reshape(-1, D)
        T = xf.shape[0]
        gate_logits = xf @ Wg.T
        gate_scores = jax.nn.sigmoid(gate_logits + balance_bias)
        topk_scores, topk_idx = jax.lax.top_k(gate_scores, TOP_K)
        topk_scores = topk_scores / (topk_scores.sum(-1, keepdims=True) + 1e-06)
        combine = jnp.zeros((T, E), xf.dtype).at[jnp.arange(T)[:, None], topk_idx].add(topk_scores)
        h = jax.nn.silu(jnp.einsum('td,edh->teh', xf, W1))
        out = jnp.einsum('teh,te,ehd->td', h, combine, W2)
        return out.reshape(B, S, D)

    def _L1_attn_ref(x, W, b):
        import jax, jax.numpy as jnp
        import numpy as np
        D_MODEL = 256
        qkv = x @ W + b
        q, k, v = jnp.split(qkv, 3, axis=-1)
        qn = q / jnp.linalg.norm(q, axis=1, keepdims=True)
        kn = k / jnp.linalg.norm(k, axis=1, keepdims=True)
        kv = jnp.sum(kn * v, axis=1, keepdims=True)
        return qn * kv

    def _L1_ffn_ref(x, w_router, we1, we3, we2, ws1, ws3, ws2):
        import jax, jax.numpy as jnp
        import numpy as np
        TOP_K = 4
        B, S, D = x.shape
        T = B * S
        E = w_router.shape[1]
        xt = x.reshape(T, D)
        probs = jax.nn.softmax(xt @ w_router, axis=-1)
        top_w, top_i = jax.lax.top_k(probs, TOP_K)
        top_w = top_w / jnp.sum(top_w, axis=-1, keepdims=True)
        cw = jnp.zeros((T, E), xt.dtype).at[jnp.arange(T)[:, None], top_i].add(top_w)
        g = jax.nn.silu(jnp.einsum('td,edh->teh', xt, we1)) * jnp.einsum('td,edh->teh', xt, we3)
        g = g * cw[:, :, None]
        moe_out = jnp.einsum('teh,ehd->td', g, we2)
        shared = jax.nn.silu(xt @ ws1) * (xt @ ws3) @ ws2
        k = TOP_K
        out = shared / (k + 1) + moe_out * (k / (k + 1))
        return out.reshape(B, S, D)
    x = L0_attn_hidden_states
    xn = _layernorm(x, axis=-1)
    x = x + _L0_attn_ref(xn, L0_attn_w_qkv, L0_attn_w_o) + _L0_ffn_ref(xn, L0_ffn_Wg, L0_ffn_balance_bias, L0_ffn_W1, L0_ffn_W2)
    xn = _layernorm(x, axis=-1)
    x = x + _L1_attn_ref(xn, L1_attn_W, L1_attn_b) + _L1_ffn_ref(xn, L1_ffn_w_router, L1_ffn_we1, L1_ffn_we3, L1_ffn_we2, L1_ffn_ws1, L1_ffn_ws3, L1_ffn_ws2)
    return x

_drawn_inputs = setup_inputs


def setup_inputs(seed=0):
    import zlib

    import numpy as np

    out = dict(_drawn_inputs(seed))
    spreads = {'L0_ffn_balance_bias': (0.0, 1.703)}
    factors = {'L0_attn_w_qkv': 4.097,
     'L0_attn_w_o': 4.103,
     'L1_attn_b': 8.0,
     'L0_ffn_Wg': 4.732,
     'L0_ffn_W1': 3.829,
     'L0_ffn_W2': 3.702}
    for name, (base, spread) in spreads.items():
        noise = np.random.default_rng([zlib.crc32(name.encode()), seed]).standard_normal(out[name].shape)
        drawn = base * np.exp(spread * noise) if base else spread * noise
        out[name] = jnp.asarray(drawn.astype(out[name].dtype))
    for name, factor in factors.items():
        out[name] = (out[name] * factor).astype(out[name].dtype)
    return out
```

```python
from contextlib import ExitStack

import concourse.bass as bass
from concourse import mybir

ALU = mybir.AluOpType
ACT = mybir.ActivationFunctionType
F32 = mybir.dt.float32
BF16 = mybir.dt.bfloat16
I32 = mybir.dt.int32
U32 = mybir.dt.uint32
AX_X = mybir.AxisListType.X

P = 128
S = 2048
D = 256
T = S // P
KH = D // P
CH = 512
C = S // CH
TC = CH // P
NH = 16
HD = D // NH
HG = 4
NG = NH // HG
E = 16
HID = 128
HS = 512
TOP0, TOP1 = 2, 4
NT0 = S * TOP0 // P + E - 1
NT1 = S * TOP1 // P + E - 1
EPS = 1e-5
NEG = -1e30
PARTS = 3
Q_PART = [0, 0, 0, 1, 1, 2]
K_PART = [0, 1, 2, 0, 1, 0]
TERMS = len(Q_PART)
KROWS = TERMS * HD
MDMA = PARTS
MROWS = KROWS + PARTS


class Steps:

    def __init__(self, eng, sem):
        self.eng, self.sem, self.n = eng, sem, 0

    def __call__(self, instruction):
        instruction.then_inc(self.sem, 1)
        self.n += 1

    def sync(self):
        self.eng.wait_ge(self.sem, self.n)

    def then(self, instruction):
        self(instruction)
        self.sync()


class Memory:

    def __init__(self, nc, ctx):
        self.nc, self.ctx = nc, ctx

    def sb(self, name, shape, dt=F32):
        return self.ctx.enter_context(self.nc.sbuf_tensor(name, shape, dt))

    def ps(self, name, shape, dt=F32):
        return self.ctx.enter_context(self.nc.psum_tensor(name, shape, dt))

    def sem(self, name):
        return self.ctx.enter_context(self.nc.semaphore(name))

    def scratch(self, name, shape, dt=F32):
        return self.nc.dram_tensor(name, shape, dt, kind="Internal").ap()


def norm_chunk(dve, step, x, xn, stat, c, std_wanted, std_ready):
    mv, var, std, tmp = stat["mv"], stat["var"], stat["std"], stat["tmp"]
    tiles = range(c * TC, (c + 1) * TC)
    cs = slice(c * TC, (c + 1) * TC)
    for i in tiles:
        step(dve.bn_stats(stat["bn"][:, i, :], x[:, i, :]))
    step.sync()
    for i in tiles:
        step(dve.bn_aggr(mv[:, i, :], stat["bn"][:, i, :]))
    step.sync()
    dve.tensor_scalar(var[:, cs], mv[:, cs, 1], EPS, None, ALU.add).then_inc(std_wanted, 1)
    dve.wait_ge(std_wanted, c + 1)
    dve.wait_ge(std_ready, c + 1)
    step.then(dve.reciprocal(std[:, cs], std[:, cs]))
    step.then(dve.tensor_tensor(tmp[:, cs], std[:, cs], std[:, cs], ALU.mult))
    step.then(dve.tensor_tensor(tmp[:, cs], tmp[:, cs], var[:, cs], ALU.mult))
    step.then(dve.tensor_scalar(tmp[:, cs], tmp[:, cs], -0.5, 1.5, ALU.mult, ALU.add))
    step.then(dve.tensor_tensor(std[:, cs], std[:, cs], tmp[:, cs], ALU.mult))
    for i in tiles:
        step(dve.tensor_scalar(xn[:, i, 0:D], x[:, i, :], mv[:, i, 0:1], std[:, i:i + 1],
                               ALU.subtract, ALU.mult))


def route(dve, step, r, scores, top, tiles, eps, factor, masks_ready, ranks_ready, slots_ready):
    best, arg, argf = r["best"], r["arg"], r["argf"]
    for i in range(T):
        step(dve.max(best[:, i, :], scores[:, i, :]))
    step.sync()
    for i in range(T):
        step(dve.max_index(arg[:, i, :], best[:, i, :], scores[:, i, :]))
    step.sync()
    step.then(dve.tensor_copy(argf[:, :, :], arg[:, :, :]))
    for k in range(top):
        step(dve.tensor_tensor(r["hot"][:, k, :, :], argf[:, :, k:k + 1].to_broadcast([P, T, E]),
                               r["iota_e"][:, 0:1, :].to_broadcast([P, T, E]), ALU.is_equal))
    step.sync()
    step.then(dve.tensor_tensor(r["any"][:, :, :], r["hot"][:, 0, :, :], r["hot"][:, 1, :, :], ALU.add))
    for k in range(2, top):
        step.then(dve.tensor_tensor(r["any"][:, :, :], r["any"][:, :, :], r["hot"][:, k, :, :], ALU.add))
    dve.tensor_copy(r["any16"][:, :, :], r["any"][:, :, :]).then_inc(masks_ready, 1)
    step.then(dve.tensor_reduce(r["sum"][:, :], best[:, :, 0:top], AX_X, ALU.add))
    if eps:
        step.then(dve.tensor_scalar(r["sum"][:, :], r["sum"][:, :], eps, None, ALU.add))
    step.then(dve.reciprocal(r["sum"][:, :], r["sum"][:, :]))
    step(dve.scalar_tensor_tensor(r["weight"][:, :, 0:top], best[:, :, 0:top], factor,
                                  r["sum"][:, :].unsqueeze(2).to_broadcast([P, T, top]), ALU.mult, ALU.mult))
    dve.wait_ge(ranks_ready, 1)
    count, before, total = r["count"], r["before"], r["total"]
    step.then(dve.tensor_copy(count[:, :, :], r["ps_count"].rearrange("p (i e) -> p e i", e=E)))
    step.then(dve.tensor_tensor_scan(before[:, :, :].rearrange("p e i -> p (e i)"),
                                     r["within"][:, :], count[:, :, :].rearrange("p e i -> p (e i)"),
                                     0.0, ALU.mult, ALU.add))
    step.then(dve.tensor_scalar(total[:, :], before[:, :, T - 1], float(P - 1), None, ALU.add))
    step.then(dve.tensor_copy(r["total_i"][:, :], total[:, :]))
    step.then(dve.tensor_scalar(r["total_i"][:, :], r["total_i"][:, :], 7, None, ALU.arith_shift_right))
    step.then(dve.tensor_copy(total[:, :], r["total_i"][:, :]))
    step.then(dve.tensor_tensor_scan(r["end"][:, :], r["ones_e"][:, :], total[:, :], 0.0, ALU.mult, ALU.add))
    step.then(dve.tensor_tensor(total[:, :], r["end"][:, :], total[:, :], ALU.subtract))
    step.then(dve.tensor_scalar(total[:, :], total[:, :], float(P), None, ALU.mult))
    step.then(dve.tensor_tensor(before[:, :, :], before[:, :, :], count[:, :, :], ALU.subtract))
    step.then(dve.tensor_tensor(before[:, :, :], before[:, :, :],
                                total[:, :].unsqueeze(2).to_broadcast([P, E, T]), ALU.add))
    step.then(dve.tensor_tensor(count[:, :, :], r["ps_rank"].rearrange("p (i e) -> p e i", e=E),
                                before[:, :, :], ALU.add))
    for k in range(top):
        step.then(dve.tensor_tensor(r["any"][:, :, :], r["hot"][:, k, :, :],
                                    count[:, :, :].rearrange("p e i -> p i e"), ALU.mult))
        step.then(dve.tensor_reduce(r["slotf"][:, k, :], r["any"][:, :, :], AX_X, ALU.add))
    dve.tensor_copy(r["slot"][:, 0:top, :], r["slotf"][:, 0:top, :]).then_inc(slots_ready, 1)
    step.then(dve.tensor_tensor(r["ended"][:, 0:tiles, :], r["end"][0:1, :].unsqueeze(1).to_broadcast([1, tiles, E]),
                                r["iota_t"][0:1, 0:tiles].unsqueeze(2).to_broadcast([1, tiles, E]), ALU.is_le))
    step.then(dve.tensor_reduce(r["tilef"][:, 0:tiles], r["ended"][:, 0:tiles, :], AX_X, ALU.add))
    step.then(dve.tensor_scalar(r["tilef"][:, 0:tiles], r["tilef"][:, 0:tiles], float(E - 1), None, ALU.min))
    dve.tensor_copy(r["tile_e"][:, 0:tiles], r["tilef"][:, 0:tiles]).then_inc(slots_ready, 1)


def route_ranks(pe, r, masks_ready, ranks_ready):
    pe.wait_ge(masks_ready, 1)
    flat = r["any16"][:, :, :].rearrange("p i e -> p (i e)")
    pe.matmul(r["ps_rank"], r["before16"][:, :], flat, start=True, stop=True)
    pe.matmul(r["ps_count"], r["ones16"][:, :], flat, start=True, stop=True).then_inc(ranks_ready, 1)


def stage_project(nc, m, a):
    with ExitStack() as ctx:
        l = Memory(nc, ctx)
        wqkv = l.sb("wqkv", [P, KH, 3 * D])
        wg = l.sb("wg", [P, KH, E])
        xt = l.sb("xt", [P, KH, S])
        xn = l.sb("xn", [P, T, D])
        parts = l.sb("parts", [P, 2, PARTS, CH], BF16)
        rest = l.sb("rest", [P, 2, CH])
        bias = l.sb("bias", [P, E])
        scores = l.sb("scores", [P, T, E])
        zeros = l.sb("zeros", [P, 2048])
        ps_t = [l.ps(f"ps_t{b}", [P, KH, P]) for b in range(2)]
        ps_qk = [l.ps(f"ps_qk{b}", [P, CH]) for b in range(2)]
        ps_v = [l.ps(f"ps_v{b}", [P, D]) for b in range(2)]
        ps_l = l.ps("ps_l", [P, T, E])
        ps_r = l.ps("ps_r0", [P, 2, D])
        stat, r = m.stat, dict(m.r)
        r["ps_rank"], r["ps_count"] = ps_r[:, 0, :], ps_r[:, 1, :]

        x_in = [l.sem(f"a_x_in{c}") for c in range(C)]
        w_in = l.sem("a_w_in")
        g_in = l.sem("a_g_in")
        b_in = l.sem("a_b_in")
        std_wanted, std_ready = l.sem("a_std_wanted"), l.sem("a_std_ready")
        step_sem = l.sem("a_dve")
        xn_ready, t_done, xt_ready = l.sem("a_xn_ready"), l.sem("a_t_done"), l.sem("a_xt_ready")
        qk_done, high_ready, rest_ready = l.sem("a_qk_done"), l.sem("a_high_ready"), l.sem("a_rest_ready")
        mid_ready, low_ready = l.sem("a_mid_ready"), l.sem("a_low_ready")
        parts_out = [l.sem(f"a_parts_out{b}") for b in range(2)]
        v_done, v_copied = l.sem("a_v_done"), l.sem("a_v_copied")
        l_done, logit_ready, exp_ready = l.sem("a_l_done"), l.sem("a_logit_ready"), l.sem("a_exp_ready")
        masks_ready, ranks_ready = l.sem("a_masks_ready"), l.sem("a_ranks_ready")
        slots_ready = l.sem("a_slots_ready")
        pool_step, consts = l.sem("a_pool"), l.sem("a_consts")
        cleared, dispatched = l.sem("a_cleared"), l.sem("a_dispatched")
        zero_ready = l.sem("a_zero_ready")

        block = ctx.enter_context(nc.Block())

        @block.sync
        def _(sp):
            for c in range(C):
                sp.dma_start(m.x[:, c * TC:(c + 1) * TC, :],
                             a["x"][0, c * CH:(c + 1) * CH, :].rearrange("(i p) d -> p i d", p=P)).then_inc(x_in[c], 16)
            sp.wait_ge(zero_ready, 1)
            for buf, tiles in ((m.xd0, NT0), (m.xd1, NT1)):
                flat = buf.rearrange("(p j) d -> p (j d)", p=P)
                for at in range(0, tiles * D, 2048):
                    w = min(2048, tiles * D - at)
                    sp.dma_start(flat[:, at:at + w], zeros[:, 0:w]).then_inc(cleared, 16)
            for n in range(4 * C):
                c, o = n // 4, n % 4
                sp.wait_ge(low_ready, n + 1)
                sp.dma_start(m.qk_parts[:, o * P:(o + 1) * P, c * CH:(c + 1) * CH].rearrange("r p t -> p r t"),
                             parts[:, n % 2, :, :]).then_inc(parts_out[n % 2], 16)
            for b in range(2):
                sp.wait_ge(parts_out[b], 16 * 2 * C)

        @block.gpsimd
        def _(pool):
            step = Steps(pool, pool_step)
            step(pool.memset(zeros[:, :], 0.0))
            pool.memset(m.ident[:, :], 0.0).then_inc(pool_step, 1)
            step.n += 1
            step.sync()
            pool.memset(m.ones_f[:, :], 1.0).then_inc(zero_ready, 1)
            step(pool.affine_select(out=m.ident[:, :], in_=m.ident[:, :], compare_op=ALU.not_equal, fill=1.0,
                                    base=0, pattern=[[-1, P]], channel_multiplier=1))
            step(pool.iota(m.iota_i[:, 0:P], [[1, P]], base=0, channel_multiplier=0))
            pool.wait_ge(zero_ready, 1)
            step(pool.affine_select(out=m.before_f[:, :], in_=m.ones_f[:, :], compare_op=ALU.is_gt, fill=0.0,
                                    base=0, pattern=[[1, P]], channel_multiplier=-1))
            step(pool.affine_select(out=m.within[:, :].rearrange("p (e i) -> p e i", i=T),
                                    in_=m.ones_f[:, 0:1].unsqueeze(2).to_broadcast([P, E, T]),
                                    compare_op=ALU.is_gt, fill=0.0, base=0, pattern=[[0, E], [1, T]],
                                    channel_multiplier=0))
            step(pool.memset(m.v_all[:, :, :, :], 0.0))
            step.sync()
            step(pool.tensor_scalar(m.mask_f[:, :], m.before_f[:, :], NEG, None, ALU.mult))
            step(pool.memset(m.v_all[:, :, :, HD:HD + 1], 1.0))
            step.sync()
            pool.tensor_copy(m.iota_f[:, :], m.iota_i[:, :]).then_inc(consts, 1)
            for n in range(4 * C):
                pool.wait_ge(rest_ready, n + 1)
                pool.tensor_copy(parts[:, n % 2, 1, :], rest[:, n % 2, :]).then_inc(mid_ready, 1)
                pool.wait_ge(mid_ready, n + 1)
                pool.tensor_tensor(parts[:, n % 2, 2, :], rest[:, n % 2, :], parts[:, n % 2, 1, :],
                                   ALU.subtract).then_inc(low_ready, 1)
            pool.wait_ge(cleared, 16 * sum(-(-t * D // 2048) for t in (NT0, NT1)))
            pool.wait_ge(slots_ready, 1)
            for k in range(TOP0):
                for i in range(T):
                    pool.indirect_dma_start(out=m.xd0, out_offset=bass.IndirectOffsetOnAxis(r["slot"][:, k, i:i + 1], 0),
                                            in_=xn[:, i, :], in_offset=None).then_inc(dispatched, 16)
            pool.wait_ge(dispatched, 16 * TOP0 * T)

        @block.scalar
        def _(act):
            act.dma_start(wqkv[:, :, :], a["w_qkv_t"].rearrange("(k p) o -> p k o", p=P)).then_inc(w_in, 16)
            act.dma_start(wg[:, :, :], a["wg_t"].rearrange("(k p) e -> p k e", p=P)).then_inc(g_in, 16)
            act.dma_start(bias[:, :], a["balance_bias"].unsqueeze(0).to_broadcast([P, E])).then_inc(b_in, 16)
            for c in range(C):
                act.wait_ge(std_wanted, c + 1)
                act.activation(stat["std"][:, c * TC:(c + 1) * TC], stat["var"][:, c * TC:(c + 1) * TC],
                               ACT.Sqrt).then_inc(std_ready, 1)
            for c in range(C):
                for i in range(c * TC, (c + 1) * TC):
                    act.wait_ge(t_done, i + 1)
                    act.copy(xt[:, :, i * P:(i + 1) * P], ps_t[i % 2][:, :, :]).then_inc(xt_ready, 1)
                for n in range(4 * c, 4 * c + 4):
                    act.wait_ge(qk_done, n + 1)
                    if n >= 2:
                        act.wait_ge(parts_out[n % 2], 16 * (n // 2))
                    act.copy(parts[:, n % 2, 0, :], ps_qk[n % 2][:, :]).then_inc(high_ready, 1)
            act.wait_ge(logit_ready, 1)
            act.activation(scores[:, :, :], scores[:, :, :], ACT.Exp, scale=-1.0).then_inc(exp_ready, 1)

        @block.vector
        def _(dve):
            step = Steps(dve, step_sem)
            for c in range(C):
                dve.wait_ge(x_in[c], 16)
                norm_chunk(dve, step, m.x, xn, stat, c, std_wanted, std_ready)
                step.sync()
                dve.sem_inc(xn_ready, 1)
                if c == 0:
                    dve.wait_ge(consts, 1)
                    step(dve.tensor_copy(m.ident16[:, :], m.ident[:, :]))
                    step(dve.tensor_copy(m.ones16[:, :], m.ones_f[:, :]))
                    step(dve.tensor_copy(m.before16[:, :], m.before_f[:, :]))
                    step(dve.tensor_copy(m.mask16[:, :], m.mask_f[:, :]))
            for c in range(C):
                for n in range(4 * c, 4 * c + 4):
                    dve.wait_ge(high_ready, n + 1)
                    if n >= 2:
                        dve.wait_ge(low_ready, n - 1)
                    dve.tensor_tensor(rest[:, n % 2, :], ps_qk[n % 2][:, :], parts[:, n % 2, 0, :],
                                      ALU.subtract).then_inc(rest_ready, 1)
                for i in range(c * TC, (c + 1) * TC):
                    dve.wait_ge(v_done, i + 1)
                    dve.tensor_copy(m.v_all[:, i, :, 0:HD],
                                    ps_v[i % 2][:, :].rearrange("p (h d) -> p h d", d=HD)).then_inc(v_copied, 1)
            dve.wait_ge(b_in, 16)
            dve.wait_ge(l_done, T)
            dve.tensor_tensor(scores[:, :, :], ps_l[:, :, :], bias[:, :].unsqueeze(1).to_broadcast([P, T, E]),
                              ALU.add).then_inc(logit_ready, 1)
            dve.wait_ge(exp_ready, 1)
            step.then(dve.tensor_scalar(scores[:, :, :], scores[:, :, :], 1.0, None, ALU.add))
            step.then(dve.reciprocal(scores[:, :, :], scores[:, :, :]))
            route(dve, step, r, scores, TOP0, NT0, 1e-6, 1.0, masks_ready, ranks_ready, slots_ready)

        @block.tensor
        def _(pe):
            pe.wait_ge(consts, 1)
            for c in range(C):
                pe.wait_ge(xn_ready, c + 1)
                for i in range(c * TC, (c + 1) * TC):
                    if i >= 2:
                        pe.wait_ge(xt_ready, i - 1)
                    for k in range(KH):
                        mm = pe.transpose(ps_t[i % 2][:, k, :], xn[:, i, k * P:(k + 1) * P], m.ident[:, :])
                    mm.then_inc(t_done, 1)
                if c == 0:
                    pe.wait_ge(w_in, 16)
                    pe.wait_ge(g_in, 16)
                pe.wait_ge(xt_ready, (c + 1) * TC)
                for n in range(4 * c, 4 * c + 4):
                    if n >= 2:
                        pe.wait_ge(rest_ready, n - 1)
                    for k in range(KH):
                        mm = pe.matmul(ps_qk[n % 2][:, :], wqkv[:, k, (n % 4) * P:(n % 4 + 1) * P],
                                       xt[:, k, c * CH:(c + 1) * CH], start=(k == 0), stop=(k == KH - 1))
                    mm.then_inc(qk_done, 1)
                for i in range(c * TC, (c + 1) * TC):
                    if i >= 2:
                        pe.wait_ge(v_copied, i - 1)
                    for k in range(KH):
                        mm = pe.matmul(ps_v[i % 2][:, :], xt[:, k, i * P:(i + 1) * P], wqkv[:, k, 2 * D:3 * D],
                                       start=(k == 0), stop=(k == KH - 1))
                    mm.then_inc(v_done, 1)
                    for k in range(KH):
                        mm = pe.matmul(ps_l[:, i, :], xt[:, k, i * P:(i + 1) * P], wg[:, k, :],
                                       start=(k == 0), stop=(k == KH - 1))
                    mm.then_inc(l_done, 1)
            route_ranks(pe, r, masks_ready, ranks_ready)


def common(nc, m):
    m.x = m.sb("x_res", [P, T, D])
    m.ident = m.sb("ident", [P, P])
    m.ident16 = m.sb("ident16", [P, P], BF16)
    m.ones_f = m.sb("ones_f", [P, P])
    m.ones16 = m.sb("ones16", [P, P], BF16)
    m.before_f = m.sb("before_f", [P, P])
    m.before16 = m.sb("before16", [P, P], BF16)
    m.mask_f = m.sb("mask_f", [P, P])
    m.mask16 = m.sb("mask16", [P, P], BF16)
    m.iota_i = m.sb("iota_i", [P, P], I32)
    m.iota_f = m.sb("iota_f", [P, P])
    m.within = m.sb("within", [P, E * T])
    m.stat = {"bn": m.sb("bn", [P, T, 6]), "mv": m.sb("mv", [P, T, 2]), "var": m.sb("var", [P, T]),
              "std": m.sb("std", [P, T]), "tmp": m.sb("ln_tmp", [P, T])}
    m.r = {
        "best": m.sb("best", [P, T, 8]), "arg": m.sb("arg", [P, T, 8], U32), "argf": m.sb("argf", [P, T, 8]),
        "hot": m.sb("hot", [P, TOP1, T, E]), "any": m.sb("any", [P, T, E]), "any16": m.sb("any16", [P, T, E], BF16),
        "sum": m.sb("top_sum", [P, T]), "weight": m.sb("weight", [P, T, TOP1]),
        "count": m.sb("count", [P, E, T]), "before": m.sb("before", [P, E, T]), "total": m.sb("total", [P, E]),
        "total_i": m.sb("total_i", [P, E], I32), "end": m.sb("end", [P, E]),
        "slotf": m.sb("slotf", [P, TOP1, T]), "slot": m.sb("slot", [P, TOP1, T], U32),
        "ended": m.sb("ended", [1, NT1, E]), "tilef": m.sb("tilef", [1, NT1]), "tile_e": m.sb("tile_e", [1, NT1], I32),
        "iota_e": m.iota_f[:, 0:E].unsqueeze(1), "iota_t": m.iota_f, "ones_e": m.ones_f[:, 0:E],
        "within": m.within, "before16": m.before16, "ones16": m.ones16,
    }
    m.xd0 = m.scratch("xd0", [NT0 * P, D])
    m.xd1 = m.scratch("xd1", [NT1 * P, D])
    m.yd0 = m.scratch("yd0", [NT0 * P, D])
    m.yd1 = m.scratch("yd1", [NT1 * P, D])
    m.qk_parts = m.scratch("qk_parts", [PARTS, 2 * D, S], BF16)


def attention_plan():
    def exps(g, c):
        return [("exp", g, c, k, pair) for k in range(TC * (c + 1)) for pair in range(HG // 2)]

    def maxes(g, c):
        out = []
        for i in range(TC):
            for j in range(c):
                out += [("max", g, c, [(h, i, j, CH)]) for h in range(HG)]
            w = (i + 1) * P
            per = CH // w
            per = 4 if per >= 4 else 2 if per >= 2 else 1
            out += [("max", g, c, [(h, i, c, w) for h in range(h0, h0 + per)]) for h0 in range(0, HG, per)]
        return out

    def lead(chunks):
        units = []
        for n, (g, c) in enumerate(chunks):
            mine = maxes(g, c)
            if n:
                mine.insert(min(4, len(mine)), ("turn", *chunks[n - 1]))
            units += mine
        return units + [("turn", *chunks[-1])]

    plan = lead([(0, 0), (0, 1)])
    for g in range(NG):
        for now, ahead in (([(g, 0), (g, 1)], [(g, 2)]), ([(g, 2)], [(g, 3)]),
                           ([(g, 3)], [(g + 1, 0), (g + 1, 1)] if g + 1 < NG else [])):
            e = [u for gc in now for u in exps(*gc)]
            s = lead(ahead) if ahead else []
            done = 0
            for n, u in enumerate(e):
                plan.append(u)
                upto = min(len(s) - 1, int((n + 1) / (0.85 * len(e)) * (len(s) - 1))) if s else 0
                if n >= 0.92 * len(e) or n == len(e) - 1:
                    upto = len(s)
                plan += s[done:upto]
                done = max(done, upto)
    return plan


def stage_attention(nc, m):
    plan = attention_plan()
    exps = [u for u in plan if u[0] == "exp"]
    rows = [u for u in plan if u[0] != "exp"]
    turns = [u for u in plan if u[0] == "turn"]
    with ExitStack() as ctx:
        l = Memory(nc, ctx)
        qs = [l.sb(f"qs{b}", [MROWS, C, HG, CH], BF16) for b in range(2)]
        ks = [l.sb(f"ks{b}", [MROWS, HG, S], BF16) for b in range(2)]
        NPB = 4
        probs = l.sb("probs", [P, NPB, 2, CH])
        part_max = [l.sb(f"part_max{b}", [P, HG, TC, C]) for b in range(2)]
        neg_max = l.sb("neg_max", [P, HG * TC])
        max_rest = l.sb("max_rest", [HG * TC, P])
        max_parts = [l.sb(f"max_parts{b}", [HG * TC, PARTS, P], BF16) for b in range(2)]
        ps_st = [l.ps(f"ps_st{b}", [P, 2, CH]) for b in range(2)]
        NSM = 3
        ps_max = [l.ps(f"ps_max{b}", [P, CH]) for b in range(NSM)]
        ps_o = l.ps("ps_o", [P, CH])

        stack_in = [l.sem(f"b_stack_in{b}") for b in range(2)]
        rows_in = [l.sem(f"b_rows_in{b}") for b in range(2)]
        ones_ready = l.sem("b_ones_ready")
        st_done, exp_done, pv_done = l.sem("b_st_done"), l.sem("b_exp_done"), l.sem("b_pv_done")
        o_copied = l.sem("b_o_copied")
        max_done, max_used = l.sem("b_max_done"), l.sem("b_max_used")
        neg_ready, parts_ready = l.sem("b_neg_ready"), l.sem("b_parts_ready")
        step_sem = l.sem("b_dve")
        block = ctx.enter_context(nc.Block())

        def last_exp(g, c):
            return max(n for n, u in enumerate(exps) if u[1:3] == (g, c)) + 1

        @block.sync
        def _(sp):
            for g in range(NG):
                if g >= 2:
                    sp.wait_ge(pv_done, last_exp(g - 2, C - 1))
                for t in range(TERMS):
                    rows_of = slice(t * HD, (t + 1) * HD)
                    src = m.qk_parts[K_PART[t], D + g * HG * HD:D + (g + 1) * HG * HD, :]
                    sp.dma_start(ks[g % 2][rows_of, :, :],
                                 src.rearrange("(h d) t -> d h t", d=HD)).then_inc(stack_in[g % 2], 16)
                    src = m.qk_parts[Q_PART[t], g * HG * HD:(g + 1) * HG * HD, :]
                    for c in range(C):
                        sp.dma_start(qs[g % 2][rows_of, c, :, :],
                                     src[:, c * CH:(c + 1) * CH].rearrange("(h d) t -> d h t", d=HD)
                                     ).then_inc(stack_in[g % 2], 16)

        @block.gpsimd
        def _(pool):
            for b in range(2):
                pool.memset(ks[b][KROWS:MROWS, :, :], 1.0).then_inc(ones_ready, 1)
            for n, (_, g, c) in enumerate(turns):
                pool.wait_ge(parts_ready, n + 1)
                for r in range(PARTS):
                    pool.dma_start(qs[g % 2][KROWS + r:KROWS + r + 1, c, :, :].rearrange("r h t -> r (h t)"),
                                   max_parts[n % 2][:, r, :]).then_inc(rows_in[n % 2], 16)
            for b in range(2):
                pool.wait_ge(rows_in[b], 16 * MDMA * len(turns) // 2)

        @block.scalar
        def _(act):
            chunks = 0

            def copy_output(n):
                g, c = exps[n][1:3]
                act.wait_ge(pv_done, n + 1)
                act.copy(m.o_t[:, g, c * CH:(c + 1) * CH], ps_o[:, :]).then_inc(o_copied, 1)

            for n, (_, g, c, k, pair) in enumerate(exps):
                off = max(0, k - TC * c) * P
                act.wait_ge(st_done, n + 1)
                if n >= NPB:
                    act.wait_ge(pv_done, n - NPB + 1)
                act.activation(probs[:, n % NPB, :, off:CH], ps_st[n % 2][:, :, off:CH], ACT.Exp,
                               scale=HD ** -0.5).then_inc(exp_done, 1)
                if n >= 1 and exps[n - 1][1:3] != (g, c):
                    copy_output(n - 1)
            copy_output(len(exps) - 1)

        @block.vector
        def _(dve):
            step = Steps(dve, step_sem)
            turned, reduced = 0, 0
            for n, u in enumerate(rows):
                g, c = u[1:3]
                dve.wait_ge(max_done, n + 1)
                bank = ps_max[n % NSM]
                if u[0] == "max":
                    pieces = u[3]
                    h, i, j, w = pieces[0]
                    k = len(pieces)
                    if reduced >= 2:
                        dve.wait_ge(neg_ready, reduced - 1)
                    dve.tensor_reduce(part_max[reduced % 2][:, h:h + k, i, j:j + 1],
                                      bank[:, 0:k * w].rearrange("p (h w) -> p h w", h=k),
                                      AX_X, ALU.max).then_inc(max_used, 1)
                    after = [v for v in rows[n + 1:] if v[0] == "max"][:1]
                    if not after or after[0][1:3] != (g, c):
                        dve.wait_ge(max_used, n + 1)
                        dve.tensor_reduce(neg_max[:, :], part_max[reduced % 2][:, :, :, 0:c + 1].rearrange("p h i j -> p (h i) j"),
                                          AX_X, ALU.max, negate=True).then_inc(neg_ready, 1)
                        reduced += 1
                else:
                    parts = max_parts[turned % 2]
                    turned_ps = bank[0:HG * TC, 0:P]
                    if turned >= 2:
                        dve.wait_ge(rows_in[turned % 2], 16 * MDMA * (turned // 2))
                    step.then(dve.tensor_copy(parts[:, 0, :], turned_ps))
                    dve.tensor_tensor(max_rest[:, :], turned_ps, parts[:, 0, :], ALU.subtract).then_inc(max_used, 1)
                    dve.wait_ge(max_used, n + 1)
                    step.then(dve.tensor_copy(parts[:, 1, :], max_rest[:, :]))
                    dve.tensor_tensor(parts[:, 2, :], max_rest[:, :], parts[:, 1, :],
                                      ALU.subtract).then_inc(parts_ready, 1)
                    dve.wait_ge(parts_ready, turned + 1)
                    turned += 1

        @block.tensor
        def _(pe):
            state = {"exp": 0, "pv": 0, "row": 0, "turn": 0, "stack": -1, "chunk": None, "out": 0}
            turn_of = {u[1:3]: n for n, u in enumerate(turns)}

            def stacks(g):
                if g > state["stack"]:
                    pe.wait_ge(stack_in[g % 2], 16 * (1 + C) * TERMS * (g // 2 + 1))
                    state["stack"] = g

            def values():
                n = state["pv"]
                _, g, c, k, pair = exps[n]
                off = max(0, k - TC * c) * P
                pe.wait_ge(exp_done, n + 1)
                if k == 0 and pair == 0 and n:
                    state["out"] += 1
                    pe.wait_ge(o_copied, state["out"])
                for h in range(2):
                    q = 2 * pair + h
                    mm = pe.matmul(ps_o[32 * q:32 * q + 32, off:CH], m.v_all[:, k, g * HG + q, :],
                                   probs[:, n % NPB, h, off:CH], start=(k == 0), stop=(k == TC * (c + 1) - 1),
                                   tile_position=(0, 32 * q))
                mm.then_inc(pv_done, 1)
                state["pv"] += 1

            for u in plan:
                g, c = u[1:3]
                if u[0] == "exp":
                    k, pair = u[3:]
                    n = state["exp"]
                    off = max(0, k - TC * c) * P
                    if n == 0:
                        pe.wait_ge(ones_ready, 2)
                    if (g, c) != state["chunk"]:
                        t = turn_of[(g, c)]
                        pe.wait_ge(rows_in[t % 2], 16 * MDMA * (t // 2 + 1))
                        state["chunk"] = (g, c)
                    if n >= 2:
                        pe.wait_ge(exp_done, n - 1)
                    for h in range(2):
                        q = 2 * pair + h
                        diagonal = k >= TC * c
                        mm = pe.matmul(ps_st[n % 2][:, h, off:CH], ks[g % 2][:, q, k * P:(k + 1) * P],
                                       qs[g % 2][:, c, q, off:CH], start=True, stop=not diagonal)
                        if diagonal:
                            mm = pe.matmul(ps_st[n % 2][:, h, off:off + P], m.mask16[:, :], m.ident16[:, :],
                                           start=False, stop=True)
                    mm.then_inc(st_done, 1)
                    state["exp"] += 1
                    if state["exp"] - state["pv"] > 2:
                        values()
                else:
                    n = state["row"]
                    stacks(g)
                    if n >= NSM:
                        pe.wait_ge(max_used, n - NSM + 1)
                    bank = ps_max[n % NSM]
                    if u[0] == "max":
                        for at, (h, i, j, w) in enumerate(u[3]):
                            cols = bank[:, at * w:(at + 1) * w]
                            mm = pe.matmul(cols, qs[g % 2][0:KROWS, c, h, i * P:(i + 1) * P],
                                           ks[g % 2][0:KROWS, h, j * CH:j * CH + w], start=True, stop=(j < c))
                            if j == c:
                                mm = pe.matmul(cols[:, w - P:w], m.ident16[:, :], m.mask16[:, :],
                                               start=False, stop=True)
                    else:
                        pe.wait_ge(neg_ready, state["turn"] + 1)
                        state["turn"] += 1
                        mm = pe.transpose(bank[0:HG * TC, 0:P], neg_max[:, :], m.ident[:, :])
                    mm.then_inc(max_done, 1)
                    state["row"] += 1
            while state["pv"] < len(exps):
                values()


def stage_output(nc, m, a):
    with ExitStack() as ctx:
        l = Memory(nc, ctx)
        wo = l.sb("wo", [P, KH, D])
        rec = l.sb("rec", [P, 2, NH])
        heads = l.sb("heads", [P, 2, NH, HD])
        heads_t = l.sb("heads_t", [P, 2, KH, P])
        ps_o = [l.ps(f"ps_oo{b}", [P, NG, P]) for b in range(2)]
        ps_h = [l.ps(f"ps_h{b}", [P, KH, P]) for b in range(2)]
        ps_w = [l.ps(f"ps_w{b}", [P, D]) for b in range(2)]
        w_in, turned, rec_ready = l.sem("c_w_in"), l.sem("c_turned"), l.sem("c_rec_ready")
        heads_ready, back, back_copied = l.sem("c_heads_ready"), l.sem("c_back"), l.sem("c_back_copied")
        w_done, added = l.sem("c_w_done"), l.sem("c_added")
        block = ctx.enter_context(nc.Block())

        @block.sync
        def _(sp):
            sp.dma_start(wo[:, :, :], a["w_o_t"].rearrange("(k p) o -> p k o", p=P)).then_inc(w_in, 16)

        @block.scalar
        def _(act):
            for i in range(T):
                act.wait_ge(back, i + 1)
                if i >= 2:
                    act.wait_ge(w_done, i - 1)
                act.copy(heads_t[:, i % 2, :, :], ps_h[i % 2][:, :, :]).then_inc(back_copied, 1)

        @block.vector
        def _(dve):
            def normalize(i):
                dve.wait_ge(turned, i + 1)
                if i >= 2:
                    dve.wait_ge(back, i - 1)
                    dve.wait_ge(heads_ready, i - 1)
                by_head = ps_o[i % 2][:, :, :].rearrange("p g (h w) -> p (g h) w", w=32)
                dve.reciprocal(rec[:, i % 2, :], by_head[:, :, HD]).then_inc(rec_ready, 1)
                dve.wait_ge(rec_ready, i + 1)
                dve.tensor_tensor(heads[:, i % 2, :, :], by_head[:, :, 0:HD],
                                  rec[:, i % 2, :].unsqueeze(2).to_broadcast([P, NH, HD]),
                                  ALU.mult).then_inc(heads_ready, 1)

            def add(i):
                dve.wait_ge(w_done, i + 1)
                dve.tensor_tensor(m.x[:, i, :], ps_w[i % 2][:, :], m.x[:, i, :], ALU.add).then_inc(added, 1)

            for i in range(T + 2):
                if i < T:
                    normalize(i)
                if i >= 2:
                    add(i - 2)

        @block.tensor
        def _(pe):
            pe.wait_ge(w_in, 16)
            for i in range(T + 2):
                if i < T:
                    if i >= 2:
                        pe.wait_ge(heads_ready, i - 1)
                    for g in range(NG):
                        mm = pe.transpose(ps_o[i % 2][:, g, :], m.o_t[:, g, i * P:(i + 1) * P], m.ident[:, :])
                    mm.then_inc(turned, 1)
                if 1 <= i <= T:
                    j = i - 1
                    pe.wait_ge(heads_ready, j + 1)
                    if j >= 2:
                        pe.wait_ge(back_copied, j - 1)
                    for k in range(KH):
                        mm = pe.transpose(ps_h[j % 2][:, k, :],
                                          heads[:, j % 2, k * NH // KH:(k + 1) * NH // KH, :].rearrange("p h d -> p (h d)"),
                                          m.ident[:, :])
                    mm.then_inc(back, 1)
                if i >= 2:
                    j = i - 2
                    pe.wait_ge(back_copied, j + 1)
                    if j >= 2:
                        pe.wait_ge(added, j - 1)
                    for k in range(KH):
                        mm = pe.matmul(ps_w[j % 2][:, :], heads_t[:, j % 2, k, :], wo[:, k, :],
                                       start=(k == 0), stop=(k == KH - 1))
                    mm.then_inc(w_done, 1)


def rolled(eng, lag, tiles, unroll, tick):
    start = -(-(lag + 2) // unroll) * unroll
    stop = start + (tiles - start) // unroll * unroll
    for j in range(start):
        tick(j, j % unroll)
    with eng.Fori(start, stop, unroll) as j:
        for u in range(unroll):
            tick(j + u, u)
    for j in range(stop, tiles + lag):
        tick(j, j % unroll)


def stage_experts(nc, m, name, xd, yd, tiles, top, gated, w1_dram, w2_dram):
    W1 = (2 if gated else 1) * HID
    U = 4
    with ExitStack() as ctx:
        l = Memory(nc, ctx)
        w1 = l.sb(f"{name}_w1", [P, KH, E, W1])
        w2 = l.sb(f"{name}_w2", [P, E, D])
        xs = l.sb(f"{name}_xs", [P, U, D])
        xs_t = l.sb(f"{name}_xs_t", [P, 2, KH, P])
        act_out = l.sb(f"{name}_act", [P, 2, HID])
        hid = l.sb(f"{name}_hid", [P, 2, HID])
        hid_t = l.sb(f"{name}_hid_t", [P, 2, P])
        ys = l.sb(f"{name}_ys", [P, 2, D])
        yg = l.sb(f"{name}_yg", [P, 2, top, D])
        ps_x = [l.ps(f"{name}_ps_x{b}", [P, KH, P]) for b in range(2)]
        ps_h = [l.ps(f"{name}_ps_h{b}", [P, W1]) for b in range(2)]
        ps_g = [l.ps(f"{name}_ps_g{b}", [P, P]) for b in range(2)]
        ps_y = [l.ps(f"{name}_ps_y{b}", [P, D]) for b in range(2)]
        w1_in, w2_in = l.sem(f"{name}_w1_in"), l.sem(f"{name}_w2_in")
        x_in = [l.sem(f"{name}_x_in{b}") for b in range(U)]
        y_out = [l.sem(f"{name}_y_out{b}") for b in range(2)]
        gathered = [l.sem(f"{name}_gathered{b}") for b in range(2)]
        x_turned, x_copied = l.sem(f"{name}_x_turned"), l.sem(f"{name}_x_copied")
        h_done, act_done, hid_ready = l.sem(f"{name}_h_done"), l.sem(f"{name}_act_done"), l.sem(f"{name}_hid_ready")
        g_turned, g_copied = l.sem(f"{name}_g_turned"), l.sem(f"{name}_g_copied")
        y_done, y_copied = l.sem(f"{name}_y_done"), l.sem(f"{name}_y_copied")
        summed = l.sem(f"{name}_summed")
        block = ctx.enter_context(nc.Block())

        def there(j):
            return not isinstance(j, int) or 0 <= j < tiles

        def since(j, n):
            return not isinstance(j, int) or j >= n

        @block.sync
        def _(sp):
            def tick(j, u):
                if there(j):
                    if since(j, U):
                        sp.wait_ge(x_turned, j - (U - 1))
                    sp.dma_start(xs[:, u, :], xd[bass.ds(j * P, P), :]).then_inc(x_in[u], 16)
                k = j - 2 * U
                if there(k):
                    sp.wait_ge(y_copied, k + 1)
                    sp.dma_start(yd[bass.ds(k * P, P), :], ys[:, u % 2, :]).then_inc(y_out[u % 2], 16)

            rolled(sp, 2 * U, tiles, U, tick)

        @block.scalar
        def _(act):
            act.dma_start(w1[:, :, :, :], w1_dram.rearrange("(k p) (e h) -> p k e h", p=P, e=E)).then_inc(w1_in, 16)
            act.dma_start(w2[:, :, :], w2_dram.rearrange("e p d -> p e d")).then_inc(w2_in, 16)

            def tick(j, u):
                if there(j):
                    b = u % 2
                    act.wait_ge(x_turned, j + 1)
                    if since(j, 2):
                        act.wait_ge(h_done, j - 1)
                    act.copy(xs_t[:, b, :, :], ps_x[b][:, :, :]).then_inc(x_copied, 1)
                j = j - 1
                if there(j):
                    b = (u - 1) % 2
                    act.wait_ge(h_done, j + 1)
                    out = act_out if gated else hid
                    if since(j, 2):
                        act.wait_ge(hid_ready if gated else g_turned, j - 1)
                    act.activation(out[:, b, :], ps_h[b][:, 0:HID], ACT.Silu).then_inc(act_done, 1)

            rolled(act, 1, tiles, U, tick)

        @block.vector
        def _(dve):
            def tick(j, u):
                if gated and there(j - 1):
                    b = (u - 1) % 2
                    dve.wait_ge(act_done, j)
                    if since(j - 1, 2):
                        dve.wait_ge(g_turned, j - 2)
                    dve.tensor_tensor(hid[:, b, :], ps_h[b][:, HID:2 * HID], act_out[:, b, :],
                                      ALU.mult).then_inc(hid_ready, 1)
                if there(j - 2):
                    b = u % 2
                    dve.wait_ge(g_turned, j - 1)
                    if since(j - 2, 2):
                        dve.wait_ge(y_done, j - 3)
                    dve.tensor_copy(hid_t[:, b, :], ps_g[b][:, :]).then_inc(g_copied, 1)
                if there(j - 3):
                    b = (u - 3) % 2
                    dve.wait_ge(y_done, j - 2)
                    if since(j - 3, 2):
                        dve.wait_ge(y_out[b], (j - 3 - b) * 8)
                    dve.tensor_copy(ys[:, b, :], ps_y[b][:, :]).then_inc(y_copied, 1)

            rolled(dve, 3, tiles, U, tick)
            for i in range(T):
                dve.wait_ge(gathered[i % 2], 16 * top * (i // 2 + 1))
                for k in range(top):
                    dve.scalar_tensor_tensor(m.x[:, i, :], yg[:, i % 2, k, :], m.r["weight"][:, i, k:k + 1],
                                             m.x[:, i, :], ALU.mult, ALU.add).then_inc(summed, 1)
                    dve.wait_ge(summed, i * top + k + 1)

        @block.gpsimd
        def _(pool):
            for b in range(2):
                pool.wait_ge(y_out[b], 16 * ((tiles + 1 - b) // 2))
            for i in range(T):
                if i >= 2:
                    pool.wait_ge(summed, (i - 1) * top)
                for k in range(top):
                    pool.indirect_dma_start(out=yg[:, i % 2, k, :], out_offset=None, in_=yd,
                                            in_offset=bass.IndirectOffsetOnAxis(m.r["slot"][:, k, i:i + 1], 0)
                                            ).then_inc(gathered[i % 2], 16)

        @block.tensor
        def _(pe):
            pe.wait_ge(w1_in, 16)
            pe.wait_ge(w2_in, 16)

            def expert(j):
                return pe.value_load(m.r["tile_e"][0:1, bass.ds(j, 1)], min_val=0, max_val=E - 1)

            def tick(j, u):
                if there(j):
                    b = u % 2
                    pe.wait_ge(x_in[u], (j - u) * 4 + 16)
                    if since(j, 2):
                        pe.wait_ge(x_copied, j - 1)
                    for k in range(KH):
                        mm = pe.transpose(ps_x[b][:, k, :], xs[:, u, k * P:(k + 1) * P], m.ident[:, :])
                    mm.then_inc(x_turned, 1)
                if there(j - 1):
                    b = (u - 1) % 2
                    e = expert(j - 1)
                    pe.wait_ge(x_copied, j)
                    if since(j - 1, 2):
                        pe.wait_ge(hid_ready if gated else act_done, j - 2)
                    for k in range(KH):
                        mm = pe.matmul(ps_h[b][:, :], xs_t[:, b, k, :], w1[:, k, bass.ds(e, 1), :],
                                       start=(k == 0), stop=(k == KH - 1))
                    mm.then_inc(h_done, 1)
                if there(j - 2):
                    b = u % 2
                    pe.wait_ge(hid_ready if gated else act_done, j - 1)
                    if since(j - 2, 2):
                        pe.wait_ge(g_copied, j - 3)
                    pe.transpose(ps_g[b][:, :], hid[:, b, :], m.ident[:, :]).then_inc(g_turned, 1)
                if there(j - 3):
                    b = (u - 3) % 2
                    e = expert(j - 3)
                    pe.wait_ge(g_copied, j - 2)
                    if since(j - 3, 2):
                        pe.wait_ge(y_copied, j - 4)
                    pe.matmul(ps_y[b][:, :], hid_t[:, b, :], w2[:, bass.ds(e, 1), :],
                              start=True, stop=True).then_inc(y_done, 1)

            rolled(pe, 3, tiles, U, tick)


def stage_second(nc, m, a):
    with ExitStack() as ctx:
        l = Memory(nc, ctx)
        DP = D + 1
        xn = l.sb("xn2", [P, T, DP])
        xt = l.sb("xt2", [P, KH, S])
        w = l.sb("w_attn", [P, KH, 3 * D])
        wr = l.sb("w_router", [P, KH, E])
        ws1 = l.sb("ws1", [P, KH, HS])
        ws3 = l.sb("ws3", [P, KH, HS])
        ws2 = l.sb("ws2", [P, HS // P, D])
        bias = l.sb("bias_qkv", [P, 3 * D])
        scores = l.sb("scores2", [P, T, E])
        peak = l.sb("peak", [P, T])
        gram = l.sb("gram", [P, KH, DP])
        sums = l.sb("sums", [P, KH, P])
        prod = l.sb("prod", [P, KH, 3 * D])
        square = l.sb("square", [P, 2 * D])
        root = l.sb("root", [P, 2 * D])
        kv = l.sb("kv", [P, D])
        t1, t2 = l.sb("t1", [P, 2 * D]), l.sb("t2", [P, D])
        wq = l.sb("wq", [P, KH, D])
        bq = l.sb("bq", [P, D])
        gate = l.sb("gate", [P, CH])
        hid = l.sb("hid_s", [P, HS // P, S])
        ps_t = [l.ps(f"ps_t2{b}", [P, CH]) for b in range(2)]
        ps_g = [l.ps(f"ps_gram{b}", [P, DP]) for b in range(KH)]
        ps_l = l.ps("ps_l2", [P, T, E])
        ps_ab = [l.ps(f"ps_ab{b}", [P, CH]) for b in range(2)]
        ps_o = l.ps("ps_o2", [P, 2, D])
        stat, r = m.stat, dict(m.r)
        w_in, b_in, s_in = l.sem("e_w_in"), l.sem("e_b_in"), l.sem("e_s_in")
        std_wanted, std_ready, step_sem = l.sem("e_std_wanted"), l.sem("e_std_ready"), l.sem("e_dve")
        ones_ready = l.sem("e_ones_ready")
        xn_ready, t_done, xt_ready, l_done = l.sem("e_xn_ready"), l.sem("e_t_done"), l.sem("e_xt_ready"), l.sem("e_l_done")
        logit_ready, exp_ready = l.sem("e_logit_ready"), l.sem("e_exp_ready")
        masks_ready, ranks_ready, slots_ready = l.sem("e_masks_ready"), l.sem("e_ranks_ready"), l.sem("e_slots_ready")
        dispatched = l.sem("e_dispatched")
        gram_done, gram_copied = l.sem("e_gram_done"), l.sem("e_gram_copied")
        gw_done, prod_ready, norms_done = l.sem("e_gw_done"), l.sem("e_prod_ready"), l.sem("e_norms_done")
        square_ready, root_ready, wq_ready = l.sem("e_square_ready"), l.sem("e_root_ready"), l.sem("e_wq_ready")
        a_done, gate_ready, b_done, hid_ready = l.sem("e_a_done"), l.sem("e_gate_ready"), l.sem("e_b_done"), l.sem("e_hid_ready")
        o_done, o_added = l.sem("e_o_done"), l.sem("e_o_added")
        r["ps_rank"], r["ps_count"] = ps_o[:, 0, :], ps_o[:, 1, :]
        block = ctx.enter_context(nc.Block())
        units = [(c, s) for c in range(C) for s in range(HS // P)]

        @block.sync
        def _(sp):
            sp.dma_start(w[:, :, :], a["w_attn"].rearrange("(k p) o -> p k o", p=P)).then_inc(w_in, 16)
            sp.dma_start(wr[:, :, :], a["w_router"].rearrange("(k p) e -> p k e", p=P)).then_inc(w_in, 16)
            sp.dma_start(bias[:, :], a["b_attn"].unsqueeze(0).to_broadcast([P, 3 * D])).then_inc(b_in, 16)
            sp.dma_start(ws1[:, :, :], a["ws1"].rearrange("(k p) o -> p k o", p=P)).then_inc(s_in, 16)
            sp.dma_start(ws3[:, :, :], a["ws3"].rearrange("(k p) o -> p k o", p=P)).then_inc(s_in, 16)
            sp.dma_start(ws2[:, :, :], a["ws2"].rearrange("(k p) o -> p k o", p=P)).then_inc(s_in, 16)

        @block.gpsimd
        def _(pool):
            pool.memset(xn[:, :, D:DP], 1.0).then_inc(ones_ready, 1)
            pool.wait_ge(slots_ready, 1)
            for k in range(TOP1):
                for i in range(T):
                    pool.indirect_dma_start(out=m.xd1, out_offset=bass.IndirectOffsetOnAxis(r["slot"][:, k, i:i + 1], 0),
                                            in_=xn[:, i, 0:D], in_offset=None).then_inc(dispatched, 16)
            pool.wait_ge(dispatched, 16 * TOP1 * T)

        @block.scalar
        def _(act):
            for c in range(C):
                act.wait_ge(std_wanted, c + 1)
                act.activation(stat["std"][:, c * TC:(c + 1) * TC], stat["var"][:, c * TC:(c + 1) * TC],
                               ACT.Sqrt).then_inc(std_ready, 1)
            for i in range(T):
                act.wait_ge(t_done, i + 1)
                act.copy(xt[:, :, i * P:(i + 1) * P],
                         ps_t[i % 2][:, 0:D].rearrange("p (k t) -> p k t", k=KH)).then_inc(xt_ready, 1)
            act.wait_ge(logit_ready, 1)
            act.activation(scores[:, :, :], scores[:, :, :], ACT.Exp).then_inc(exp_ready, 1)
            act.wait_ge(gram_done, 1)
            for k in range(KH):
                act.copy(gram[:, k, :], ps_g[k][:, :]).then_inc(gram_copied, 1)
            act.wait_ge(square_ready, 1)
            act.activation(root[:, :], square[:, :], ACT.Sqrt).then_inc(root_ready, 1)
            for n in range(len(units)):
                act.wait_ge(a_done, n + 1)
                if n >= 1:
                    act.wait_ge(hid_ready, n)
                act.activation(gate[:, :], ps_ab[0][:, :], ACT.Silu).then_inc(gate_ready, 1)

        @block.vector
        def _(dve):
            step = Steps(dve, step_sem)
            for c in range(C):
                norm_chunk(dve, step, m.x, xn, stat, c, std_wanted, std_ready)
                step.sync()
                dve.sem_inc(xn_ready, 1)
            dve.wait_ge(l_done, T)
            step.then(dve.tensor_reduce(peak[:, :], ps_l[:, :, :], AX_X, ALU.max))
            dve.tensor_tensor(scores[:, :, :], ps_l[:, :, :], peak[:, :].unsqueeze(2).to_broadcast([P, T, E]),
                              ALU.subtract).then_inc(logit_ready, 1)
            dve.wait_ge(exp_ready, 1)
            step.then(dve.tensor_reduce(peak[:, :], scores[:, :, :], AX_X, ALU.add))
            step.then(dve.reciprocal(peak[:, :], peak[:, :]))
            step.then(dve.tensor_tensor(scores[:, :, :], scores[:, :, :],
                                        peak[:, :].unsqueeze(2).to_broadcast([P, T, E]), ALU.mult))
            route(dve, step, r, scores, TOP1, NT1, 0.0, TOP1 / (TOP1 + 1), masks_ready, ranks_ready, slots_ready)
            dve.wait_ge(gram_copied, KH)
            for k in range(KH):
                dve.tensor_copy(sums[:, k, :], gram[:, k, D:DP].to_broadcast([P, P])).then_inc(gram_copied, 1)
            dve.wait_ge(b_in, 16)
            for k in range(KH):
                dve.wait_ge(gw_done, k + 1)
                step(dve.tensor_tensor(prod[:, k, 0:2 * D], ps_t[k][:, :], w[:, k, 0:2 * D], ALU.mult))
                step(dve.tensor_tensor(prod[:, k, 2 * D:3 * D], ps_t[k][:, D:2 * D], w[:, k, 2 * D:3 * D], ALU.mult))
            step.sync()
            dve.sem_inc(prod_ready, 1)
            bqk, bk, bv = bias[:, 0:2 * D], bias[:, D:2 * D], bias[:, 2 * D:3 * D]
            dve.wait_ge(norms_done, 1)
            step.then(dve.tensor_scalar(t1[:, :], bqk, float(S), None, ALU.mult))
            step.then(dve.scalar_tensor_tensor(t1[:, :], ps_ab[1][:, :], 2.0, t1[:, :], ALU.mult, ALU.add))
            step.then(dve.tensor_tensor(t1[:, :], t1[:, :], bqk, ALU.mult))
            dve.tensor_tensor(square[:, :], ps_ab[0][:, :], t1[:, :], ALU.add).then_inc(square_ready, 1)
            step.then(dve.scalar_tensor_tensor(kv[:, :], bv, float(S), ps_o[:, 1, :], ALU.mult, ALU.add))
            step.then(dve.tensor_tensor(kv[:, :], kv[:, :], bk, ALU.mult))
            step.then(dve.tensor_tensor(t2[:, :], ps_ab[1][:, D:2 * D], bv, ALU.mult))
            step.then(dve.tensor_tensor(kv[:, :], kv[:, :], t2[:, :], ALU.add))
            step.then(dve.tensor_tensor(kv[:, :], ps_o[:, 0, :], kv[:, :], ALU.add))
            dve.wait_ge(square_ready, 1)
            dve.wait_ge(root_ready, 1)
            step.then(dve.tensor_tensor(t2[:, :], root[:, 0:D], root[:, D:2 * D], ALU.mult))
            step.then(dve.reciprocal(t2[:, :], t2[:, :]))
            step.then(dve.tensor_tensor(t1[:, 0:D], square[:, 0:D], t2[:, :], ALU.mult))
            step.then(dve.tensor_tensor(t1[:, D:2 * D], square[:, D:2 * D], t2[:, :], ALU.mult))
            step.then(dve.tensor_tensor(t1[:, 0:D], t1[:, 0:D], t1[:, D:2 * D], ALU.mult))
            step.then(dve.tensor_scalar(t1[:, 0:D], t1[:, 0:D], -0.5, 1.5, ALU.mult, ALU.add))
            step.then(dve.tensor_tensor(t2[:, :], t2[:, :], t1[:, 0:D], ALU.mult))
            step.then(dve.tensor_tensor(kv[:, :], kv[:, :], t2[:, :], ALU.mult))
            step(dve.tensor_tensor(bq[:, :], bias[:, 0:D], kv[:, :], ALU.mult))
            step(dve.tensor_tensor(wq[:, :, :], w[:, :, 0:D], kv[:, :].unsqueeze(1).to_broadcast([P, KH, D]), ALU.mult))
            step.sync()
            step(dve.tensor_tensor(m.x[:, :, :], m.x[:, :, :], bq[:, :].unsqueeze(1).to_broadcast([P, T, D]), ALU.add))
            step.sync()
            dve.sem_inc(wq_ready, 1)
            for n, (c, s) in enumerate(units):
                dve.wait_ge(gate_ready, n + 1)
                dve.wait_ge(b_done, n + 1)
                dve.tensor_tensor(hid[:, s, c * CH:(c + 1) * CH], ps_ab[1][:, :], gate[:, :],
                                  ALU.mult).then_inc(hid_ready, 1)
            for n in range(2 * T):
                i = n // 2
                dve.wait_ge(o_done, n + 1)
                if n:
                    dve.wait_ge(o_added, n)
                dve.scalar_tensor_tensor(m.x[:, i, :], ps_t[n % 2][:, 0:D], 1.0 / (TOP1 + 1) if n % 2 == 0 else 1.0,
                                         m.x[:, i, :], ALU.mult, ALU.add).then_inc(o_added, 1)

        @block.tensor
        def _(pe):
            pe.wait_ge(w_in, 32)
            pe.wait_ge(ones_ready, 1)
            for c in range(C):
                pe.wait_ge(xn_ready, c + 1)
                for i in range(c * TC, (c + 1) * TC):
                    if i >= 2:
                        pe.wait_ge(xt_ready, i - 1)
                    for k in range(KH):
                        mm = pe.transpose(ps_t[i % 2][:, k * P:(k + 1) * P], xn[:, i, k * P:(k + 1) * P], m.ident[:, :])
                    mm.then_inc(t_done, 1)
                    for k in range(KH):
                        mm = pe.matmul(ps_g[k][:, :], xn[:, i, k * P:(k + 1) * P], xn[:, i, :],
                                       start=(i == 0), stop=(i == T - 1))
                    if i == T - 1:
                        mm.then_inc(gram_done, 1)
                for i in range(c * TC, (c + 1) * TC):
                    pe.wait_ge(xt_ready, i + 1)
                    for k in range(KH):
                        mm = pe.matmul(ps_l[:, i, :], xt[:, k, i * P:(i + 1) * P], wr[:, k, :],
                                       start=(k == 0), stop=(k == KH - 1))
                    mm.then_inc(l_done, 1)
            route_ranks(pe, r, masks_ready, ranks_ready)
            pe.wait_ge(gram_copied, 2 * KH)
            for k in range(KH):
                for j in range(KH):
                    mm = pe.matmul(ps_t[k][:, :], gram[:, j, k * P:(k + 1) * P], w[:, j, 0:2 * D],
                                   start=(j == 0), stop=(j == KH - 1))
                mm.then_inc(gw_done, 1)
            for k in range(KH):
                pe.matmul(ps_ab[1][:, :], sums[:, k, :], w[:, k, 0:2 * D], start=(k == 0), stop=(k == KH - 1))
            pe.wait_ge(slots_ready, 1)
            for k in range(KH):
                pe.matmul(ps_o[:, 1, :], sums[:, k, :], w[:, k, 2 * D:3 * D], start=(k == 0), stop=(k == KH - 1))
            pe.wait_ge(prod_ready, 1)
            for k in range(KH):
                pe.matmul(ps_ab[0][:, :], m.ones_f[:, :], prod[:, k, 0:2 * D], start=(k == 0), stop=(k == KH - 1))
            for k in range(KH):
                mm = pe.matmul(ps_o[:, 0, :], m.ones_f[:, :], prod[:, k, 2 * D:3 * D],
                               start=(k == 0), stop=(k == KH - 1))
            mm.then_inc(norms_done, 1)
            pe.wait_ge(s_in, 48)
            pe.wait_ge(wq_ready, 1)
            for n, (c, s) in enumerate(units):
                if n:
                    pe.wait_ge(gate_ready, n)
                for k in range(KH):
                    mm = pe.matmul(ps_ab[0][:, :], ws1[:, k, s * P:(s + 1) * P], xt[:, k, c * CH:(c + 1) * CH],
                                   start=(k == 0), stop=(k == KH - 1))
                mm.then_inc(a_done, 1)
                if n:
                    pe.wait_ge(hid_ready, n)
                for k in range(KH):
                    mm = pe.matmul(ps_ab[1][:, :], ws3[:, k, s * P:(s + 1) * P], xt[:, k, c * CH:(c + 1) * CH],
                                   start=(k == 0), stop=(k == KH - 1))
                mm.then_inc(b_done, 1)
            for n in range(2 * T):
                i = n // 2
                if n >= 2:
                    pe.wait_ge(o_added, n - 1)
                if n % 2 == 0:
                    pe.wait_ge(hid_ready, (i // TC + 1) * (HS // P))
                    for s in range(HS // P):
                        mm = pe.matmul(ps_t[0][:, 0:D], hid[:, s, i * P:(i + 1) * P], ws2[:, s, :],
                                       start=(s == 0), stop=(s == HS // P - 1))
                else:
                    for k in range(KH):
                        mm = pe.matmul(ps_t[1][:, 0:D], xt[:, k, i * P:(i + 1) * P], wq[:, k, :],
                                       start=(k == 0), stop=(k == KH - 1))
                mm.then_inc(o_done, 1)


def stage_store(nc, m, out):
    with ExitStack() as ctx:
        stored = Memory(nc, ctx).sem("stored")
        block = ctx.enter_context(nc.Block())

        @block.sync
        def _(sp):
            for c in range(C):
                sp.dma_start(out[0, c * CH:(c + 1) * CH, :].rearrange("(i p) d -> p i d", p=P),
                             m.x[:, c * TC:(c + 1) * TC, :]).then_inc(stored, 16)
            sp.wait_ge(stored, 16 * C)


def two_layers(nc, a, out):
    with ExitStack() as ctx:
        m = Memory(nc, ctx)
        common(nc, m)
        with ExitStack() as attention:
            l = Memory(nc, attention)
            m.o_t = l.sb("o_t", [P, NG, S])
            m.v_all = l.sb("v_all", [P, T, NH, 32])
            stage_project(nc, m, a)
            stage_attention(nc, m)
            stage_output(nc, m, a)
        stage_experts(nc, m, "moe0", m.xd0, m.yd0, NT0, TOP0, False, a["w1"], a["w2"])
        stage_second(nc, m, a)
        stage_experts(nc, m, "moe1", m.xd1, m.yd1, NT1, TOP1, True, a["we13"], a["we2"])
        stage_store(nc, m, out)


def kernel(L0_attn_hidden_states, L0_attn_w_qkv, L0_attn_w_o, L0_ffn_Wg, L0_ffn_balance_bias, L0_ffn_W1, L0_ffn_W2,
           L1_attn_W, L1_attn_b, L1_ffn_w_router, L1_ffn_we1, L1_ffn_we3, L1_ffn_we2, L1_ffn_ws1, L1_ffn_ws3,
           L1_ffn_ws2):
    import numpy as np
    import concourse.bacc as bacc
    from concourse.bass_utils import run_bass_kernel_spmd

    def experts_last(w):
        return w.transpose(1, 0, 2).reshape(w.shape[1], -1)

    arrays = {
        "x": L0_attn_hidden_states, "w_qkv_t": L0_attn_w_qkv.T, "w_o_t": L0_attn_w_o.T, "wg_t": L0_ffn_Wg.T,
        "balance_bias": L0_ffn_balance_bias, "w1": experts_last(np.asarray(L0_ffn_W1)), "w2": L0_ffn_W2,
        "w_attn": L1_attn_W, "b_attn": L1_attn_b, "w_router": L1_ffn_w_router,
        "we13": experts_last(np.concatenate([np.asarray(L1_ffn_we1), np.asarray(L1_ffn_we3)], axis=2)),
        "we2": L1_ffn_we2, "ws1": L1_ffn_ws1, "ws3": L1_ffn_ws3, "ws2": L1_ffn_ws2,
    }
    arrays = {name: np.ascontiguousarray(v) for name, v in arrays.items()}
    nc = bacc.Bacc("TRN2", target_bir_lowering=False, num_devices=1)
    a = {name: nc.dram_tensor(f"in_{name}", v.shape, mybir.dt.from_np(v.dtype), kind="ExternalInput").ap()
         for name, v in arrays.items()}
    out = nc.dram_tensor("out", (1, S, D), F32, kind="ExternalOutput").ap()
    two_layers(nc, a, out)
    result = run_bass_kernel_spmd(nc, [{f"in_{name}": v for name, v in arrays.items()}], core_ids=[0])
    return result.results[0]["out"]
```

```python
from contextlib import ExitStack

import concourse.bass as bass
from concourse import mybir

ALU = mybir.AluOpType
ACT = mybir.ActivationFunctionType
F32 = mybir.dt.float32
BF16 = mybir.dt.bfloat16
I32 = mybir.dt.int32
U32 = mybir.dt.uint32
AX_X = mybir.AxisListType.X

P = 128
S = 2048
D = 256
T = S // P
KH = D // P
CH = 512
C = S // CH
TC = CH // P
NH = 16
HD = D // NH
HG = 4
NG = NH // HG
E = 16
HID = 128
HS = 512
TOP0, TOP1 = 2, 4
NT0 = S * TOP0 // P + E - 1
NT1 = S * TOP1 // P + E - 1
EPAD = 8
IN_RANGE = "the routing counts from zero and takes the minimum with E - 1"
EPS = 1e-5
NEG = -1e30
PARTS = 3
Q_PART = [0, 0, 0, 1, 1, 2]
K_PART = [0, 1, 2, 0, 1, 0]
TERMS = len(Q_PART)
KROWS = TERMS * HD
MDMA = PARTS
MROWS = KROWS + PARTS


class Steps:

    def __init__(self, eng, sem):
        self.eng, self.sem, self.n = eng, sem, 0

    def __call__(self, instruction):
        instruction.then_inc(self.sem, 1)
        self.n += 1

    def sync(self):
        self.eng.wait_ge(self.sem, self.n)

    def then(self, instruction):
        self(instruction)
        self.sync()


class Memory:

    def __init__(self, nc, ctx):
        self.nc, self.ctx = nc, ctx

    def sb(self, name, shape, dt=F32):
        return self.ctx.enter_context(self.nc.sbuf_tensor(name, shape, dt))

    def ps(self, name, shape, dt=F32):
        return self.ctx.enter_context(self.nc.psum_tensor(name, shape, dt))

    def sem(self, name):
        return self.ctx.enter_context(self.nc.semaphore(name))

    def scratch(self, name, shape, dt=F32):
        return self.nc.dram_tensor(name, shape, dt, kind="Internal").ap()


def norm_chunk(dve, step, x, xn, stat, c, std_wanted, std_ready):
    mv, var, std, tmp = stat["mv"], stat["var"], stat["std"], stat["tmp"]
    tiles = range(c * TC, (c + 1) * TC)
    cs = slice(c * TC, (c + 1) * TC)
    for i in tiles:
        step(dve.bn_stats(stat["bn"][:, i, :], x[:, i, :]))
    step.sync()
    for i in tiles:
        step(dve.bn_aggr(mv[:, i, :], stat["bn"][:, i, :]))
    step.sync()
    dve.tensor_scalar(var[:, cs], mv[:, cs, 1], EPS, None, ALU.add).then_inc(std_wanted, 1)
    dve.wait_ge(std_wanted, c + 1)
    dve.wait_ge(std_ready, c + 1)
    step.then(dve.reciprocal(std[:, cs], std[:, cs]))
    step.then(dve.tensor_tensor(tmp[:, cs], std[:, cs], std[:, cs], ALU.mult))
    step.then(dve.tensor_tensor(tmp[:, cs], tmp[:, cs], var[:, cs], ALU.mult))
    step.then(dve.tensor_scalar(tmp[:, cs], tmp[:, cs], -0.5, 1.5, ALU.mult, ALU.add))
    step.then(dve.tensor_tensor(std[:, cs], std[:, cs], tmp[:, cs], ALU.mult))
    for i in tiles:
        step(dve.tensor_scalar(xn[:, i, 0:D], x[:, i, :], mv[:, i, 0:1], std[:, i:i + 1],
                               ALU.subtract, ALU.mult))


def route(dve, step, r, scores, top, tiles, eps, factor, masks_ready, ranks_ready, slots_ready):
    best, arg, argf = r["best"], r["arg"], r["argf"]
    for i in range(T):
        step(dve.max(best[:, i, :], scores[:, i, :]))
    step.sync()
    yield
    for i in range(T):
        step(dve.max_index(arg[:, i, :], best[:, i, :], scores[:, i, :]))
    step.sync()
    yield
    step.then(dve.tensor_copy(argf[:, :, :], arg[:, :, :]))
    yield
    for k in range(top):
        step(dve.tensor_tensor(r["hot"][:, k, :, :], argf[:, :, k:k + 1].to_broadcast([P, T, E]),
                               r["iota_e"][:, 0:1, :].to_broadcast([P, T, E]), ALU.is_equal))
    step.sync()
    yield
    step.then(dve.tensor_tensor(r["any"][:, :, :], r["hot"][:, 0, :, :], r["hot"][:, 1, :, :], ALU.add))
    yield
    for k in range(2, top):
        step.then(dve.tensor_tensor(r["any"][:, :, :], r["any"][:, :, :], r["hot"][:, k, :, :], ALU.add))
        yield
    dve.tensor_copy(r["any16"][:, :, :], r["any"][:, :, :]).then_inc(masks_ready, 1)
    yield "masks"
    step.then(dve.tensor_reduce(r["sum"][:, :], best[:, :, 0:top], AX_X, ALU.add))
    yield
    if eps:
        step.then(dve.tensor_scalar(r["sum"][:, :], r["sum"][:, :], eps, None, ALU.add))
        yield
    step.then(dve.reciprocal(r["sum"][:, :], r["sum"][:, :]))
    yield
    step(dve.scalar_tensor_tensor(r["weight"][:, :, 0:top], best[:, :, 0:top], factor,
                                  r["sum"][:, :].unsqueeze(2).to_broadcast([P, T, top]), ALU.mult, ALU.mult))
    dve.wait_ge(ranks_ready, 1)
    count, before, total = r["count"], r["before"], r["total"]
    step.then(dve.tensor_copy(count[:, :, :], r["ps_count"].rearrange("p (i e) -> p e i", e=E)))
    yield
    step.then(dve.tensor_tensor_scan(before[:, :, :].rearrange("p e i -> p (e i)"),
                                     r["within"][:, :], count[:, :, :].rearrange("p e i -> p (e i)"),
                                     0.0, ALU.mult, ALU.add))
    yield
    step.then(dve.tensor_scalar(total[:, :], before[:, :, T - 1], float(P - 1), None, ALU.add))
    yield
    step.then(dve.tensor_copy(r["total_i"][:, :], total[:, :]))
    yield
    step.then(dve.tensor_scalar(r["total_i"][:, :], r["total_i"][:, :], 7, None, ALU.arith_shift_right))
    yield
    step.then(dve.tensor_copy(total[:, :], r["total_i"][:, :]))
    yield
    step.then(dve.tensor_tensor_scan(r["end"][:, :], r["ones_e"][:, :], total[:, :], 0.0, ALU.mult, ALU.add))
    yield
    step.then(dve.tensor_tensor(total[:, :], r["end"][:, :], total[:, :], ALU.subtract))
    yield
    step.then(dve.tensor_scalar(total[:, :], total[:, :], float(P), None, ALU.mult))
    yield
    step.then(dve.tensor_tensor(before[:, :, :], before[:, :, :], count[:, :, :], ALU.subtract))
    yield
    step.then(dve.tensor_tensor(before[:, :, :], before[:, :, :],
                                total[:, :].unsqueeze(2).to_broadcast([P, E, T]), ALU.add))
    yield
    step.then(dve.tensor_tensor(count[:, :, :], r["ps_rank"].rearrange("p (i e) -> p e i", e=E),
                                before[:, :, :], ALU.add))
    yield
    for k in range(top):
        step.then(dve.tensor_tensor(r["any"][:, :, :], r["hot"][:, k, :, :],
                                    count[:, :, :].rearrange("p e i -> p i e"), ALU.mult))
        yield
        step.then(dve.tensor_reduce(r["slotf"][:, k, :], r["any"][:, :, :], AX_X, ALU.add))
        yield
    dve.tensor_copy(r["slot"][:, 0:top, :], r["slotf"][:, 0:top, :]).then_inc(slots_ready, 1)
    step.then(dve.tensor_tensor(r["ended"][:, 0:tiles, :], r["end"][0:1, :].unsqueeze(1).to_broadcast([1, tiles, E]),
                                r["iota_t"][0:1, 0:tiles].unsqueeze(2).to_broadcast([1, tiles, E]), ALU.is_le))
    yield
    step.then(dve.tensor_reduce(r["tilef"][:, 0:tiles], r["ended"][:, 0:tiles, :], AX_X, ALU.add))
    yield
    step.then(dve.tensor_scalar(r["tilef"][:, 0:tiles], r["tilef"][:, 0:tiles], float(E - 1), None, ALU.min))
    yield
    dve.tensor_copy(r["tile_e"][:, EPAD:EPAD + tiles], r["tilef"][:, 0:tiles]).then_inc(slots_ready, 1)


def route_ranks(pe, r, masks_ready, ranks_ready):
    pe.wait_ge(masks_ready, 1)
    flat = r["any16"][:, :, :].rearrange("p i e -> p (i e)")
    pe.matmul(r["ps_rank"], r["before16"][:, :], flat, start=True, stop=True)
    pe.matmul(r["ps_count"], r["ones16"][:, :], flat, start=True, stop=True).then_inc(ranks_ready, 1)


PB = 4
RANKS_AFTER = 5


def load_keys(eng, m, g, tokens, done):
    for t in range(TERMS):
        src = m.qk_parts[K_PART[t], D + g * HG * HD:D + (g + 1) * HG * HD, tokens]
        eng.dma_start(m.ks[g % 2][t * HD:(t + 1) * HD, :, tokens], src.rearrange("(h d) t -> d h t", d=HD)).then_inc(done, 16)


def load_queries(eng, m, g, c, done):
    for t in range(TERMS):
        src = m.qk_parts[Q_PART[t], g * HG * HD:(g + 1) * HG * HD, c * CH:(c + 1) * CH]
        eng.dma_start(m.qs[c][t * HD:(t + 1) * HD, :, :], src.rearrange("(h d) t -> d h t", d=HD)).then_inc(done, 16)


def load_first_group(eng, m, c):
    for n in range(4 * c, 4 * c + 4):
        eng.wait_ge(m.parts_out[n], 16)
    load_keys(eng, m, 0, slice(c * CH, (c + 1) * CH), m.first_in[c])
    load_queries(eng, m, 0, c, m.first_in[c])


CLEAR = 16


def clear(eng, m, buf, first, last, done):
    for at in range(first, last, CLEAR):
        n = min(CLEAR, last - at)
        eng.dma_start(buf.rearrange("(j p) d -> p j d", p=P)[:, at:at + n, :],
                      m.zeros[:, :].unsqueeze(1).to_broadcast([P, n, D])).then_inc(done, 16)


def stage_project(nc, m, a):
    with ExitStack() as ctx:
        l = Memory(nc, ctx)
        wqk = l.sb("wqk", [P, KH, 2 * D])
        wvg = l.sb("wvg", [P, KH, D + E])
        xt = l.sb("xt", [P, KH, S])
        xn = m.xn
        parts = m.o_t[:, 0:2, :].rearrange("p g s -> p (g s)").bitcast(BF16)[:, 0:PB * PARTS * CH].rearrange(
            "p (b r t) -> p b r t", b=PB, r=PARTS)
        rest = l.sb("rest", [P, 2, CH])
        bias = l.sb("bias", [P, E])
        scores = l.sb("scores", [P, T, E])
        ps_t = [l.ps(f"ps_t{b}", [P, KH, P]) for b in range(2)]
        ps_qk = [l.ps(f"ps_qk{b}", [P, CH]) for b in range(2)]
        ps_v = [l.ps(f"ps_v{b}", [P, D + E]) for b in range(2)]
        ps_r = l.ps("ps_r0", [P, 2, D])
        stat, r = m.stat, dict(m.r)
        r["ps_rank"], r["ps_count"] = ps_r[:, 0, :], ps_r[:, 1, :]

        x_in = [l.sem(f"a_x_in{c}") for c in range(C)]
        w_in = l.sem("a_w_in")
        vg_in = l.sem("a_vg_in")
        b_in = l.sem("a_b_in")
        std_wanted, std_ready = l.sem("a_std_wanted"), l.sem("a_std_ready")
        step_sem = l.sem("a_dve")
        xn_ready, t_done, xt_ready = l.sem("a_xn_ready"), l.sem("a_t_done"), l.sem("a_xt_ready")
        qk_done, high_ready, rest_ready = l.sem("a_qk_done"), l.sem("a_high_ready"), l.sem("a_rest_ready")
        mid_ready, low_ready = l.sem("a_mid_ready"), l.sem("a_low_ready")
        v_done, v_copied = l.sem("a_v_done"), l.sem("a_v_copied")
        logit_ready, exp_ready = l.sem("a_logit_ready"), l.sem("a_exp_ready")
        masks_ready, ranks_ready = l.sem("a_masks_ready"), l.sem("a_ranks_ready")
        slots_ready = l.sem("a_slots_ready")
        pool_step, consts = l.sem("a_pool"), l.sem("a_consts")
        zero_ready = l.sem("a_zero_ready")

        block = ctx.enter_context(nc.Block())

        @block.sync
        def _(sp):
            for c in range(C):
                sp.dma_start(m.x[:, c * TC:(c + 1) * TC, :],
                             a["x"][0, c * CH:(c + 1) * CH, :].rearrange("(i p) d -> p i d", p=P)).then_inc(x_in[c], 16)
            sp.wait_ge(zero_ready, 1)

            clear(sp, m, m.xd0, 0, NT0, m.cleared[0])
            for n in range(4 * C):
                c, o = n // 4, n % 4
                sp.wait_ge(low_ready, n + 1)
                sp.dma_start(m.qk_parts[:, o * P:(o + 1) * P, c * CH:(c + 1) * CH].rearrange("r p t -> p r t"),
                             parts[:, n % PB, :, :]).then_inc(m.parts_out[n], 16)
                if 0 < c <= 2 and o == 1:
                    load_first_group(sp, m, c - 1)

        @block.gpsimd
        def _(pool):
            step = Steps(pool, pool_step)
            step(pool.memset(m.zeros[:, :], 0.0))
            step(pool.memset(m.zero16[:, :], 0.0))
            pool.memset(m.ident[:, :], 0.0).then_inc(pool_step, 1)
            step.n += 1
            step.sync()
            pool.memset(m.ones_f[:, :], 1.0).then_inc(zero_ready, 1)
            step(pool.affine_select(out=m.ident[:, :], in_=m.ident[:, :], compare_op=ALU.not_equal, fill=1.0,
                                    base=0, pattern=[[-1, P]], channel_multiplier=1))
            step(pool.iota(m.iota_i[:, 0:P], [[1, P]], base=0, channel_multiplier=0))
            pool.wait_ge(zero_ready, 1)
            step(pool.affine_select(out=m.before_f[:, :], in_=m.ones_f[:, :], compare_op=ALU.is_gt, fill=0.0,
                                    base=0, pattern=[[1, P]], channel_multiplier=-1))
            step(pool.affine_select(out=m.within[:, :].rearrange("p (e i) -> p e i", i=T),
                                    in_=m.ones_f[:, 0:1].unsqueeze(2).to_broadcast([P, E, T]),
                                    compare_op=ALU.is_gt, fill=0.0, base=0, pattern=[[0, E], [1, T]],
                                    channel_multiplier=0))
            step(pool.memset(m.r["tile_e"][:, :], 0))
            step.sync()
            step(pool.tensor_scalar(m.mask_f[:, :], m.before_f[:, :], NEG, None, ALU.mult))
            step(pool.memset(m.v_all[:, :, :, HD:HD + 1], 1.0))
            step.sync()
            pool.tensor_copy(m.iota_f[:, :], m.iota_i[:, :]).then_inc(consts, 1)
            pool.wait_ge(consts, 1)
            for b in range(2):
                step.then(pool.memset(m.ks[b][KROWS:MROWS, :, :], 1.0))
            for n in range(4 * C):
                pool.wait_ge(mid_ready, n + 1)
                pool.tensor_tensor(parts[:, n % PB, 2, :], rest[:, n % 2, :], parts[:, n % PB, 1, :],
                                   ALU.subtract).then_inc(low_ready, 1)

        @block.scalar
        def _(act):
            w_qkv = a["w_qkv_t"].rearrange("(k p) o -> p k o", p=P)
            act.dma_start(wvg[:, :, 0:D], w_qkv[:, :, 2 * D:3 * D]).then_inc(vg_in, 16)
            act.dma_start(wvg[:, :, D:D + E], a["wg_t"].rearrange("(k p) e -> p k e", p=P)).then_inc(vg_in, 16)
            act.dma_start(wqk[:, :, :], w_qkv[:, :, 0:2 * D]).then_inc(w_in, 16)
            act.dma_start(bias[:, :], a["balance_bias"].unsqueeze(0).to_broadcast([P, E])).then_inc(b_in, 16)
            act.dma_start(m.w1[:, :, :, :], a["w1"].rearrange("(k p) (e h) -> p k e h", p=P, e=E)).then_inc(m.moe0_w_in, 16)
            act.dma_start(m.w2[:, :, :], a["w2"].rearrange("e p d -> p e d")).then_inc(m.moe0_w_in, 16)
            def root(c):
                act.wait_ge(std_wanted, c + 1)
                act.activation(stat["std"][:, c * TC:(c + 1) * TC], stat["var"][:, c * TC:(c + 1) * TC],
                               ACT.Sqrt).then_inc(std_ready, 1)

            root(0)
            for i in range(T + 2):
                if i < T:
                    if i % TC == 0 and i // TC + 1 < C:
                        root(i // TC + 1)
                    act.wait_ge(t_done, i + 1)
                    act.copy(xt[:, :, i * P:(i + 1) * P], ps_t[i % 2][:, :, :]).then_inc(xt_ready, 1)
                if i >= 2:
                    act.wait_ge(v_done, i - 1)
                    act.copy(m.v_all[:, i - 2, :, 0:HD], ps_v[i % 2][:, 0:D].rearrange("p (h d) -> p h d", d=HD))
                    act.copy(scores[:, i - 2, :], ps_v[i % 2][:, D:D + E]).then_inc(v_copied, 1)
            act.wait_ge(logit_ready, 1)
            act.activation(scores[:, :, :], scores[:, :, :], ACT.Exp, scale=-1.0).then_inc(exp_ready, 1)
            for n in range(4 * C):
                act.wait_ge(qk_done, n + 1)
                if n >= PB:
                    act.wait_ge(m.parts_out[n - PB], 16)
                act.copy(parts[:, n % PB, 0, :], ps_qk[n % 2][:, :]).then_inc(high_ready, 1)
                act.wait_ge(rest_ready, n + 1)
                act.copy(parts[:, n % PB, 1, :], rest[:, n % 2, :]).then_inc(mid_ready, 1)

        @block.vector
        def _(dve):
            step = Steps(dve, step_sem)
            for c in range(C):
                dve.wait_ge(x_in[c], 16)
                norm_chunk(dve, step, m.x, xn, stat, c, std_wanted, std_ready)
                step.sync()
                dve.sem_inc(xn_ready, 1)
                if c == 0:
                    dve.wait_ge(consts, 1)
                    step(dve.tensor_copy(m.ident16[:, :], m.ident[:, :]))
                    step(dve.tensor_copy(m.ones16[:, :], m.ones_f[:, :]))
                    step(dve.tensor_copy(m.before16[:, :], m.before_f[:, :]))
                    step(dve.tensor_copy(m.mask16[:, :], m.mask_f[:, :]))
            dve.wait_ge(b_in, 16)
            dve.wait_ge(v_copied, T)
            dve.tensor_tensor(scores[:, :, :], scores[:, :, :], bias[:, :].unsqueeze(1).to_broadcast([P, T, E]),
                              ALU.add).then_inc(logit_ready, 1)
            dve.wait_ge(exp_ready, 1)
            step.then(dve.tensor_scalar(scores[:, :, :], scores[:, :, :], 1.0, None, ALU.add))
            step.then(dve.reciprocal(scores[:, :, :], scores[:, :, :]))
            routing = route(dve, step, r, scores, TOP0, NT0, 1e-6, 0.5, masks_ready, ranks_ready, slots_ready)
            for n in range(4 * C):
                dve.wait_ge(high_ready, n + 1)
                if n >= 2:
                    dve.wait_ge(low_ready, n - 1)
                dve.tensor_tensor(rest[:, n % 2, :], ps_qk[n % 2][:, :], parts[:, n % PB, 0, :],
                                  ALU.subtract).then_inc(rest_ready, 1)
                if n == RANKS_AFTER - 2:
                    while next(routing) != "masks":
                        pass
                    continue
                for _ in range(1 if n < RANKS_AFTER - 2 else 2 if n <= RANKS_AFTER else 5):
                    next(routing, None)
            for _ in routing:
                pass

        @block.tensor
        def _(pe):
            pe.wait_ge(consts, 1)
            for c in range(C):
                pe.wait_ge(xn_ready, c + 1)
                for i in range(c * TC, (c + 1) * TC):
                    if i >= 2:
                        pe.wait_ge(xt_ready, i - 1)
                    for k in range(KH):
                        mm = pe.transpose(ps_t[i % 2][:, k, :], xn[:, i, k * P:(k + 1) * P], m.ident[:, :])
                    mm.then_inc(t_done, 1)
                if c == 0:
                    pe.wait_ge(vg_in, 32)
                for i in range(c * TC, (c + 1) * TC):
                    pe.wait_ge(xt_ready, i + 1)
                    if i >= 2:
                        pe.wait_ge(v_copied, i - 1)
                    for k in range(KH):
                        mm = pe.matmul(ps_v[i % 2][:, :], xt[:, k, i * P:(i + 1) * P], wvg[:, k, :],
                                       start=(k == 0), stop=(k == KH - 1))
                    mm.then_inc(v_done, 1)
            pe.wait_ge(w_in, 16)
            for n in range(4 * C):
                c = n // 4
                if n >= 2:
                    pe.wait_ge(rest_ready, n - 1)
                for k in range(KH):
                    mm = pe.matmul(ps_qk[n % 2][:, :], wqk[:, k, (n % 4) * P:(n % 4 + 1) * P],
                                   xt[:, k, c * CH:(c + 1) * CH], start=(k == 0), stop=(k == KH - 1))
                mm.then_inc(qk_done, 1)
                if n == RANKS_AFTER:
                    route_ranks(pe, r, masks_ready, ranks_ready)


def common(nc, m):
    m.x = m.sb("x_res", [P, T, D])
    m.ident = m.sb("ident", [P, P])
    m.ident16 = m.sb("ident16", [P, P], BF16)
    m.ones_f = m.sb("ones_f", [P, P])
    m.ones16 = m.sb("ones16", [P, P], BF16)
    m.before_f = m.sb("before_f", [P, P])
    m.before16 = m.sb("before16", [P, P], BF16)
    m.mask_f = m.sb("mask_f", [P, P])
    m.mask16 = m.sb("mask16", [P, P], BF16)
    m.iota_i = m.sb("iota_i", [P, P], I32)
    m.iota_f = m.sb("iota_f", [P, P])
    m.within = m.sb("within", [P, E * T])
    m.stat = {"bn": m.sb("bn", [P, T, 6]), "mv": m.sb("mv", [P, T, 2]), "var": m.sb("var", [P, T]),
              "std": m.sb("std", [P, T]), "tmp": m.sb("ln_tmp", [P, T])}
    masks = m.sb("masks", [P, TOP1 + 1, T, E])
    m.r = {
        "best": m.sb("best", [P, T, 8]), "arg": m.sb("arg", [P, T, 8], U32), "argf": m.sb("argf", [P, T, 8]),
        "hot": masks[:, 0:TOP1, :, :], "any": masks[:, TOP1, :, :], "any16": m.sb("any16", [P, T, E], BF16),
        "sum": m.sb("top_sum", [P, T]), "weight": m.sb("weight", [P, T, TOP1]),
        "count": m.sb("count", [P, E, T]), "before": m.sb("before", [P, E, T]), "total": m.sb("total", [P, E]),
        "total_i": m.sb("total_i", [P, E], I32), "end": m.sb("end", [P, E]),
        "slotf": m.sb("slotf", [P, TOP1, T]), "slot": m.sb("slot", [P, TOP1, T], U32),
        "ended": masks[0:1, :, :, :].rearrange("p k i e -> p (k i e)")[:, 0:NT1 * E].rearrange("p (t e) -> p t e", e=E),
        "tilef": m.sb("tilef", [1, NT1]), "tile_e": m.sb("tile_e", [1, EPAD + NT1 + 3 * EPAD], I32),
        "iota_e": m.iota_f[:, 0:E].unsqueeze(1), "iota_t": m.iota_f, "ones_e": m.ones_f[:, 0:E],
        "within": m.within, "before16": m.before16, "ones16": m.ones16,
    }
    m.xd0 = m.scratch("xd0", [NT0 * P, D])
    m.xd1 = m.scratch("xd1", [NT1 * P, D])
    m.yd0 = m.scratch("yd0", [NT0 * P, D])
    m.yd1 = m.scratch("yd1", [NT1 * P, D])
    m.qk_parts = m.scratch("qk_parts", [PARTS, 2 * D, S], BF16)


def attention_plan():
    def exps(g, c):
        return [("exp", g, c, k, pair) for k in range(TC * (c + 1)) for pair in range(HG // 2)]

    def maxes(g, c):
        out = []
        for i in range(TC):
            for j in range(c):
                out += [("max", g, c, [(h, i, j, CH)]) for h in range(HG)]
            w = (i + 1) * P
            per = CH // w
            per = 4 if per >= 4 else 2 if per >= 2 else 1
            out += [("max", g, c, [(h, i, c, w) for h in range(h0, h0 + per)]) for h0 in range(0, HG, per)]
        return out

    def lead(chunks):
        units = []
        for n, (g, c) in enumerate(chunks):
            mine = maxes(g, c)
            if n:
                mine.insert(min(4, len(mine)), ("turn", *chunks[n - 1]))
            units += mine
        return units + [("turn", *chunks[-1])]

    plan = lead([(0, 0), (0, 1)])
    for g in range(NG):
        for now, ahead in (([(g, 0), (g, 1)], [(g, 2)]), ([(g, 2)], [(g, 3)]),
                           ([(g, 3)], [(g + 1, 0), (g + 1, 1)] if g + 1 < NG else [])):
            e = [u for gc in now for u in exps(*gc)]
            s = lead(ahead) if ahead else []
            done = 0
            for n, u in enumerate(e):
                plan.append(u)
                upto = min(len(s), int((n + 1) / (len(e) - TURN_AHEAD) * len(s)))
                plan += s[done:upto]
                done = max(done, upto)
    return with_experts(plan)


TURN_AHEAD = 7
MOE_START = 40
MOE_SPACE = 4.5
SUM_SPACE = 2


def with_experts(plan):
    moe = {}
    for slot in range(NT0 + 3):
        for k, name in enumerate("xhgy"):
            if 0 <= slot - k < NT0:
                moe.setdefault(MOE_START + int(MOE_SPACE * slot) + k, []).append((name, slot - k))
    first_sum = max(moe) + 8
    for i in range(T):
        moe.setdefault(first_sum + SUM_SPACE * i, []).append(("sum", i))
    out, at = [], 0
    for u in plan:
        out.append(u)
        if u[0] == "exp":
            at += 1
            out += moe.pop(at, [])
    for at in sorted(moe):
        out += moe[at]
    return out


def stage_attention(nc, m):
    plan = attention_plan()
    exps = [u for u in plan if u[0] == "exp"]
    rows = [u for u in plan if u[0] not in ("exp", "sum")]
    turns = [u for u in plan if u[0] == "turn"]
    row_of = {u[0:2]: n for n, u in enumerate(rows) if u[0] in "xhgy"}
    with ExitStack() as ctx:
        l = Memory(nc, ctx)
        qs, ks = m.qs, m.ks
        NPB = 6
        probs = l.sb("probs", [P, NPB, 2, CH])
        part_max = [l.sb(f"part_max{b}", [P, HG, TC, C]) for b in range(2)]
        neg_max = l.sb("neg_max", [P, HG * TC])
        max_rest = l.sb("max_rest", [HG * TC, P])
        max_parts = [l.sb(f"max_parts{b}", [HG * TC, PARTS, P], BF16) for b in range(2)]
        XB = 4
        xs = l.sb("moe0_xs", [P, XB, D])
        xs_t = l.sb("moe0_xs_t", [P, 2, KH, P])
        h_tanh = l.sb("moe0_h_tanh", [P, 2, HID])
        h_copy = l.sb("moe0_h_copy", [P, 2, HID])
        hid = l.sb("moe0_hid", [P, 2, HID])
        hid_t = l.sb("moe0_hid_t", [P, 2, P])
        ys = l.sb("moe0_ys", [P, XB, D])
        yg = l.sb("moe0_yg", [P, 2, TOP0, D])
        ps_st = [l.ps(f"ps_st{b}", [P, 2, CH]) for b in range(2)]
        NSM = 3
        ps_row = [l.ps(f"ps_row{b}", [P, CH]) for b in range(NSM)]
        ps_o = l.ps("ps_o", [P, CH])

        k_in = [l.sem(f"b_k_in{b}") for b in range(2)]
        q_in = [l.sem(f"b_q_in{c}") for c in range(C)]
        rows_in = [l.sem(f"b_rows_in{b}") for b in range(2)]
        st_done, exp_done, pv_done = l.sem("b_st_done"), l.sem("b_exp_done"), l.sem("b_pv_done")
        o_copied = l.sem("b_o_copied")
        row_done, row_used = l.sem("b_row_done"), l.sem("b_row_used")
        neg_ready, parts_ready = l.sem("b_neg_ready"), l.sem("b_parts_ready")
        step_sem, pool_sem = l.sem("b_dve"), l.sem("b_pool")
        dispatched = l.sem("b_dispatched")
        x_in = [l.sem(f"moe0_x_in{b}") for b in range(XB)]
        y_out = [l.sem(f"moe0_y_out{b}") for b in range(XB)]
        h_used, hid_ready = l.sem("moe0_h_used"), l.sem("moe0_hid_ready")
        gathered = [l.sem(f"moe0_gathered{b}") for b in range(2)]
        summed = l.sem("moe0_summed")
        block = ctx.enter_context(nc.Block())

        def last_pv(g, c):
            return (max(n for n, u in enumerate(exps) if u[1:3] == (g, c)) + 1) // 2

        def used(n):
            return sum(u[0] != "h" for u in rows[:n + 1])

        @block.sync
        def _(sp):
            for n in range(4 * 2, 4 * C):
                sp.wait_ge(m.parts_out[n], 16)
            load_keys(sp, m, 1, slice(0, S), k_in[1])
            at_tile = 0
            for n, (_, g, c) in enumerate(turns):
                sp.wait_ge(parts_ready, n + 1)
                for r in range(PARTS):
                    sp.dma_start(qs[c][KROWS + r:KROWS + r + 1, :, :].rearrange("r h t -> r (h t)"),
                                 max_parts[n % 2][:, r, :]).then_inc(rows_in[n % 2], 16)
                if c == 1 and g >= 1:
                    sp.wait_ge(pv_done, last_pv(g - 1, 3))
                    load_queries(sp, m, g, 3, q_in[3])
                if c == 2 and g + 1 < NG:
                    sp.wait_ge(pv_done, last_pv(g, 1))
                    load_queries(sp, m, g + 1, 0, q_in[0])
                    load_queries(sp, m, g + 1, 1, q_in[1])
                    if g >= 1:
                        load_keys(sp, m, g + 1, slice(0, S), k_in[(g + 1) % 2])
                if c == 3 and g + 1 < NG:
                    sp.wait_ge(pv_done, last_pv(g, 2))
                    load_queries(sp, m, g + 1, 2, q_in[2])
                if c >= 2 and at_tile < NT1:
                    clear(sp, m, m.xd1, at_tile, min(NT1, at_tile + CLEAR), m.cleared[1])
                    at_tile += CLEAR
            for b in range(2):
                sp.wait_ge(rows_in[b], 16 * MDMA * len(turns) // 2)

        @block.gpsimd
        def _(pool):
            step = Steps(pool, pool_sem)
            pool.wait_ge(m.cleared[0], 16 * -(-NT0 // CLEAR))
            for k in range(TOP0):
                for i in range(T):
                    pool.indirect_dma_start(out=m.xd0, out_offset=bass.IndirectOffsetOnAxis(m.r["slot"][:, k, i:i + 1], 0),
                                            in_=m.xn[:, i, :], in_offset=None).then_inc(dispatched, 16)
            pool.wait_ge(dispatched, 16 * TOP0 * T)

            def load(j):
                if j < NT0:
                    if j >= XB:
                        pool.wait_ge(row_done, row_of["x", j - XB] + 1)
                    pool.dma_start(xs[:, j % XB, :], m.xd0[j * P:(j + 1) * P, :]).then_inc(x_in[j % XB], 16)

            for j in range(3):
                load(j)
            for slot in range(NT0 + 3):
                load(slot + 3)
                j = slot - 1
                if 0 <= j < NT0:
                    pool.wait_ge(h_used, j + 1)
                    step.then(pool.tensor_scalar(h_tanh[:, j % 2, :], h_tanh[:, j % 2, :], 1.0, None, ALU.add))
                    if j >= 2:
                        pool.wait_ge(row_done, row_of["g", j - 2] + 1)
                    pool.tensor_tensor(hid[:, j % 2, :], h_tanh[:, j % 2, :], h_copy[:, j % 2, :],
                                       ALU.mult).then_inc(hid_ready, 1)
                j = slot - 3
                if j >= 0:
                    pool.wait_ge(row_used, used(row_of["y", j]))
                    pool.dma_start(m.yd0[j * P:(j + 1) * P, :], ys[:, j % XB, :]).then_inc(y_out[j % XB], 16)
            for b in range(XB):
                pool.wait_ge(y_out[b], 16 * len(range(b, NT0, XB)))
            for i in range(T):
                if i >= 2:
                    pool.wait_ge(summed, (i - 1) * TOP0)
                for k in range(TOP0):
                    pool.indirect_dma_start(out=yg[:, i % 2, k, :], out_offset=None, in_=m.yd0,
                                            in_offset=bass.IndirectOffsetOnAxis(m.r["slot"][:, k, i:i + 1], 0)
                                            ).then_inc(gathered[i % 2], 16)

        @block.scalar
        def _(act):
            def copy_output(at):
                g, c = exps[at][1:3]
                act.wait_ge(pv_done, (at + 1) // 2)
                act.copy(m.o_t[:, g, c * CH:(c + 1) * CH], ps_o[:, :]).then_inc(o_copied, 1)

            for c in range(2, C):
                load_first_group(act, m, c)
            at = 0
            for u in plan:
                if u[0] == "exp":
                    g, c, k = u[1:4]
                    off = max(0, k - TC * c) * P
                    act.wait_ge(st_done, at + 1)
                    if at >= NPB:
                        act.wait_ge(pv_done, (at - NPB) // 2 + 1)
                    act.activation(probs[:, at % NPB, :, off:CH], ps_st[at % 2][:, :, off:CH], ACT.Exp,
                                   scale=HD ** -0.5).then_inc(exp_done, 1)
                    if at >= 2 and exps[at - 2][1:3] != (g, c) and exps[at - 1][1:3] == (g, c):
                        copy_output(at - 2)
                    at += 1
                elif u[0] == "h":
                    j = u[1]
                    act.wait_ge(row_done, row_of["h", j] + 1)
                    if j >= 2:
                        act.wait_ge(hid_ready, j - 1)
                    bank = ps_row[row_of["h", j] % NSM]
                    act.activation(h_tanh[:, j % 2, :], bank[:, 0:HID], ACT.Tanh, scale=0.5)
                    act.copy(h_copy[:, j % 2, :], bank[:, 0:HID]).then_inc(h_used, 1)
            copy_output(len(exps) - 1)

        @block.vector
        def _(dve):
            step = Steps(dve, step_sem)
            turned, reduced, n = 0, 0, -1
            for u in plan:
                if u[0] == "exp":
                    continue
                if u[0] == "sum":
                    i = u[1]
                    dve.wait_ge(gathered[i % 2], 16 * TOP0 * (i // 2 + 1))
                    for k in range(TOP0):
                        dve.scalar_tensor_tensor(m.x[:, i, :], yg[:, i % 2, k, :], m.r["weight"][:, i, k:k + 1],
                                                 m.x[:, i, :], ALU.mult, ALU.add).then_inc(summed, 1)
                        dve.wait_ge(summed, i * TOP0 + k + 1)
                    continue
                n += 1
                if u[0] == "h":
                    continue
                dve.wait_ge(row_done, n + 1)
                bank = ps_row[n % NSM]
                if u[0] == "x":
                    dve.tensor_copy(xs_t[:, u[1] % 2, :, :],
                                    bank[:, 0:D].rearrange("p (k t) -> p k t", k=KH)).then_inc(row_used, 1)
                elif u[0] == "g":
                    dve.tensor_copy(hid_t[:, u[1] % 2, :], bank[:, 0:P]).then_inc(row_used, 1)
                elif u[0] == "y":
                    j = u[1]
                    if j >= XB:
                        dve.wait_ge(y_out[j % XB], 16 * (j // XB))
                    dve.tensor_copy(ys[:, j % XB, :], bank[:, 0:D]).then_inc(row_used, 1)
                elif u[0] == "max":
                    g, c, pieces = u[1:]
                    h, i, j, w = pieces[0]
                    k = len(pieces)
                    if reduced >= 2:
                        dve.wait_ge(neg_ready, reduced - 1)
                    dve.tensor_reduce(part_max[reduced % 2][:, h:h + k, i, j:j + 1],
                                      bank[:, 0:k * w].rearrange("p (h w) -> p h w", h=k),
                                      AX_X, ALU.max).then_inc(row_used, 1)
                    after = [v for v in rows[n + 1:] if v[0] == "max"][:1]
                    if not after or after[0][1:3] != (g, c):
                        dve.wait_ge(row_used, used(n))
                        dve.tensor_reduce(neg_max[:, :], part_max[reduced % 2][:, :, :, 0:c + 1].rearrange("p h i j -> p (h i) j"),
                                          AX_X, ALU.max, negate=True).then_inc(neg_ready, 1)
                        reduced += 1
                else:
                    parts = max_parts[turned % 2]
                    turned_ps = bank[0:HG * TC, 0:P]
                    if turned >= 2:
                        dve.wait_ge(rows_in[turned % 2], 16 * MDMA * (turned // 2))
                    step.then(dve.tensor_copy(parts[:, 0, :], turned_ps))
                    dve.tensor_tensor(max_rest[:, :], turned_ps, parts[:, 0, :], ALU.subtract).then_inc(row_used, 1)
                    dve.wait_ge(row_used, used(n))
                    step.then(dve.tensor_copy(parts[:, 1, :], max_rest[:, :]))
                    dve.tensor_tensor(parts[:, 2, :], max_rest[:, :], parts[:, 1, :],
                                      ALU.subtract).then_inc(parts_ready, 1)
                    dve.wait_ge(parts_ready, turned + 1)
                    turned += 1

        @block.tensor
        def _(pe):
            state = {"exp": 0, "pv": 0, "row": 0, "turn": 0, "parts": None, "chunk": None, "out": 0}
            turn_of = {u[1:3]: n for n, u in enumerate(turns)}
            experts = {}

            def parts_there(g, c):
                if (g, c) == state["parts"]:
                    return
                state["parts"] = (g, c)
                if g == 0:
                    pe.wait_ge(m.first_in[c], 16 * 2 * TERMS)
                    return
                pe.wait_ge(q_in[c], 16 * TERMS * g)
                if c == 0:
                    pe.wait_ge(k_in[g % 2], 16 * TERMS * ((g + 1) // 2))

            def values():
                at = state["pv"]
                _, g, c, k, _ = exps[at]
                off = max(0, k - TC * c) * P
                pe.wait_ge(exp_done, at + 2)
                if k == 0 and at:
                    state["out"] += 1
                    pe.wait_ge(o_copied, state["out"])
                for q in range(HG):
                    mm = pe.matmul(ps_o[32 * q:32 * q + HD + 1, off:CH], m.v_all[:, k, g * HG + q, :],
                                   probs[:, (at + q // 2) % NPB, q % 2, off:CH], start=(k == 0),
                                   stop=(k == TC * (c + 1) - 1), tile_position=(0, 32 * q))
                mm.then_inc(pv_done, 1)
                state["pv"] += 2

            def bank_free(n):
                if n < NSM:
                    return
                before = rows[n - NSM]
                if before[0] == "h":
                    pe.wait_ge(h_used, before[1] + 1)
                else:
                    pe.wait_ge(row_used, used(n - NSM))

            for i in range(TC):
                pe.matmul(ps_o[:, i * P:(i + 1) * P], m.zero16[:, :], m.ident16[:, :], start=True, stop=True)
            for u in plan:
                if u[0] == "exp":
                    g, c, k, pair = u[1:]
                    n = state["exp"]
                    off = max(0, k - TC * c) * P
                    if (g, c) != state["chunk"]:
                        t = turn_of[(g, c)]
                        pe.wait_ge(rows_in[t % 2], 16 * MDMA * (t // 2 + 1))
                        state["chunk"] = (g, c)
                    if n >= 2:
                        pe.wait_ge(exp_done, n - 1)
                    for h in range(2):
                        q = 2 * pair + h
                        diagonal = k >= TC * c
                        mm = pe.matmul(ps_st[n % 2][:, h, off:CH], ks[g % 2][:, q, k * P:(k + 1) * P],
                                       qs[c][:, q, off:CH], start=True, stop=not diagonal)
                        if diagonal:
                            mm = pe.matmul(ps_st[n % 2][:, h, off:off + P], m.mask16[:, :], m.ident16[:, :],
                                           start=False, stop=True)
                    mm.then_inc(st_done, 1)
                    state["exp"] += 1
                    if state["exp"] - state["pv"] > 3:
                        values()
                    continue
                if u[0] == "sum":
                    continue
                n = state["row"]
                state["row"] += 1
                bank = ps_row[n % NSM]
                if u[0] == "max":
                    g, c, pieces = u[1:]
                    parts_there(g, c)
                    bank_free(n)
                    for at, (h, i, j, w) in enumerate(pieces):
                        cols = bank[:, at * w:(at + 1) * w]
                        mm = pe.matmul(cols, qs[c][0:KROWS, h, i * P:(i + 1) * P],
                                       ks[g % 2][0:KROWS, h, j * CH:j * CH + w], start=True, stop=(j < c))
                        if j == c:
                            mm = pe.matmul(cols[:, w - P:w], m.ident16[:, :], m.mask16[:, :],
                                           start=False, stop=True)
                elif u[0] == "turn":
                    bank_free(n)
                    pe.wait_ge(neg_ready, state["turn"] + 1)
                    state["turn"] += 1
                    mm = pe.transpose(bank[0:HG * TC, 0:P], neg_max[:, :], m.ident[:, :])
                elif u[0] == "x":
                    j = u[1]
                    if j == 0:
                        pe.wait_ge(m.moe0_w_in, 32)
                    if j % 8 == 0:
                        loaded = nc.values_load_multi_w_load_instructions(
                            m.r["tile_e"][0:1, EPAD + j:EPAD + j + 8], engines=[mybir.EngineType.PE], min_val=0,
                            max_val=E - 1, skip_runtime_bounds_check_because=IN_RANGE)[1]
                        experts.update({j + n: e for n, e in enumerate(loaded)})
                    bank_free(n)
                    pe.wait_ge(x_in[j % XB], 16 * (j // XB + 1))
                    for k in range(KH):
                        mm = pe.transpose(bank[:, k * P:(k + 1) * P], xs[:, j % XB, k * P:(k + 1) * P], m.ident[:, :])
                elif u[0] == "h":
                    j = u[1]
                    bank_free(n)
                    pe.wait_ge(row_used, used(row_of["x", j]))
                    for k in range(KH):
                        mm = pe.matmul(bank[:, 0:HID], xs_t[:, j % 2, k, :], m.w1[:, k, bass.ds(experts[j], 1), :],
                                       start=(k == 0), stop=(k == KH - 1))
                elif u[0] == "g":
                    j = u[1]
                    bank_free(n)
                    pe.wait_ge(hid_ready, j + 1)
                    mm = pe.transpose(bank[:, 0:P], hid[:, j % 2, :], m.ident[:, :])
                else:
                    j = u[1]
                    bank_free(n)
                    pe.wait_ge(row_used, used(row_of["g", j]))
                    mm = pe.matmul(bank[:, 0:D], hid_t[:, j % 2, :], m.w2[:, bass.ds(experts.pop(j), 1), :],
                                   start=True, stop=True)
                mm.then_inc(row_done, 1)
            while state["pv"] < len(exps):
                values()


def stage_output(nc, m, a):
    with ExitStack() as ctx:
        l = Memory(nc, ctx)
        wo = l.sb("wo", [P, KH, D])
        rec = l.sb("rec", [P, 2, NH])
        heads = l.sb("heads", [P, 2, NH, HD])
        heads_t = l.sb("heads_t", [P, 2, KH, P])
        ps_o = [l.ps(f"ps_oo{b}", [P, NG, P]) for b in range(2)]
        ps_h = [l.ps(f"ps_h{b}", [P, KH, P]) for b in range(2)]
        ps_w = [l.ps(f"ps_w{b}", [P, D]) for b in range(2)]
        w_in, turned, rec_ready = l.sem("c_w_in"), l.sem("c_turned"), l.sem("c_rec_ready")
        heads_ready, back, back_copied = l.sem("c_heads_ready"), l.sem("c_back"), l.sem("c_back_copied")
        w_done, added = l.sem("c_w_done"), l.sem("c_added")
        block = ctx.enter_context(nc.Block())

        @block.sync
        def _(sp):
            sp.dma_start(wo[:, :, :], a["w_o_t"].rearrange("(k p) o -> p k o", p=P)).then_inc(w_in, 16)

        @block.scalar
        def _(act):
            for i in range(T):
                act.wait_ge(back, i + 1)
                if i >= 2:
                    act.wait_ge(w_done, i - 1)
                act.copy(heads_t[:, i % 2, :, :], ps_h[i % 2][:, :, :]).then_inc(back_copied, 1)

        @block.vector
        def _(dve):
            def normalize(i):
                dve.wait_ge(turned, i + 1)
                if i >= 2:
                    dve.wait_ge(back, i - 1)
                    dve.wait_ge(heads_ready, i - 1)
                by_head = ps_o[i % 2][:, :, :].rearrange("p g (h w) -> p (g h) w", w=32)
                dve.reciprocal(rec[:, i % 2, :], by_head[:, :, HD]).then_inc(rec_ready, 1)
                dve.wait_ge(rec_ready, i + 1)
                dve.tensor_tensor(heads[:, i % 2, :, :], by_head[:, :, 0:HD],
                                  rec[:, i % 2, :].unsqueeze(2).to_broadcast([P, NH, HD]),
                                  ALU.mult).then_inc(heads_ready, 1)

            def add(i):
                dve.wait_ge(w_done, i + 1)
                dve.tensor_tensor(m.x[:, i, :], ps_w[i % 2][:, :], m.x[:, i, :], ALU.add).then_inc(added, 1)

            for i in range(T + 2):
                if i < T:
                    normalize(i)
                if i >= 2:
                    add(i - 2)

        @block.tensor
        def _(pe):
            pe.wait_ge(w_in, 16)
            for i in range(T + 2):
                if i < T:
                    if i >= 2:
                        pe.wait_ge(heads_ready, i - 1)
                    for g in range(NG):
                        mm = pe.transpose(ps_o[i % 2][:, g, :], m.o_t[:, g, i * P:(i + 1) * P], m.ident[:, :])
                    mm.then_inc(turned, 1)
                if 1 <= i <= T:
                    j = i - 1
                    pe.wait_ge(heads_ready, j + 1)
                    if j >= 2:
                        pe.wait_ge(back_copied, j - 1)
                    for k in range(KH):
                        mm = pe.transpose(ps_h[j % 2][:, k, :],
                                          heads[:, j % 2, k * NH // KH:(k + 1) * NH // KH, :].rearrange("p h d -> p (h d)"),
                                          m.ident[:, :])
                    mm.then_inc(back, 1)
                if i >= 2:
                    j = i - 2
                    pe.wait_ge(back_copied, j + 1)
                    if j >= 2:
                        pe.wait_ge(added, j - 1)
                    for k in range(KH):
                        mm = pe.matmul(ps_w[j % 2][:, :], heads_t[:, j % 2, k, :], wo[:, k, :],
                                       start=(k == 0), stop=(k == KH - 1))
                    mm.then_inc(w_done, 1)


def rolled(eng, lag, tiles, unroll, tick, ahead=lambda j: None):
    start = -(-(lag + 2) // unroll) * unroll
    stop = start + (tiles - start) // unroll * unroll
    for j in range(start):
        if j % unroll == 0:
            ahead(j)
        tick(j, j % unroll)
    with eng.Fori(start, stop, unroll) as j:
        ahead(j)
        for u in range(unroll):
            tick(j + u, u)
    for j in range(stop, tiles + lag):
        if j % unroll == 0:
            ahead(j)
        tick(j, j % unroll)


def stage_experts(nc, m, out):
    tiles, top, xd, yd = NT1, TOP1, m.xd1, m.yd1
    W1 = 2 * HID
    OUT = 2
    U = 4
    BODY = 16
    with ExitStack() as ctx:
        l = Memory(nc, ctx)
        w1, w2 = m.w13, m.we2
        xs = l.sb("moe1_xs", [P, U, D])
        xs_t = l.sb("moe1_xs_t", [P, 2, KH, P])
        act_out = l.sb("moe1_act", [P, 2, HID])
        hid = l.sb("moe1_hid", [P, 2, HID])
        hid_t = l.sb("moe1_hid_t", [P, 2, P])
        ys = l.sb("moe1_ys", [P, U, D])
        yg = l.sb("moe1_yg", [P, 2, top, D])
        ps_x = [l.ps(f"moe1_ps_x{b}", [P, KH, P]) for b in range(2)]
        ps_h = [l.ps(f"moe1_ps_h{b}", [P, W1]) for b in range(2)]
        ps_g = [l.ps(f"moe1_ps_g{b}", [P, P]) for b in range(2)]
        ps_y = [l.ps(f"moe1_ps_y{b}", [P, D]) for b in range(2)]
        x_in = [l.sem(f"moe1_x_in{b}") for b in range(U)]
        y_out = [l.sem(f"moe1_y_out{b}") for b in range(U)]
        gathered = [l.sem(f"moe1_gathered{b}") for b in range(2)]
        x_turned, x_copied = l.sem("moe1_x_turned"), l.sem("moe1_x_copied")
        h_done, act_done, hid_ready = l.sem("moe1_h_done"), l.sem("moe1_act_done"), l.sem("moe1_hid_ready")
        g_turned, g_copied = l.sem("moe1_g_turned"), l.sem("moe1_g_copied")
        y_done, y_copied = l.sem("moe1_y_done"), l.sem("moe1_y_copied")
        summed = l.sem("moe1_summed")
        tail_done, tail_added, stored = l.sem("tail_done"), l.sem("tail_added"), l.sem("stored")
        block = ctx.enter_context(nc.Block())

        def there(j):
            return not isinstance(j, int) or 0 <= j < tiles

        def since(j, n):
            return not isinstance(j, int) or j >= n

        @block.sync
        def _(sp):
            def tick(j, u):
                if there(j):
                    if since(j, U):
                        sp.wait_ge(x_turned, j - (U - 1))
                    sp.dma_start(xs[:, u % U, :], xd[bass.ds(j * P, P), :]).then_inc(x_in[u % U], 16)
                k = j - 2 * U
                if there(k):
                    sp.wait_ge(y_copied, k + 1)
                    sp.dma_start(yd[bass.ds(k * P, P), :], ys[:, u % U, :]).then_inc(y_out[u % U], 16)

            rolled(sp, 2 * U, tiles, BODY, tick)
            for i in range(0, T, OUT):
                sp.wait_ge(summed, (i + OUT) * top)
                sp.dma_start(out[0, i * P:(i + OUT) * P, :].rearrange("(i p) d -> p i d", p=P),
                             m.x[:, i:i + OUT, :]).then_inc(stored, 16)
            sp.wait_ge(stored, 16 * T // OUT)

        @block.scalar
        def _(act):
            def tick(j, u):
                if there(j):
                    b = u % 2
                    act.wait_ge(x_turned, j + 1)
                    if since(j, 2):
                        act.wait_ge(h_done, j - 1)
                    act.copy(xs_t[:, b, :, :], ps_x[b][:, :, :]).then_inc(x_copied, 1)
                j = j - 1
                if there(j):
                    b = (u - 1) % 2
                    act.wait_ge(h_done, j + 1)
                    if since(j, 2):
                        act.wait_ge(hid_ready, j - 1)
                    act.activation(act_out[:, b, :], ps_h[b][:, 0:HID], ACT.Silu).then_inc(act_done, 1)

            rolled(act, 1, tiles, BODY, tick)

        @block.vector
        def _(dve):
            def tick(j, u):
                if there(j - 1):
                    b = (u - 1) % 2
                    dve.wait_ge(act_done, j)
                    if since(j - 1, 2):
                        dve.wait_ge(g_turned, j - 2)
                    dve.tensor_tensor(hid[:, b, :], ps_h[b][:, HID:2 * HID], act_out[:, b, :],
                                      ALU.mult).then_inc(hid_ready, 1)
                if there(j - 2):
                    b = u % 2
                    dve.wait_ge(g_turned, j - 1)
                    if since(j - 2, 2):
                        dve.wait_ge(y_done, j - 3)
                    dve.tensor_copy(hid_t[:, b, :], ps_g[b][:, :]).then_inc(g_copied, 1)
                if there(j - 3):
                    b = (u - 3) % 2
                    dve.wait_ge(y_done, j - 2)
                    to = (u - 3) % U
                    if since(j - 3, U):
                        dve.wait_ge(y_out[to], (j - 3 - to) * (16 // U))
                    dve.tensor_copy(ys[:, to, :], ps_y[b][:, :]).then_inc(y_copied, 1)

            rolled(dve, 3, tiles, BODY, tick)
            for i in range(T):
                dve.wait_ge(tail_done, i + 1)
                dve.scalar_tensor_tensor(m.x[:, i, :], ps_h[i % 2][:, 0:D], 1.0 / (TOP1 + 1), m.x[:, i, :],
                                         ALU.mult, ALU.add).then_inc(tail_added, 1)
            dve.wait_ge(tail_added, T)
            for i in range(T):
                dve.wait_ge(gathered[i % 2], 16 * top * (i // 2 + 1))
                for k in range(top):
                    dve.scalar_tensor_tensor(m.x[:, i, :], yg[:, i % 2, k, :], m.r["weight"][:, i, k:k + 1],
                                             m.x[:, i, :], ALU.mult, ALU.add).then_inc(summed, 1)
                    dve.wait_ge(summed, i * top + k + 1)

        @block.gpsimd
        def _(pool):
            for b in range(U):
                pool.wait_ge(y_out[b], 16 * len(range(b, tiles, U)))
            for i in range(T):
                if i >= 2:
                    pool.wait_ge(summed, (i - 1) * top)
                for k in range(top):
                    pool.indirect_dma_start(out=yg[:, i % 2, k, :], out_offset=None, in_=yd,
                                            in_offset=bass.IndirectOffsetOnAxis(m.r["slot"][:, k, i:i + 1], 0)
                                            ).then_inc(gathered[i % 2], 16)

        @block.tensor
        def _(pe):
            pe.wait_ge(m.moe1_w_in, 32)

            experts = []

            def load_experts(j):
                experts[:] = nc.values_load_multi_w_load_instructions(
                    m.r["tile_e"][0:1, bass.ds(j + (EPAD - U), U + BODY)], engines=[mybir.EngineType.PE], min_val=0,
                    max_val=E - 1, skip_runtime_bounds_check_because=IN_RANGE)[1]

            def tick(j, u):
                if there(j):
                    b = u % 2
                    pe.wait_ge(x_in[u % U], (j - u % U) * (16 // U) + 16)
                    if since(j, 2):
                        pe.wait_ge(x_copied, j - 1)
                    for k in range(KH):
                        mm = pe.transpose(ps_x[b][:, k, :], xs[:, u % U, k * P:(k + 1) * P], m.ident[:, :])
                    mm.then_inc(x_turned, 1)
                if there(j - 1):
                    b = (u - 1) % 2
                    e = experts[U + u - 1]
                    pe.wait_ge(x_copied, j)
                    if since(j - 1, 2):
                        pe.wait_ge(hid_ready, j - 2)
                    for k in range(KH):
                        mm = pe.matmul(ps_h[b][:, :], xs_t[:, b, k, :], w1[:, k, bass.ds(e, 1), :],
                                       start=(k == 0), stop=(k == KH - 1))
                    mm.then_inc(h_done, 1)
                if there(j - 2):
                    b = u % 2
                    pe.wait_ge(hid_ready, j - 1)
                    if since(j - 2, 2):
                        pe.wait_ge(g_copied, j - 3)
                    pe.transpose(ps_g[b][:, :], hid[:, b, :], m.ident[:, :]).then_inc(g_turned, 1)
                if there(j - 3):
                    b = (u - 3) % 2
                    e = experts[U + u - 3]
                    pe.wait_ge(g_copied, j - 2)
                    if since(j - 3, 2):
                        pe.wait_ge(y_copied, j - 4)
                    pe.matmul(ps_y[b][:, :], hid_t[:, b, :], w2[:, bass.ds(e, 1), :],
                              start=True, stop=True).then_inc(y_done, 1)

            rolled(pe, 3, tiles, BODY, tick, load_experts)
            pe.wait_ge(m.tail_in, 16)
            pe.wait_ge(hid_ready, tiles)
            for i in range(T):
                if i >= 2:
                    pe.wait_ge(tail_added, i - 1)
                for s in range(HS // P):
                    pe.matmul(ps_h[i % 2][:, 0:D], m.hid_s[:, s, i * P:(i + 1) * P], m.ws2[:, s, :],
                              start=(s == 0), stop=False)
                for k in range(KH):
                    mm = pe.matmul(ps_h[i % 2][:, 0:D], m.xt2[:, k, i * P:(i + 1) * P], m.wq[:, k, :],
                                   start=False, stop=(k == KH - 1))
                mm.then_inc(tail_done, 1)


ROUTE_FIRST = 14
GRAM_FIRST = 8


def stage_second(nc, m, a):
    with ExitStack() as ctx:
        l = Memory(nc, ctx)
        DP = D + 1
        xn = l.sb("xn2", [P, T, DP])
        w = l.sb("w_attn", [P, KH, 3 * D])
        wr = l.sb("w_router", [P, KH, E])
        ws1 = l.sb("ws1", [P, KH, HS])
        ws3 = l.sb("ws3", [P, KH, HS])
        bias = l.sb("bias_qkv", [P, 3 * D])
        scores = l.sb("scores2", [P, T, E])
        peak = l.sb("peak", [P, T])
        gram = l.sb("gram", [P, KH, DP])
        sums = l.sb("sums", [P, KH, P])
        prod = l.sb("prod", [P, KH, 3 * D])
        square = l.sb("square", [P, 2 * D])
        root = l.sb("root", [P, 2 * D])
        kv = l.sb("kv", [P, D])
        t1, t2 = l.sb("t1", [P, 2 * D]), l.sb("t2", [P, D])
        bq = l.sb("bq", [P, D])
        gate = l.sb("gate", [P, 2, CH])
        xt, hid, wq = m.xt2, m.hid_s, m.wq
        ps_t = [l.ps(f"ps_t2{b}", [P, CH]) for b in range(2)]
        ps_g = [l.ps(f"ps_gram{b}", [P, DP]) for b in range(KH)]
        ps_l = l.ps("ps_l2", [P, T, E])
        ps_ab = [l.ps(f"ps_ab{b}", [P, CH]) for b in range(2)]
        ps_o = l.ps("ps_o2", [P, 2, D])
        stat, r = m.stat, dict(m.r)
        w_in, b_in, s_in = l.sem("e_w_in"), l.sem("e_b_in"), l.sem("e_s_in")
        std_wanted, std_ready, step_sem = l.sem("e_std_wanted"), l.sem("e_std_ready"), l.sem("e_dve")
        ones_ready = l.sem("e_ones_ready")
        xn_ready, t_done, xt_ready, l_done = l.sem("e_xn_ready"), l.sem("e_t_done"), l.sem("e_xt_ready"), l.sem("e_l_done")
        logit_ready, exp_ready = l.sem("e_logit_ready"), l.sem("e_exp_ready")
        masks_ready, ranks_ready, slots_ready = l.sem("e_masks_ready"), l.sem("e_ranks_ready"), l.sem("e_slots_ready")
        dispatched = l.sem("e_dispatched")
        gram_done, gram_copied = l.sem("e_gram_done"), l.sem("e_gram_copied")
        gw_done, prod_ready, norms_done = l.sem("e_gw_done"), l.sem("e_prod_ready"), l.sem("e_norms_done")
        square_ready, root_ready = l.sem("e_square_ready"), l.sem("e_root_ready")
        a_done, gate_ready, b_done, hid_ready = l.sem("e_a_done"), l.sem("e_gate_ready"), l.sem("e_b_done"), l.sem("e_hid_ready")
        ab = [ps_ab, ps_t]
        r["ps_rank"], r["ps_count"] = ps_o[:, 0, :], ps_o[:, 1, :]
        block = ctx.enter_context(nc.Block())
        units = [(c, s) for c in range(C) for s in range(HS // P)]

        @block.sync
        def _(sp):
            sp.dma_start(w[:, :, :], a["w_attn"].rearrange("(k p) o -> p k o", p=P)).then_inc(w_in, 16)
            sp.dma_start(wr[:, :, :], a["w_router"].rearrange("(k p) e -> p k e", p=P)).then_inc(w_in, 16)
            sp.dma_start(bias[:, :], a["b_attn"].unsqueeze(0).to_broadcast([P, 3 * D])).then_inc(b_in, 16)
            sp.dma_start(ws1[:, :, :], a["ws1"].rearrange("(k p) o -> p k o", p=P)).then_inc(s_in, 16)
            sp.dma_start(ws3[:, :, :], a["ws3"].rearrange("(k p) o -> p k o", p=P)).then_inc(s_in, 16)
            sp.dma_start(m.ws2[:, :, :], a["ws2"].rearrange("(k p) o -> p k o", p=P)).then_inc(m.tail_in, 16)
            sp.dma_start(m.w13[:, :, :, :], a["we13"].rearrange("(k p) (e h) -> p k e h", p=P, e=E)).then_inc(m.moe1_w_in, 16)
            sp.dma_start(m.we2[:, :, :], a["we2"].rearrange("e p d -> p e d")).then_inc(m.moe1_w_in, 16)

        @block.gpsimd
        def _(pool):
            pool.memset(xn[:, :, D:DP], 1.0).then_inc(ones_ready, 1)
            pool.wait_ge(m.cleared[1], 16 * -(-NT1 // CLEAR))
            pool.wait_ge(slots_ready, 1)
            for k in range(TOP1):
                for i in range(T):
                    pool.indirect_dma_start(out=m.xd1, out_offset=bass.IndirectOffsetOnAxis(r["slot"][:, k, i:i + 1], 0),
                                            in_=xn[:, i, 0:D], in_offset=None).then_inc(dispatched, 16)
            pool.wait_ge(dispatched, 16 * TOP1 * T)

        @block.scalar
        def _(act):
            def root_of(c):
                act.wait_ge(std_wanted, c + 1)
                act.activation(stat["std"][:, c * TC:(c + 1) * TC], stat["var"][:, c * TC:(c + 1) * TC],
                               ACT.Sqrt).then_inc(std_ready, 1)

            root_of(0)
            for i in range(T):
                if i % TC == 0 and i // TC + 1 < C:
                    root_of(i // TC + 1)
                act.wait_ge(t_done, i + 1)
                act.copy(xt[:, :, i * P:(i + 1) * P],
                         ps_t[i % 2][:, 0:D].rearrange("p (k t) -> p k t", k=KH)).then_inc(xt_ready, 1)
            act.wait_ge(logit_ready, 1)
            act.activation(scores[:, :, :], scores[:, :, :], ACT.Exp).then_inc(exp_ready, 1)
            act.wait_ge(gram_done, 1)
            for k in range(KH):
                act.copy(gram[:, k, :], ps_g[k][:, :]).then_inc(gram_copied, 1)
            for n in range(len(units)):
                act.wait_ge(a_done, n + 1)
                if n >= 2:
                    act.wait_ge(hid_ready, n - 1)
                act.activation(gate[:, n % 2, :], ab[n % 2][0][:, :], ACT.Silu).then_inc(gate_ready, 1)
            act.wait_ge(square_ready, 1)
            act.activation(root[:, :], square[:, :], ACT.Sqrt).then_inc(root_ready, 1)

        @block.vector
        def _(dve):
            step = Steps(dve, step_sem)
            for c in range(C):
                norm_chunk(dve, step, m.x, xn, stat, c, std_wanted, std_ready)
                step.sync()
                dve.sem_inc(xn_ready, 1)
            dve.wait_ge(l_done, T)
            step.then(dve.tensor_reduce(peak[:, :], ps_l[:, :, :], AX_X, ALU.max))
            dve.tensor_tensor(scores[:, :, :], ps_l[:, :, :], peak[:, :].unsqueeze(2).to_broadcast([P, T, E]),
                              ALU.subtract).then_inc(logit_ready, 1)
            dve.wait_ge(exp_ready, 1)
            step.then(dve.tensor_reduce(peak[:, :], scores[:, :, :], AX_X, ALU.add))
            step.then(dve.reciprocal(peak[:, :], peak[:, :]))
            step.then(dve.tensor_tensor(scores[:, :, :], scores[:, :, :],
                                        peak[:, :].unsqueeze(2).to_broadcast([P, T, E]), ALU.mult))
            routing = route(dve, step, r, scores, TOP1, NT1, 0.0, TOP1 / (TOP1 + 1), masks_ready, ranks_ready, slots_ready)
            while next(routing) != "masks":
                pass

            def gated(n):
                c, s = units[n]
                dve.wait_ge(gate_ready, n + 1)
                dve.wait_ge(b_done, n + 1)
                dve.tensor_tensor(hid[:, s, c * CH:(c + 1) * CH], ab[n % 2][1][:, :], gate[:, n % 2, :],
                                  ALU.mult).then_inc(hid_ready, 1)

            for _ in range(ROUTE_FIRST):
                next(routing)
            gated(0)
            for _ in routing:
                pass
            for n in range(1, len(units)):
                gated(n)
            dve.wait_ge(gram_copied, KH)
            for k in range(KH):
                dve.tensor_copy(sums[:, k, :], gram[:, k, D:DP].to_broadcast([P, P])).then_inc(gram_copied, 1)
            dve.wait_ge(b_in, 16)
            for k in range(KH):
                dve.wait_ge(gw_done, k + 1)
                step(dve.tensor_tensor(prod[:, k, 0:2 * D], ps_t[k][:, :], w[:, k, 0:2 * D], ALU.mult))
                step(dve.tensor_tensor(prod[:, k, 2 * D:3 * D], ps_t[k][:, D:2 * D], w[:, k, 2 * D:3 * D], ALU.mult))
            step.sync()
            dve.sem_inc(prod_ready, 1)
            bqk, bk, bv = bias[:, 0:2 * D], bias[:, D:2 * D], bias[:, 2 * D:3 * D]
            dve.wait_ge(norms_done, 1)
            step.then(dve.tensor_scalar(t1[:, :], bqk, float(S), None, ALU.mult))
            step.then(dve.scalar_tensor_tensor(t1[:, :], ps_ab[1][:, :], 2.0, t1[:, :], ALU.mult, ALU.add))
            step.then(dve.tensor_tensor(t1[:, :], t1[:, :], bqk, ALU.mult))
            dve.tensor_tensor(square[:, :], ps_ab[0][:, :], t1[:, :], ALU.add).then_inc(square_ready, 1)
            step.then(dve.scalar_tensor_tensor(kv[:, :], bv, float(S), ps_o[:, 1, :], ALU.mult, ALU.add))
            step.then(dve.tensor_tensor(kv[:, :], kv[:, :], bk, ALU.mult))
            step.then(dve.tensor_tensor(t2[:, :], ps_ab[1][:, D:2 * D], bv, ALU.mult))
            step.then(dve.tensor_tensor(kv[:, :], kv[:, :], t2[:, :], ALU.add))
            step.then(dve.tensor_tensor(kv[:, :], ps_o[:, 0, :], kv[:, :], ALU.add))
            dve.wait_ge(square_ready, 1)
            dve.wait_ge(root_ready, 1)
            step.then(dve.tensor_tensor(t2[:, :], root[:, 0:D], root[:, D:2 * D], ALU.mult))
            step.then(dve.reciprocal(t2[:, :], t2[:, :]))
            step.then(dve.tensor_tensor(t1[:, 0:D], square[:, 0:D], t2[:, :], ALU.mult))
            step.then(dve.tensor_tensor(t1[:, D:2 * D], square[:, D:2 * D], t2[:, :], ALU.mult))
            step.then(dve.tensor_tensor(t1[:, 0:D], t1[:, 0:D], t1[:, D:2 * D], ALU.mult))
            step.then(dve.tensor_scalar(t1[:, 0:D], t1[:, 0:D], -0.5, 1.5, ALU.mult, ALU.add))
            step.then(dve.tensor_tensor(t2[:, :], t2[:, :], t1[:, 0:D], ALU.mult))
            step.then(dve.tensor_tensor(kv[:, :], kv[:, :], t2[:, :], ALU.mult))
            step(dve.tensor_tensor(bq[:, :], bias[:, 0:D], kv[:, :], ALU.mult))
            step.then(dve.tensor_scalar(t2[:, :], kv[:, :], float(TOP1 + 1), None, ALU.mult))
            step(dve.tensor_tensor(wq[:, :, :], w[:, :, 0:D], t2[:, :].unsqueeze(1).to_broadcast([P, KH, D]), ALU.mult))
            step.sync()
            step(dve.tensor_tensor(m.x[:, :, :], m.x[:, :, :], bq[:, :].unsqueeze(1).to_broadcast([P, T, D]), ALU.add))

        @block.tensor
        def _(pe):
            pe.wait_ge(w_in, 32)
            pe.wait_ge(ones_ready, 1)
            for c in range(C):
                pe.wait_ge(xn_ready, c + 1)
                for i in range(c * TC, (c + 1) * TC):
                    if i >= 2:
                        pe.wait_ge(xt_ready, i - 1)
                    for k in range(KH):
                        mm = pe.transpose(ps_t[i % 2][:, k * P:(k + 1) * P], xn[:, i, k * P:(k + 1) * P], m.ident[:, :])
                    mm.then_inc(t_done, 1)
                for i in range(c * TC, (c + 1) * TC):
                    pe.wait_ge(xt_ready, i + 1)
                    for k in range(KH):
                        mm = pe.matmul(ps_l[:, i, :], xt[:, k, i * P:(i + 1) * P], wr[:, k, :],
                                       start=(k == 0), stop=(k == KH - 1))
                    mm.then_inc(l_done, 1)
            for i in range(T):
                for k in range(KH):
                    mm = pe.matmul(ps_g[k][:, :], xn[:, i, k * P:(k + 1) * P], xn[:, i, :],
                                   start=(i == 0), stop=(i == T - 1))
                if i == GRAM_FIRST:
                    route_ranks(pe, r, masks_ready, ranks_ready)
            mm.then_inc(gram_done, 1)
            pe.wait_ge(s_in, 32)
            for n, (c, s) in enumerate(units):
                if n >= 2:
                    pe.wait_ge(gate_ready, n - 1)
                for k in range(KH):
                    mm = pe.matmul(ab[n % 2][0][:, :], ws1[:, k, s * P:(s + 1) * P], xt[:, k, c * CH:(c + 1) * CH],
                                   start=(k == 0), stop=(k == KH - 1))
                mm.then_inc(a_done, 1)
                if n >= 2:
                    pe.wait_ge(hid_ready, n - 1)
                for k in range(KH):
                    mm = pe.matmul(ab[n % 2][1][:, :], ws3[:, k, s * P:(s + 1) * P], xt[:, k, c * CH:(c + 1) * CH],
                                   start=(k == 0), stop=(k == KH - 1))
                mm.then_inc(b_done, 1)
            pe.wait_ge(hid_ready, len(units))
            pe.wait_ge(gram_copied, 2 * KH)
            for k in range(KH):
                for j in range(KH):
                    mm = pe.matmul(ps_t[k][:, :], gram[:, j, k * P:(k + 1) * P], w[:, j, 0:2 * D],
                                   start=(j == 0), stop=(j == KH - 1))
                mm.then_inc(gw_done, 1)
            for k in range(KH):
                pe.matmul(ps_ab[1][:, :], sums[:, k, :], w[:, k, 0:2 * D], start=(k == 0), stop=(k == KH - 1))
            pe.wait_ge(slots_ready, 1)
            for k in range(KH):
                pe.matmul(ps_o[:, 1, :], sums[:, k, :], w[:, k, 2 * D:3 * D], start=(k == 0), stop=(k == KH - 1))
            pe.wait_ge(prod_ready, 1)
            for k in range(KH):
                pe.matmul(ps_ab[0][:, :], m.ones_f[:, :], prod[:, k, 0:2 * D], start=(k == 0), stop=(k == KH - 1))
            for k in range(KH):
                mm = pe.matmul(ps_o[:, 0, :], m.ones_f[:, :], prod[:, k, 2 * D:3 * D],
                               start=(k == 0), stop=(k == KH - 1))
            mm.then_inc(norms_done, 1)


def two_layers(nc, a, out):
    with ExitStack() as ctx:
        m = Memory(nc, ctx)
        common(nc, m)
        m.cleared = [m.sem(f"cleared{layer}") for layer in range(2)]
        with ExitStack() as attention:
            l = Memory(nc, attention)
            m.o_t = l.sb("o_t", [P, NG, S])
            m.xn = m.o_t[:, NG // 2:NG, :].rearrange("p g (i d) -> p (g i) d", d=D)
            m.v_all = l.sb("v_all", [P, T, NH, HD + 1])
            m.qs = [l.sb(f"qs{c}", [MROWS, HG, CH], BF16) for c in range(C)]
            m.ks = [l.sb(f"ks{b}", [MROWS, HG, S], BF16) for b in range(2)]
            m.w1 = l.sb("moe0_w1", [P, KH, E, HID])
            m.w2 = l.sb("moe0_w2", [P, E, D])
            m.zeros = l.sb("zeros", [P, D])
            m.zero16 = l.sb("zero16", [P, P], BF16)
            m.parts_out = [l.sem(f"parts_out{n}") for n in range(4 * C)]
            m.first_in = [l.sem(f"first_in{c}") for c in range(C)]
            m.moe0_w_in = l.sem("moe0_w_in")
            stage_project(nc, m, a)
            stage_attention(nc, m)
            stage_output(nc, m, a)
        m.xt2 = m.sb("xt2", [P, KH, S])
        m.hid_s = m.sb("hid_s", [P, HS // P, S])
        m.w13 = m.sb("w13", [P, KH, E, 2 * HID])
        m.we2 = m.sb("we2", [P, E, D])
        m.ws2 = m.sb("ws2", [P, HS // P, D])
        m.wq = m.sb("wq", [P, KH, D])
        m.tail_in, m.moe1_w_in = m.sem("tail_in"), m.sem("moe1_w_in")
        stage_second(nc, m, a)
        stage_experts(nc, m, out)


def kernel(L0_attn_hidden_states, L0_attn_w_qkv, L0_attn_w_o, L0_ffn_Wg, L0_ffn_balance_bias, L0_ffn_W1, L0_ffn_W2,
           L1_attn_W, L1_attn_b, L1_ffn_w_router, L1_ffn_we1, L1_ffn_we3, L1_ffn_we2, L1_ffn_ws1, L1_ffn_ws3,
           L1_ffn_ws2):
    import numpy as np
    import concourse.bacc as bacc
    from concourse.bass_utils import run_bass_kernel_spmd

    def experts_last(w):
        return w.transpose(1, 0, 2).reshape(w.shape[1], -1)

    arrays = {
        "x": L0_attn_hidden_states, "w_qkv_t": L0_attn_w_qkv.T, "w_o_t": L0_attn_w_o.T, "wg_t": L0_ffn_Wg.T,
        "balance_bias": L0_ffn_balance_bias, "w1": experts_last(np.asarray(L0_ffn_W1)), "w2": L0_ffn_W2,
        "w_attn": L1_attn_W, "b_attn": L1_attn_b, "w_router": L1_ffn_w_router,
        "we13": experts_last(np.concatenate([np.asarray(L1_ffn_we1), np.asarray(L1_ffn_we3)], axis=2)),
        "we2": L1_ffn_we2, "ws1": L1_ffn_ws1, "ws3": L1_ffn_ws3, "ws2": L1_ffn_ws2,
    }
    arrays = {name: np.ascontiguousarray(v) for name, v in arrays.items()}
    nc = bacc.Bacc("TRN2", target_bir_lowering=False, num_devices=1)
    a = {name: nc.dram_tensor(f"in_{name}", v.shape, mybir.dt.from_np(v.dtype), kind="ExternalInput").ap()
         for name, v in arrays.items()}
    out = nc.dram_tensor("out", (1, S, D), F32, kind="ExternalOutput").ap()
    two_layers(nc, a, out)
    result = run_bass_kernel_spmd(nc, [{f"in_{name}": v for name, v in arrays.items()}], core_ids=[0])
    return result.results[0]["out"]
```

```python
from contextlib import ExitStack

import concourse.bass as bass
from concourse import mybir

ALU = mybir.AluOpType
ACT = mybir.ActivationFunctionType
F32 = mybir.dt.float32
BF16 = mybir.dt.bfloat16
I32 = mybir.dt.int32
U32 = mybir.dt.uint32
AX_X = mybir.AxisListType.X

P = 128
S = 2048
D = 256
T = S // P
KH = D // P
CH = 512
C = S // CH
TC = CH // P
NH = 16
HD = D // NH
HG = 4
NG = NH // HG
E = 16
HID = 128
HS = 512
TOP0, TOP1 = 2, 4
NT0 = S * TOP0 // P + E - 1
NT1 = S * TOP1 // P + E - 1
EPAD = 8
IN_RANGE = "the routing counts from zero and takes the minimum with E - 1"
EPS = 1e-5
NEG = -1e30
PARTS = 3
Q_PART = [0, 0, 0, 1, 1, 2]
K_PART = [0, 1, 2, 0, 1, 0]
TERMS = len(Q_PART)
KROWS = TERMS * HD
MDMA = PARTS
MROWS = KROWS + PARTS


class Steps:

    def __init__(self, eng, sem):
        self.eng, self.sem, self.n = eng, sem, 0

    def __call__(self, instruction):
        instruction.then_inc(self.sem, 1)
        self.n += 1

    def sync(self):
        self.eng.wait_ge(self.sem, self.n)

    def then(self, instruction):
        self(instruction)
        self.sync()


class Memory:

    def __init__(self, nc, ctx):
        self.nc, self.ctx = nc, ctx

    def sb(self, name, shape, dt=F32):
        return self.ctx.enter_context(self.nc.sbuf_tensor(name, shape, dt))

    def ps(self, name, shape, dt=F32):
        return self.ctx.enter_context(self.nc.psum_tensor(name, shape, dt))

    def sem(self, name):
        return self.ctx.enter_context(self.nc.semaphore(name))

    def scratch(self, name, shape, dt=F32):
        return self.nc.dram_tensor(name, shape, dt, kind="Internal").ap()


def inverse_deviation(dve, step, stat, c, std_wanted, std_ready):
    var, std, tmp = stat["var"], stat["std"], stat["tmp"]
    cs = slice(c * TC, (c + 1) * TC)
    dve.wait_ge(std_wanted, c + 1)
    dve.wait_ge(std_ready, c + 1)
    step.then(dve.reciprocal(std[:, cs], std[:, cs]))
    step.then(dve.tensor_tensor(tmp[:, cs], std[:, cs], std[:, cs], ALU.mult))
    step.then(dve.tensor_tensor(tmp[:, cs], tmp[:, cs], var[:, cs], ALU.mult))
    step.then(dve.tensor_scalar(tmp[:, cs], tmp[:, cs], -0.5, 1.5, ALU.mult, ALU.add))
    step.then(dve.tensor_tensor(std[:, cs], std[:, cs], tmp[:, cs], ALU.mult))


def normalized(dve, step, x, xn, stat, i):
    step(dve.tensor_scalar(xn[:, i, 0:D], x[:, i, :], stat["mv"][:, i, 0:1], stat["std"][:, i:i + 1],
                           ALU.subtract, ALU.mult))


def norm_chunk(dve, step, x, xn, stat, c, std_wanted, std_ready):
    tiles = range(c * TC, (c + 1) * TC)
    for i in tiles:
        step(dve.bn_stats(stat["bn"][:, i, :], x[:, i, :]))
    step.sync()
    for i in tiles:
        step(dve.bn_aggr(stat["mv"][:, i, :], stat["bn"][:, i, :]))
    step.sync()
    dve.tensor_scalar(stat["var"][:, c * TC:(c + 1) * TC], stat["mv"][:, c * TC:(c + 1) * TC, 1], EPS, None,
                      ALU.add).then_inc(std_wanted, 1)
    inverse_deviation(dve, step, stat, c, std_wanted, std_ready)
    for i in tiles:
        normalized(dve, step, x, xn, stat, i)


def route(dve, step, r, scores, top, tiles, eps, factor, masks_ready, ranks_ready, slots_ready):
    best, arg, argf = r["best"], r["arg"], r["argf"]
    for i in range(T):
        step(dve.max(best[:, i, :], scores[:, i, :]))
    step.sync()
    yield
    for i in range(T):
        step(dve.max_index(arg[:, i, :], best[:, i, :], scores[:, i, :]))
    step.sync()
    yield
    step.then(dve.tensor_copy(argf[:, :, :], arg[:, :, :]))
    yield
    for k in range(top):
        step(dve.tensor_tensor(r["hot"][:, k, :, :], argf[:, :, k:k + 1].to_broadcast([P, T, E]),
                               r["iota_e"][:, 0:1, :].to_broadcast([P, T, E]), ALU.is_equal))
    step.sync()
    yield
    step.then(dve.tensor_tensor(r["any"][:, :, :], r["hot"][:, 0, :, :], r["hot"][:, 1, :, :], ALU.add))
    yield
    for k in range(2, top):
        step.then(dve.tensor_tensor(r["any"][:, :, :], r["any"][:, :, :], r["hot"][:, k, :, :], ALU.add))
        yield
    dve.tensor_copy(r["any16"][:, :, :], r["any"][:, :, :]).then_inc(masks_ready, 1)
    yield "masks"
    step.then(dve.tensor_reduce(r["sum"][:, :], best[:, :, 0:top], AX_X, ALU.add))
    yield
    if eps:
        step.then(dve.tensor_scalar(r["sum"][:, :], r["sum"][:, :], eps, None, ALU.add))
        yield
    step.then(dve.reciprocal(r["sum"][:, :], r["sum"][:, :]))
    yield
    step(dve.scalar_tensor_tensor(r["weight"][:, :, 0:top], best[:, :, 0:top], factor,
                                  r["sum"][:, :].unsqueeze(2).to_broadcast([P, T, top]), ALU.mult, ALU.mult))
    dve.wait_ge(ranks_ready, 1)
    count, before, total = r["count"], r["before"], r["total"]
    step.then(dve.tensor_copy(count[:, :, :], r["ps_count"].rearrange("p (i e) -> p e i", e=E)))
    yield
    step.then(dve.tensor_tensor_scan(before[:, :, :].rearrange("p e i -> p (e i)"),
                                     r["within"][:, :], count[:, :, :].rearrange("p e i -> p (e i)"),
                                     0.0, ALU.mult, ALU.add))
    yield
    step.then(dve.tensor_scalar(total[:, :], before[:, :, T - 1], float(P - 1), None, ALU.add))
    yield
    step.then(dve.tensor_copy(r["total_i"][:, :], total[:, :]))
    yield
    step.then(dve.tensor_scalar(r["total_i"][:, :], r["total_i"][:, :], 7, None, ALU.arith_shift_right))
    yield
    step.then(dve.tensor_copy(total[:, :], r["total_i"][:, :]))
    yield
    step.then(dve.tensor_tensor_scan(r["end"][:, :], r["ones_e"][:, :], total[:, :], 0.0, ALU.mult, ALU.add))
    yield
    step.then(dve.tensor_tensor(total[:, :], r["end"][:, :], total[:, :], ALU.subtract))
    yield
    step.then(dve.tensor_scalar(total[:, :], total[:, :], float(P), None, ALU.mult))
    yield
    step.then(dve.tensor_tensor(before[:, :, :], before[:, :, :], count[:, :, :], ALU.subtract))
    yield
    step.then(dve.tensor_tensor(before[:, :, :], before[:, :, :],
                                total[:, :].unsqueeze(2).to_broadcast([P, E, T]), ALU.add))
    yield
    step.then(dve.tensor_tensor(count[:, :, :], r["ps_rank"].rearrange("p (i e) -> p e i", e=E),
                                before[:, :, :], ALU.add))
    yield
    for k in range(top):
        step.then(dve.tensor_tensor(r["any"][:, :, :], r["hot"][:, k, :, :],
                                    count[:, :, :].rearrange("p e i -> p i e"), ALU.mult))
        yield
        step.then(dve.tensor_reduce(r["slotf"][:, k, :], r["any"][:, :, :], AX_X, ALU.add))
        dve.tensor_copy(r["slot"][:, k, :], r["slotf"][:, k, :]).then_inc(slots_ready, 1)
        yield
    step.then(dve.tensor_tensor(r["ended"][:, 0:tiles, :], r["end"][0:1, :].unsqueeze(1).to_broadcast([1, tiles, E]),
                                r["iota_t"][0:1, 0:tiles].unsqueeze(2).to_broadcast([1, tiles, E]), ALU.is_le))
    yield
    step.then(dve.tensor_reduce(r["tilef"][:, 0:tiles], r["ended"][:, 0:tiles, :], AX_X, ALU.add))
    yield
    step.then(dve.tensor_scalar(r["tilef"][:, 0:tiles], r["tilef"][:, 0:tiles], float(E - 1), None, ALU.min))
    yield
    dve.tensor_copy(r["tile_e"][:, EPAD:EPAD + tiles], r["tilef"][:, 0:tiles]).then_inc(slots_ready, 1)


def route_ranks(pe, r, masks_ready, ranks_ready):
    pe.wait_ge(masks_ready, 1)
    flat = r["any16"][:, :, :].rearrange("p i e -> p (i e)")
    pe.matmul(r["ps_rank"], r["before16"][:, :], flat, start=True, stop=True)
    pe.matmul(r["ps_count"], r["ones16"][:, :], flat, start=True, stop=True).then_inc(ranks_ready, 1)


PB = 4
RANKS_AFTER = 4


def load_keys(eng, m, g, tokens, done):
    for t in range(TERMS):
        src = m.qk_parts[K_PART[t], D + g * HG * HD:D + (g + 1) * HG * HD, tokens]
        eng.dma_start(m.ks[g % 2][t * HD:(t + 1) * HD, :, tokens], src.rearrange("(h d) t -> d h t", d=HD)).then_inc(done, 16)


def load_queries(eng, m, g, c, done):
    for t in range(TERMS):
        src = m.qk_parts[Q_PART[t], g * HG * HD:(g + 1) * HG * HD, c * CH:(c + 1) * CH]
        eng.dma_start(m.qs[c][t * HD:(t + 1) * HD, :, :], src.rearrange("(h d) t -> d h t", d=HD)).then_inc(done, 16)


def load_first_group(eng, m, c):
    for n in range(4 * c, 4 * c + 4):
        eng.wait_ge(m.parts_out[n], 16)
    load_keys(eng, m, 0, slice(c * CH, (c + 1) * CH), m.first_in[c])
    load_queries(eng, m, 0, c, m.first_in[c])


CLEAR = 16


def clear(eng, m, buf, first, last, done):
    for at in range(first, last, CLEAR):
        n = min(CLEAR, last - at)
        eng.dma_start(buf.rearrange("(j p) d -> p j d", p=P)[:, at:at + n, :],
                      m.zeros[:, :].unsqueeze(1).to_broadcast([P, n, D])).then_inc(done, 16)


def stage_project(nc, m, a):
    with ExitStack() as ctx:
        l = Memory(nc, ctx)
        wqk = l.sb("wqk", [P, KH, 2 * D])
        wvg = l.sb("wvg", [P, KH, D + E])
        xt = l.sb("xt", [P, KH, S])
        xn = m.xn
        parts = m.o_t[:, 0:2, :].rearrange("p g s -> p (g s)").bitcast(BF16)[:, 0:PB * PARTS * CH].rearrange(
            "p (b r t) -> p b r t", b=PB, r=PARTS)
        rest = l.sb("rest", [P, 2, CH])
        bias = l.sb("bias", [P, E])
        scores = l.sb("scores", [P, T, E])
        ps_t = [l.ps(f"ps_t{b}", [P, KH, P]) for b in range(2)]
        ps_qk = [l.ps(f"ps_qk{b}", [P, CH]) for b in range(2)]
        ps_v = [l.ps(f"ps_v{b}", [P, D + E]) for b in range(2)]
        ps_r = l.ps("ps_r0", [P, 2, D])
        stat, r = m.stat, dict(m.r)
        r["ps_rank"], r["ps_count"] = ps_r[:, 0, :], ps_r[:, 1, :]

        x_in = [l.sem(f"a_x_in{c}") for c in range(C)]
        w_in = l.sem("a_w_in")
        vg_in = l.sem("a_vg_in")
        b_in = l.sem("a_b_in")
        std_wanted, std_ready = l.sem("a_std_wanted"), l.sem("a_std_ready")
        step_sem = l.sem("a_dve")
        xn_ready, t_done, xt_ready = l.sem("a_xn_ready"), l.sem("a_t_done"), l.sem("a_xt_ready")
        qk_done, high_ready, rest_ready = l.sem("a_qk_done"), l.sem("a_high_ready"), l.sem("a_rest_ready")
        mid_ready, low_ready = l.sem("a_mid_ready"), l.sem("a_low_ready")
        v_done, v_copied = l.sem("a_v_done"), l.sem("a_v_copied")
        logit_ready, exp_ready = l.sem("a_logit_ready"), l.sem("a_exp_ready")
        masks_ready, ranks_ready = l.sem("a_masks_ready"), l.sem("a_ranks_ready")
        slots_ready = l.sem("a_slots_ready")
        pool_step, consts = l.sem("a_pool"), l.sem("a_consts")
        zero_ready = l.sem("a_zero_ready")

        block = ctx.enter_context(nc.Block())

        @block.sync
        def _(sp):
            for c in range(C):
                sp.dma_start(m.x[:, c * TC:(c + 1) * TC, :],
                             a["x"][0, c * CH:(c + 1) * CH, :].rearrange("(i p) d -> p i d", p=P)).then_inc(x_in[c], 16)
            sp.wait_ge(zero_ready, 1)

            clear(sp, m, m.xd0, 0, NT0, m.cleared[0])
            for n in range(4 * C):
                c, o = n // 4, n % 4
                sp.wait_ge(low_ready, n + 1)
                sp.dma_start(m.qk_parts[:, o * P:(o + 1) * P, c * CH:(c + 1) * CH].rearrange("r p t -> p r t"),
                             parts[:, n % PB, :, :]).then_inc(m.parts_out[n], 16)
                if 0 < c <= 2 and o == 1:
                    load_first_group(sp, m, c - 1)

        @block.gpsimd
        def _(pool):
            step = Steps(pool, pool_step)
            step(pool.memset(m.zeros[:, :], 0.0))
            step(pool.memset(m.zero16[:, :], 0.0))
            pool.memset(m.ident[:, :], 0.0).then_inc(pool_step, 1)
            step.n += 1
            step.sync()
            pool.memset(m.ones_f[:, :], 1.0).then_inc(zero_ready, 1)
            step(pool.affine_select(out=m.ident[:, :], in_=m.ident[:, :], compare_op=ALU.not_equal, fill=1.0,
                                    base=0, pattern=[[-1, P]], channel_multiplier=1))
            step(pool.iota(m.iota_i[:, 0:P], [[1, P]], base=0, channel_multiplier=0))
            pool.wait_ge(zero_ready, 1)
            step(pool.affine_select(out=m.before_f[:, :], in_=m.ones_f[:, :], compare_op=ALU.is_gt, fill=0.0,
                                    base=0, pattern=[[1, P]], channel_multiplier=-1))
            step(pool.affine_select(out=m.within[:, :].rearrange("p (e i) -> p e i", i=T),
                                    in_=m.ones_f[:, 0:1].unsqueeze(2).to_broadcast([P, E, T]),
                                    compare_op=ALU.is_gt, fill=0.0, base=0, pattern=[[0, E], [1, T]],
                                    channel_multiplier=0))
            step(pool.memset(m.r["tile_e"][:, :], 0))
            step.sync()
            step(pool.tensor_scalar(m.mask_f[:, :], m.before_f[:, :], NEG, None, ALU.mult))
            step(pool.memset(m.v_all[:, :, :, HD:HD + 1], 1.0))
            step.sync()
            pool.tensor_copy(m.iota_f[:, :], m.iota_i[:, :]).then_inc(consts, 1)
            pool.wait_ge(consts, 1)
            for b in range(2):
                step.then(pool.memset(m.ks[b][KROWS:MROWS, :, :], 1.0))
            for n in range(4 * C):
                pool.wait_ge(mid_ready, n + 1)
                pool.tensor_tensor(parts[:, n % PB, 2, :], rest[:, n % 2, :], parts[:, n % PB, 1, :],
                                   ALU.subtract).then_inc(low_ready, 1)

        @block.scalar
        def _(act):
            w_qkv = a["w_qkv_t"].rearrange("(k p) o -> p k o", p=P)
            act.dma_start(wvg[:, :, 0:D], w_qkv[:, :, 2 * D:3 * D]).then_inc(vg_in, 16)
            act.dma_start(wvg[:, :, D:D + E], a["wg_t"].rearrange("(k p) e -> p k e", p=P)).then_inc(vg_in, 16)
            act.dma_start(wqk[:, :, :], w_qkv[:, :, 0:2 * D]).then_inc(w_in, 16)
            act.dma_start(bias[:, :], a["balance_bias"].unsqueeze(0).to_broadcast([P, E])).then_inc(b_in, 16)
            act.dma_start(m.w1[:, :, :, :], a["w1"].rearrange("(k p) (e h) -> p k e h", p=P, e=E)).then_inc(m.moe0_w_in, 16)
            act.dma_start(m.w2[:, :, :], a["w2"].rearrange("e p d -> p e d")).then_inc(m.moe0_w_in, 16)
            def root(c):
                act.wait_ge(std_wanted, c + 1)
                act.activation(stat["std"][:, c * TC:(c + 1) * TC], stat["var"][:, c * TC:(c + 1) * TC],
                               ACT.Sqrt).then_inc(std_ready, 1)

            root(0)
            for i in range(T + 2):
                if i < T:
                    if i % TC == 0 and i // TC + 1 < C:
                        root(i // TC + 1)
                    act.wait_ge(t_done, i + 1)
                    act.copy(xt[:, :, i * P:(i + 1) * P], ps_t[i % 2][:, :, :]).then_inc(xt_ready, 1)
                if i >= 2:
                    act.wait_ge(v_done, i - 1)
                    act.copy(m.v_all[:, i - 2, :, 0:HD], ps_v[i % 2][:, 0:D].rearrange("p (h d) -> p h d", d=HD))
                    act.copy(scores[:, i - 2, :], ps_v[i % 2][:, D:D + E]).then_inc(v_copied, 1)
            act.wait_ge(logit_ready, 1)
            act.activation(scores[:, :, :], scores[:, :, :], ACT.Exp, scale=-1.0).then_inc(exp_ready, 1)
            for n in range(4 * C):
                act.wait_ge(qk_done, n + 1)
                if n >= PB:
                    act.wait_ge(m.parts_out[n - PB], 16)
                act.copy(parts[:, n % PB, 0, :], ps_qk[n % 2][:, :]).then_inc(high_ready, 1)
                act.wait_ge(rest_ready, n + 1)
                act.copy(parts[:, n % PB, 1, :], rest[:, n % 2, :]).then_inc(mid_ready, 1)

        @block.vector
        def _(dve):
            step = Steps(dve, step_sem)
            for c in range(C):
                dve.wait_ge(x_in[c], 16)
                norm_chunk(dve, step, m.x, xn, stat, c, std_wanted, std_ready)
                step.sync()
                dve.sem_inc(xn_ready, 1)
                if c == 0:
                    dve.wait_ge(consts, 1)
                    step(dve.tensor_copy(m.ident16[:, :], m.ident[:, :]))
                    step(dve.tensor_copy(m.ones16[:, :], m.ones_f[:, :]))
                    step(dve.tensor_copy(m.before16[:, :], m.before_f[:, :]))
                    step(dve.tensor_copy(m.mask16[:, :], m.mask_f[:, :]))
            dve.wait_ge(b_in, 16)
            dve.wait_ge(v_copied, T)
            dve.tensor_tensor(scores[:, :, :], scores[:, :, :], bias[:, :].unsqueeze(1).to_broadcast([P, T, E]),
                              ALU.add).then_inc(logit_ready, 1)
            dve.wait_ge(exp_ready, 1)
            step.then(dve.tensor_scalar(scores[:, :, :], scores[:, :, :], 1.0, None, ALU.add))
            step.then(dve.reciprocal(scores[:, :, :], scores[:, :, :]))
            routing = route(dve, step, r, scores, TOP0, NT0, 1e-6, 0.5, masks_ready, ranks_ready, slots_ready)
            for n in range(4 * C):
                dve.wait_ge(high_ready, n + 1)
                if n >= 2:
                    dve.wait_ge(low_ready, n - 1)
                dve.tensor_tensor(rest[:, n % 2, :], ps_qk[n % 2][:, :], parts[:, n % PB, 0, :],
                                  ALU.subtract).then_inc(rest_ready, 1)
                if n == RANKS_AFTER - 2:
                    while next(routing) != "masks":
                        pass
                    continue
                for _ in range(1 if n < RANKS_AFTER - 2 else 2 if n <= RANKS_AFTER else 5):
                    next(routing, None)
            for _ in routing:
                pass

        @block.tensor
        def _(pe):
            pe.wait_ge(consts, 1)
            for c in range(C):
                pe.wait_ge(xn_ready, c + 1)
                for i in range(c * TC, (c + 1) * TC):
                    if i >= 2:
                        pe.wait_ge(xt_ready, i - 1)
                    for k in range(KH):
                        mm = pe.transpose(ps_t[i % 2][:, k, :], xn[:, i, k * P:(k + 1) * P], m.ident[:, :])
                    mm.then_inc(t_done, 1)
                if c == 0:
                    pe.wait_ge(vg_in, 32)
                for i in range(c * TC, (c + 1) * TC):
                    pe.wait_ge(xt_ready, i + 1)
                    if i >= 2:
                        pe.wait_ge(v_copied, i - 1)
                    for k in range(KH):
                        mm = pe.matmul(ps_v[i % 2][:, :], xt[:, k, i * P:(i + 1) * P], wvg[:, k, :],
                                       start=(k == 0), stop=(k == KH - 1))
                    mm.then_inc(v_done, 1)
            pe.wait_ge(w_in, 16)
            for n in range(4 * C):
                c = n // 4
                if n >= 2:
                    pe.wait_ge(rest_ready, n - 1)
                for k in range(KH):
                    mm = pe.matmul(ps_qk[n % 2][:, :], wqk[:, k, (n % 4) * P:(n % 4 + 1) * P],
                                   xt[:, k, c * CH:(c + 1) * CH], start=(k == 0), stop=(k == KH - 1))
                mm.then_inc(qk_done, 1)
                if n == RANKS_AFTER:
                    route_ranks(pe, r, masks_ready, ranks_ready)


def common(nc, m):
    m.x = m.sb("x_res", [P, T, D])
    m.ident = m.sb("ident", [P, P])
    m.ident16 = m.sb("ident16", [P, P], BF16)
    m.ones_f = m.sb("ones_f", [P, P])
    m.ones16 = m.sb("ones16", [P, P], BF16)
    m.before_f = m.sb("before_f", [P, P])
    m.before16 = m.sb("before16", [P, P], BF16)
    m.mask_f = m.sb("mask_f", [P, P])
    m.mask16 = m.sb("mask16", [P, P], BF16)
    m.iota_i = m.sb("iota_i", [P, P], I32)
    m.iota_f = m.sb("iota_f", [P, P])
    m.within = m.sb("within", [P, E * T])
    m.stat = {"bn": m.sb("bn", [P, T, 6]), "mv": m.sb("mv", [P, T, 2]), "var": m.sb("var", [P, T]),
              "std": m.sb("std", [P, T]), "tmp": m.sb("ln_tmp", [P, T])}
    masks = m.sb("masks", [P, TOP1 + 1, T, E])
    m.r = {
        "best": m.sb("best", [P, T, 8]), "arg": m.sb("arg", [P, T, 8], U32), "argf": m.sb("argf", [P, T, 8]),
        "hot": masks[:, 0:TOP1, :, :], "any": masks[:, TOP1, :, :], "any16": m.sb("any16", [P, T, E], BF16),
        "sum": m.sb("top_sum", [P, T]), "weight": m.sb("weight", [P, T, TOP1]),
        "count": m.sb("count", [P, E, T]), "before": m.sb("before", [P, E, T]), "total": m.sb("total", [P, E]),
        "total_i": m.sb("total_i", [P, E], I32), "end": m.sb("end", [P, E]),
        "slotf": m.sb("slotf", [P, TOP1, T]), "slot": m.sb("slot", [P, TOP1, T], U32),
        "ended": masks[0:1, :, :, :].rearrange("p k i e -> p (k i e)")[:, 0:NT1 * E].rearrange("p (t e) -> p t e", e=E),
        "tilef": m.sb("tilef", [1, NT1]), "tile_e": m.sb("tile_e", [1, EPAD + NT1 + 3 * EPAD], I32),
        "iota_e": m.iota_f[:, 0:E].unsqueeze(1), "iota_t": m.iota_f, "ones_e": m.ones_f[:, 0:E],
        "within": m.within, "before16": m.before16, "ones16": m.ones16,
    }
    m.xd0 = m.scratch("xd0", [NT0 * P, D])
    m.xd1 = m.scratch("xd1", [NT1 * P, D])
    m.yd0 = m.scratch("yd0", [NT0 * P, D])
    m.yd1 = m.scratch("yd1", [NT1 * P, D])
    m.qk_parts = m.scratch("qk_parts", [PARTS, 2 * D, S], BF16)


TURN_AHEAD = 5
FIRST_ROWS = 10
LOAD_AHEAD = 4
ROW_COST, TURN_COST, EXP_COST = 0.1, 1.0, 0.2


def attention_plan():
    def exps(g, c):
        return [("exp", g, c, k, pair) for k in range(TC * (c + 1)) for pair in range(HG // 2)]

    def maxes(g, c):
        out = []
        for i in range(TC):
            for j in range(c):
                out += [("max", g, c, [(h, i, j, CH)]) for h in range(HG)]
            w = (i + 1) * P
            per = CH // w
            per = 4 if per >= 4 else 2 if per >= 2 else 1
            out += [("max", g, c, [(h, i, c, w) for h in range(h0, h0 + per)]) for h0 in range(0, HG, per)]
        return out

    pairs = [(g, c) for g in range(NG) for c in range(C)]
    exp_units = [u for p in pairs for u in exps(*p)]
    rows = []
    for n, pair in enumerate(pairs):
        mine = maxes(*pair)
        if n:
            mine.insert(min(4, len(mine)), ("turn", *pairs[n - 1]))
        rows += mine
    rows.append(("turn", *pairs[-1]))

    def row_cost(u):
        return TURN_COST if u[0] == "turn" else ROW_COST + len(u[3]) * u[3][0][3] / CH

    def exp_cost(u):
        return EXP_COST + 2 * (1 - max(0, u[3] - TC * u[2]) * P / CH)

    rows_upto, exps_upto = [0], [0]
    for u in rows:
        rows_upto.append(rows_upto[-1] + row_cost(u))
    for u in exp_units:
        exps_upto.append(exps_upto[-1] + exp_cost(u))
    first = {pair: min(n for n, u in enumerate(exp_units) if u[1:3] == pair) for pair in pairs}
    deadlines = [(rows.index(("turn", *pair)) + 1, max(0, first[pair] - TURN_AHEAD)) for pair in pairs]
    release = {(g, c): first[(g - 1, c)] + 2 * TC * (c + 1) + LOAD_AHEAD for g, c in pairs if g}
    deadlines.append((rows.index(("turn", *pairs[0])) + 1 + FIRST_ROWS, 0))
    plan, done, debt = [], 0, 0.0
    for at, u in enumerate(exp_units):
        for count, by in deadlines:
            if by <= at:
                while done < count:
                    plan.append(rows[done])
                    done += 1
        ahead = [(rows_upto[count] - rows_upto[done]) / (exps_upto[by] - exps_upto[at])
                 for count, by in deadlines if by > at and count > done]
        debt += max(ahead, default=0) * exp_cost(u)
        plan.append(u)
        while done < len(rows) and debt >= row_cost(rows[done]) / 2:
            if rows[done][0] == "max" and at < release.get(rows[done][1:3], 0):
                break
            debt -= row_cost(rows[done])
            plan.append(rows[done])
            done += 1
    return with_experts(plan)


MOE_START = 42
MOE_SPACE = 4.5
SUM_SPACE = 2


def with_experts(plan):
    moe = {}
    for slot in range(NT0 + 3):
        for k, name in enumerate("xhgy"):
            if 0 <= slot - k < NT0:
                moe.setdefault(MOE_START + int(MOE_SPACE * slot) + k, []).append((name, slot - k))
    first_sum = max(moe) + 14
    for i in range(T):
        moe.setdefault(first_sum + SUM_SPACE * i, []).append(("sum", i))
    out, at = [], 0
    for u in plan:
        out.append(u)
        if u[0] == "exp":
            at += 1
            out += moe.pop(at, [])
    for at in sorted(moe):
        out += moe[at]
    return out


def stage_attention(nc, m):
    plan = attention_plan()
    exps = [u for u in plan if u[0] == "exp"]
    rows = [u for u in plan if u[0] not in ("exp", "sum")]
    turns = [u for u in plan if u[0] == "turn"]
    row_of = {u[0:2]: n for n, u in enumerate(rows) if u[0] in "xhgy"}
    with ExitStack() as ctx:
        l = Memory(nc, ctx)
        qs, ks = m.qs, m.ks
        NPB = 6
        probs = l.sb("probs", [P, NPB, 2, CH])
        part_max = [l.sb(f"part_max{b}", [P, HG, TC, C]) for b in range(2)]
        neg_max = l.sb("neg_max", [P, HG * TC])
        max_rest = l.sb("max_rest", [HG * TC, P])
        max_parts = [l.sb(f"max_parts{b}", [HG * TC, PARTS, P], BF16) for b in range(2)]
        XB = 4
        xs = l.sb("moe0_xs", [P, XB, D])
        xs_t = l.sb("moe0_xs_t", [P, 2, KH, P])
        h_tanh = l.sb("moe0_h_tanh", [P, 2, HID])
        h_copy = l.sb("moe0_h_copy", [P, 2, HID])
        hid = l.sb("moe0_hid", [P, 2, HID])
        hid_t = l.sb("moe0_hid_t", [P, 2, P])
        ys = l.sb("moe0_ys", [P, XB, D])
        yg = l.sb("moe0_yg", [P, 2, TOP0, D])
        ps_st = [l.ps(f"ps_st{b}", [P, 2, CH]) for b in range(2)]
        NSM = 3
        ps_row = [l.ps(f"ps_row{b}", [P, CH]) for b in range(NSM)]
        ps_o = l.ps("ps_o", [P, CH])

        k_in = [l.sem(f"b_k_in{b}") for b in range(2)]
        q_in = [l.sem(f"b_q_in{c}") for c in range(C)]
        rows_in = [l.sem(f"b_rows_in{b}") for b in range(2)]
        st_done, exp_done, pv_done = l.sem("b_st_done"), l.sem("b_exp_done"), l.sem("b_pv_done")
        o_copied = l.sem("b_o_copied")
        row_done, row_used = l.sem("b_row_done"), l.sem("b_row_used")
        neg_ready, parts_ready = l.sem("b_neg_ready"), l.sem("b_parts_ready")
        step_sem, pool_sem = l.sem("b_dve"), l.sem("b_pool")
        dispatched = l.sem("b_dispatched")
        x_in = [l.sem(f"moe0_x_in{b}") for b in range(XB)]
        y_out = [l.sem(f"moe0_y_out{b}") for b in range(XB)]
        h_used, hid_ready = l.sem("moe0_h_used"), l.sem("moe0_hid_ready")
        gathered = [l.sem(f"moe0_gathered{b}") for b in range(2)]
        summed = l.sem("moe0_summed")
        block = ctx.enter_context(nc.Block())

        def last_pv(g, c):
            return (max(n for n, u in enumerate(exps) if u[1:3] == (g, c)) + 1) // 2

        def used(n):
            return sum(u[0] != "h" for u in rows[:n + 1])

        @block.sync
        def _(sp):
            for n in range(4 * 2, 4 * C):
                sp.wait_ge(m.parts_out[n], 16)
            load_keys(sp, m, 1, slice(0, S), k_in[1])
            at_tile = 0
            for n, (_, g, c) in enumerate(turns):
                sp.wait_ge(parts_ready, n + 1)
                for r in range(PARTS):
                    sp.dma_start(qs[c][KROWS + r:KROWS + r + 1, :, :].rearrange("r h t -> r (h t)"),
                                 max_parts[n % 2][:, r, :]).then_inc(rows_in[n % 2], 16)
                if c == 0 and g >= 1:
                    sp.wait_ge(pv_done, last_pv(g - 1, 3))
                    load_queries(sp, m, g, 3, q_in[3])
                if c == 2 and g + 1 < NG:
                    sp.wait_ge(pv_done, last_pv(g, 1))
                    load_queries(sp, m, g + 1, 0, q_in[0])
                    load_queries(sp, m, g + 1, 1, q_in[1])
                    if g >= 1:
                        load_keys(sp, m, g + 1, slice(0, S), k_in[(g + 1) % 2])
                if c == 3 and g + 1 < NG:
                    sp.wait_ge(pv_done, last_pv(g, 2))
                    load_queries(sp, m, g + 1, 2, q_in[2])
                if c >= 2 and at_tile < NT1:
                    clear(sp, m, m.xd1, at_tile, min(NT1, at_tile + CLEAR), m.cleared[1])
                    at_tile += CLEAR
            for b in range(2):
                sp.wait_ge(rows_in[b], 16 * MDMA * len(turns) // 2)

        @block.gpsimd
        def _(pool):
            step = Steps(pool, pool_sem)
            pool.wait_ge(m.cleared[0], 16 * -(-NT0 // CLEAR))
            for k in range(TOP0):
                for i in range(T):
                    pool.indirect_dma_start(out=m.xd0, out_offset=bass.IndirectOffsetOnAxis(m.r["slot"][:, k, i:i + 1], 0),
                                            in_=m.xn[:, i, :], in_offset=None).then_inc(dispatched, 16)
            pool.wait_ge(dispatched, 16 * TOP0 * T)

            def load(j):
                if j < NT0:
                    if j >= XB:
                        pool.wait_ge(row_done, row_of["x", j - XB] + 1)
                    pool.dma_start(xs[:, j % XB, :], m.xd0[j * P:(j + 1) * P, :]).then_inc(x_in[j % XB], 16)

            for j in range(3):
                load(j)
            for slot in range(NT0 + 3):
                load(slot + 3)
                j = slot - 1
                if 0 <= j < NT0:
                    pool.wait_ge(h_used, j + 1)
                    step.then(pool.tensor_scalar(h_tanh[:, j % 2, :], h_tanh[:, j % 2, :], 1.0, None, ALU.add))
                    if j >= 2:
                        pool.wait_ge(row_done, row_of["g", j - 2] + 1)
                    pool.tensor_tensor(hid[:, j % 2, :], h_tanh[:, j % 2, :], h_copy[:, j % 2, :],
                                       ALU.mult).then_inc(hid_ready, 1)
                j = slot - 3
                if j >= 0:
                    pool.wait_ge(row_used, used(row_of["y", j]))
                    pool.dma_start(m.yd0[j * P:(j + 1) * P, :], ys[:, j % XB, :]).then_inc(y_out[j % XB], 16)
            for b in range(XB):
                pool.wait_ge(y_out[b], 16 * len(range(b, NT0, XB)))
            for i in range(T):
                if i >= 2:
                    pool.wait_ge(summed, (i - 1) * TOP0)
                for k in range(TOP0):
                    pool.indirect_dma_start(out=yg[:, i % 2, k, :], out_offset=None, in_=m.yd0,
                                            in_offset=bass.IndirectOffsetOnAxis(m.r["slot"][:, k, i:i + 1], 0)
                                            ).then_inc(gathered[i % 2], 16)

        @block.scalar
        def _(act):
            def copy_output(at):
                g, c = exps[at][1:3]
                act.wait_ge(pv_done, (at + 1) // 2)
                act.copy(m.o_t[:, g, c * CH:(c + 1) * CH], ps_o[:, :]).then_inc(o_copied, 1)

            for c in range(2, C):
                load_first_group(act, m, c)
            at = 0
            for u in plan:
                if u[0] == "exp":
                    g, c, k = u[1:4]
                    off = max(0, k - TC * c) * P
                    act.wait_ge(st_done, at + 1)
                    if at >= NPB:
                        act.wait_ge(pv_done, (at - NPB) // 2 + 1)
                    act.activation(probs[:, at % NPB, :, off:CH], ps_st[at % 2][:, :, off:CH], ACT.Exp,
                                   scale=HD ** -0.5).then_inc(exp_done, 1)
                    if at >= 2 and exps[at - 2][1:3] != (g, c) and exps[at - 1][1:3] == (g, c):
                        copy_output(at - 2)
                    at += 1
                elif u[0] == "h":
                    j = u[1]
                    act.wait_ge(row_done, row_of["h", j] + 1)
                    if j >= 2:
                        act.wait_ge(hid_ready, j - 1)
                    bank = ps_row[row_of["h", j] % NSM]
                    act.activation(h_tanh[:, j % 2, :], bank[:, 0:HID], ACT.Tanh, scale=0.5)
                    act.copy(h_copy[:, j % 2, :], bank[:, 0:HID]).then_inc(h_used, 1)
            copy_output(len(exps) - 1)

        @block.vector
        def _(dve):
            step = Steps(dve, step_sem)
            turned, reduced, n = 0, 0, -1
            for u in plan:
                if u[0] == "exp":
                    continue
                if u[0] == "sum":
                    i = u[1]
                    dve.wait_ge(gathered[i % 2], 16 * TOP0 * (i // 2 + 1))
                    for k in range(TOP0):
                        dve.scalar_tensor_tensor(m.x[:, i, :], yg[:, i % 2, k, :], m.r["weight"][:, i, k:k + 1],
                                                 m.x[:, i, :], ALU.mult, ALU.add).then_inc(summed, 1)
                        dve.wait_ge(summed, i * TOP0 + k + 1)
                    continue
                n += 1
                if u[0] == "h":
                    continue
                dve.wait_ge(row_done, n + 1)
                bank = ps_row[n % NSM]
                if u[0] == "x":
                    dve.tensor_copy(xs_t[:, u[1] % 2, :, :],
                                    bank[:, 0:D].rearrange("p (k t) -> p k t", k=KH)).then_inc(row_used, 1)
                elif u[0] == "g":
                    dve.tensor_copy(hid_t[:, u[1] % 2, :], bank[:, 0:P]).then_inc(row_used, 1)
                elif u[0] == "y":
                    j = u[1]
                    if j >= XB:
                        dve.wait_ge(y_out[j % XB], 16 * (j // XB))
                    dve.tensor_copy(ys[:, j % XB, :], bank[:, 0:D]).then_inc(row_used, 1)
                elif u[0] == "max":
                    g, c, pieces = u[1:]
                    h, i, j, w = pieces[0]
                    k = len(pieces)
                    if reduced >= 2:
                        dve.wait_ge(neg_ready, reduced - 1)
                    dve.tensor_reduce(part_max[reduced % 2][:, h:h + k, i, j:j + 1],
                                      bank[:, 0:k * w].rearrange("p (h w) -> p h w", h=k),
                                      AX_X, ALU.max).then_inc(row_used, 1)
                    after = [v for v in rows[n + 1:] if v[0] == "max"][:1]
                    if not after or after[0][1:3] != (g, c):
                        dve.wait_ge(row_used, used(n))
                        dve.tensor_reduce(neg_max[:, :], part_max[reduced % 2][:, :, :, 0:c + 1].rearrange("p h i j -> p (h i) j"),
                                          AX_X, ALU.max, negate=True).then_inc(neg_ready, 1)
                        reduced += 1
                else:
                    parts = max_parts[turned % 2]
                    turned_ps = bank[0:HG * TC, 0:P]
                    if turned >= 2:
                        dve.wait_ge(rows_in[turned % 2], 16 * MDMA * (turned // 2))
                    step.then(dve.tensor_copy(parts[:, 0, :], turned_ps))
                    dve.tensor_tensor(max_rest[:, :], turned_ps, parts[:, 0, :], ALU.subtract).then_inc(row_used, 1)
                    dve.wait_ge(row_used, used(n))
                    step.then(dve.tensor_copy(parts[:, 1, :], max_rest[:, :]))
                    dve.tensor_tensor(parts[:, 2, :], max_rest[:, :], parts[:, 1, :],
                                      ALU.subtract).then_inc(parts_ready, 1)
                    dve.wait_ge(parts_ready, turned + 1)
                    turned += 1

        @block.tensor
        def _(pe):
            state = {"exp": 0, "pv": 0, "row": 0, "turn": 0, "parts": None, "chunk": None, "out": 0}
            turn_of = {u[1:3]: n for n, u in enumerate(turns)}
            experts = {}

            def parts_there(g, c):
                if (g, c) == state["parts"]:
                    return
                state["parts"] = (g, c)
                if g == 0:
                    pe.wait_ge(m.first_in[c], 16 * 2 * TERMS)
                    return
                pe.wait_ge(q_in[c], 16 * TERMS * g)
                if c == 0:
                    pe.wait_ge(k_in[g % 2], 16 * TERMS * ((g + 1) // 2))

            def values(half):
                at = state["pv"]
                _, g, c, k, _ = exps[at]
                off = max(0, k - TC * c) * P
                middle = off + (CH - off + P) // (2 * P) * P
                if half == 0:
                    pe.wait_ge(exp_done, at + 2)
                    if k == 0:
                        if at:
                            state["out"] += 1
                            pe.wait_ge(o_copied, state["out"])
                        pe.matmul(ps_o[:, :].rearrange("p (i t) -> p i t", t=P), m.zero16[:, :],
                                  m.ident16[:, :].unsqueeze(1).to_broadcast([P, TC, P]), start=True, stop=False)
                lo, hi = ((off, middle), (middle, CH))[half]
                for q in range(HG if lo < hi else 0):
                    mm = pe.matmul(ps_o[32 * q:32 * q + HD + 1, lo:hi], m.v_all[:, k, g * HG + q, :],
                                   probs[:, (at + q // 2) % NPB, q % 2, lo:hi], start=False,
                                   stop=(k == TC * (c + 1) - 1), tile_position=(0, 32 * q))
                    if half == 1 or middle == CH:
                        state["last"] = mm
                if half == 1:
                    state["last"].then_inc(pv_done, 1)
                    state["pv"] += 2

            def bank_free(n):
                if n < NSM:
                    return
                before = rows[n - NSM]
                if before[0] == "h":
                    pe.wait_ge(h_used, before[1] + 1)
                else:
                    pe.wait_ge(row_used, used(n - NSM))

            for u in plan:
                if u[0] == "exp":
                    g, c, k, pair = u[1:]
                    n = state["exp"]
                    off = max(0, k - TC * c) * P
                    if (g, c) != state["chunk"]:
                        t = turn_of[(g, c)]
                        pe.wait_ge(rows_in[t % 2], 16 * MDMA * (t // 2 + 1))
                        state["chunk"] = (g, c)
                    if n - state["pv"] > 3:
                        values(n % 2)
                    if n >= 2:
                        pe.wait_ge(exp_done, n - 1)
                    for h in range(2):
                        q = 2 * pair + h
                        diagonal = k >= TC * c
                        mm = pe.matmul(ps_st[n % 2][:, h, off:CH], ks[g % 2][:, q, k * P:(k + 1) * P],
                                       qs[c][:, q, off:CH], start=True, stop=not diagonal)
                        if diagonal:
                            mm = pe.matmul(ps_st[n % 2][:, h, off:off + P], m.mask16[:, :], m.ident16[:, :],
                                           start=False, stop=True)
                    mm.then_inc(st_done, 1)
                    state["exp"] += 1
                    continue
                if u[0] == "sum":
                    continue
                n = state["row"]
                state["row"] += 1
                bank = ps_row[n % NSM]
                if u[0] == "max":
                    g, c, pieces = u[1:]
                    parts_there(g, c)
                    bank_free(n)
                    for at, (h, i, j, w) in enumerate(pieces):
                        cols = bank[:, at * w:(at + 1) * w]
                        mm = pe.matmul(cols, qs[c][0:KROWS, h, i * P:(i + 1) * P],
                                       ks[g % 2][0:KROWS, h, j * CH:j * CH + w], start=True, stop=(j < c))
                        if j == c:
                            mm = pe.matmul(cols[:, w - P:w], m.ident16[:, :], m.mask16[:, :],
                                           start=False, stop=True)
                elif u[0] == "turn":
                    bank_free(n)
                    pe.wait_ge(neg_ready, state["turn"] + 1)
                    state["turn"] += 1
                    mm = pe.transpose(bank[0:HG * TC, 0:P], neg_max[:, :], m.ident[:, :])
                elif u[0] == "x":
                    j = u[1]
                    if j == 0:
                        pe.wait_ge(m.moe0_w_in, 32)
                    if j % 8 == 0:
                        loaded = nc.values_load_multi_w_load_instructions(
                            m.r["tile_e"][0:1, EPAD + j:EPAD + j + 8], engines=[mybir.EngineType.PE], min_val=0,
                            max_val=E - 1, skip_runtime_bounds_check_because=IN_RANGE)[1]
                        experts.update({j + n: e for n, e in enumerate(loaded)})
                    bank_free(n)
                    pe.wait_ge(x_in[j % XB], 16 * (j // XB + 1))
                    for k in range(KH):
                        mm = pe.transpose(bank[:, k * P:(k + 1) * P], xs[:, j % XB, k * P:(k + 1) * P], m.ident[:, :])
                elif u[0] == "h":
                    j = u[1]
                    bank_free(n)
                    pe.wait_ge(row_used, used(row_of["x", j]))
                    for k in range(KH):
                        mm = pe.matmul(bank[:, 0:HID], xs_t[:, j % 2, k, :], m.w1[:, k, bass.ds(experts[j], 1), :],
                                       start=(k == 0), stop=(k == KH - 1))
                elif u[0] == "g":
                    j = u[1]
                    bank_free(n)
                    pe.wait_ge(hid_ready, j + 1)
                    mm = pe.transpose(bank[:, 0:P], hid[:, j % 2, :], m.ident[:, :])
                else:
                    j = u[1]
                    bank_free(n)
                    pe.wait_ge(row_used, used(row_of["g", j]))
                    mm = pe.matmul(bank[:, 0:D], hid_t[:, j % 2, :], m.w2[:, bass.ds(experts.pop(j), 1), :],
                                   start=True, stop=True)
                mm.then_inc(row_done, 1)
            while state["pv"] < len(exps):
                values(0)
                values(1)


def rolled(eng, lag, tiles, unroll, tick, ahead=lambda j: None):
    start = -(-(lag + 2) // unroll) * unroll
    stop = start + (tiles - start) // unroll * unroll
    for j in range(start):
        if j % unroll == 0:
            ahead(j)
        tick(j, j % unroll)
    with eng.Fori(start, stop, unroll) as j:
        ahead(j)
        for u in range(unroll):
            tick(j + u, u)
    for j in range(stop, tiles + lag):
        if j % unroll == 0:
            ahead(j)
        tick(j, j % unroll)


def stage_experts(nc, m, out):
    tiles, top, xd, yd = NT1, TOP1, m.xd1, m.yd1
    W1 = 2 * HID
    YG = 4
    OUT = 2
    U = 4
    BODY = 16
    with ExitStack() as ctx:
        l = Memory(nc, ctx)
        w1, w2 = m.w13, m.we2
        xs = l.sb("moe1_xs", [P, U, D])
        xs_t = l.sb("moe1_xs_t", [P, 2, KH, P])
        act_out = l.sb("moe1_act", [P, 2, HID])
        hid = l.sb("moe1_hid", [P, 2, HID])
        hid_t = l.sb("moe1_hid_t", [P, 2, P])
        ys = l.sb("moe1_ys", [P, U, D])
        yg = l.sb("moe1_yg", [P, YG, top, D])
        ps_x = [l.ps(f"moe1_ps_x{b}", [P, KH, P]) for b in range(2)]
        ps_h = [l.ps(f"moe1_ps_h{b}", [P, W1]) for b in range(2)]
        ps_g = [l.ps(f"moe1_ps_g{b}", [P, P]) for b in range(2)]
        ps_y = [l.ps(f"moe1_ps_y{b}", [P, D]) for b in range(2)]
        x_in = [l.sem(f"moe1_x_in{b}") for b in range(U)]
        y_out = [l.sem(f"moe1_y_out{b}") for b in range(U)]
        gathered = [l.sem(f"moe1_gathered{b}") for b in range(YG)]
        x_turned, x_copied = l.sem("moe1_x_turned"), l.sem("moe1_x_copied")
        h_done, act_done, hid_ready = l.sem("moe1_h_done"), l.sem("moe1_act_done"), l.sem("moe1_hid_ready")
        g_turned, g_copied = l.sem("moe1_g_turned"), l.sem("moe1_g_copied")
        y_done, y_copied = l.sem("moe1_y_done"), l.sem("moe1_y_copied")
        summed = l.sem("moe1_summed")
        tail_done, tail_added, bias_added = l.sem("tail_done"), l.sem("tail_added"), l.sem("bias_added")
        stored = l.sem("stored")
        block = ctx.enter_context(nc.Block())

        def there(j):
            return not isinstance(j, int) or 0 <= j < tiles

        def since(j, n):
            return not isinstance(j, int) or j >= n

        @block.sync
        def _(sp):
            def tick(j, u):
                if there(j):
                    if since(j, U):
                        sp.wait_ge(x_turned, j - (U - 1))
                    sp.dma_start(xs[:, u % U, :], xd[bass.ds(j * P, P), :]).then_inc(x_in[u % U], 16)
                k = j - 2 * U
                if there(k):
                    sp.wait_ge(y_copied, k + 1)
                    sp.dma_start(yd[bass.ds(k * P, P), :], ys[:, u % U, :]).then_inc(y_out[u % U], 16)

            rolled(sp, 2 * U, tiles, BODY, tick)
            for i in range(0, T, OUT):
                sp.wait_ge(summed, (i + OUT) * top)
                sp.dma_start(out[0, i * P:(i + OUT) * P, :].rearrange("(i p) d -> p i d", p=P),
                             m.x[:, i:i + OUT, :]).then_inc(stored, 16)
            sp.wait_ge(stored, 16 * T // OUT)

        @block.scalar
        def _(act):
            def tick(j, u):
                if there(j):
                    b = u % 2
                    act.wait_ge(x_turned, j + 1)
                    if since(j, 2):
                        act.wait_ge(h_done, j - 1)
                    act.copy(xs_t[:, b, :, :], ps_x[b][:, :, :]).then_inc(x_copied, 1)
                j = j - 1
                if there(j):
                    b = (u - 1) % 2
                    act.wait_ge(h_done, j + 1)
                    if since(j, 2):
                        act.wait_ge(hid_ready, j - 1)
                    act.activation(act_out[:, b, :], ps_h[b][:, 0:HID], ACT.Silu).then_inc(act_done, 1)

            rolled(act, 1, tiles, BODY, tick)

        @block.vector
        def _(dve):
            dve.tensor_tensor(m.x[:, :, :], m.x[:, :, :], m.bq[:, :].unsqueeze(1).to_broadcast([P, T, D]),
                              ALU.add).then_inc(bias_added, 1)
            dve.wait_ge(bias_added, 1)

            def tick(j, u):
                if there(j - 1):
                    b = (u - 1) % 2
                    dve.wait_ge(act_done, j)
                    if since(j - 1, 2):
                        dve.wait_ge(g_turned, j - 2)
                    dve.tensor_tensor(hid[:, b, :], ps_h[b][:, HID:2 * HID], act_out[:, b, :],
                                      ALU.mult).then_inc(hid_ready, 1)
                if there(j - 2):
                    b = u % 2
                    dve.wait_ge(g_turned, j - 1)
                    if since(j - 2, 2):
                        dve.wait_ge(y_done, j - 3)
                    dve.tensor_copy(hid_t[:, b, :], ps_g[b][:, :]).then_inc(g_copied, 1)
                if there(j - 3):
                    b = (u - 3) % 2
                    dve.wait_ge(y_done, j - 2)
                    to = (u - 3) % U
                    if since(j - 3, U):
                        dve.wait_ge(y_out[to], (j - 3 - to) * (16 // U))
                    dve.tensor_copy(ys[:, to, :], ps_y[b][:, :]).then_inc(y_copied, 1)

            rolled(dve, 3, tiles, BODY, tick)
            for i in range(T):
                dve.wait_ge(tail_done, i + 1)
                dve.scalar_tensor_tensor(m.x[:, i, :], ps_h[i % 2][:, 0:D], 1.0 / (TOP1 + 1), m.x[:, i, :],
                                         ALU.mult, ALU.add).then_inc(tail_added, 1)
                dve.wait_ge(tail_added, i + 1)
                dve.wait_ge(gathered[i % YG], 16 * top * (i // YG + 1))
                for k in range(top):
                    dve.scalar_tensor_tensor(m.x[:, i, :], yg[:, i % YG, k, :], m.r["weight"][:, i, k:k + 1],
                                             m.x[:, i, :], ALU.mult, ALU.add).then_inc(summed, 1)
                    dve.wait_ge(summed, i * top + k + 1)

        @block.gpsimd
        def _(pool):
            for b in range(U):
                pool.wait_ge(y_out[b], 16 * len(range(b, tiles, U)))
            for i in range(T):
                if i >= YG:
                    pool.wait_ge(summed, (i - YG + 1) * top)
                for k in range(top):
                    pool.indirect_dma_start(out=yg[:, i % YG, k, :], out_offset=None, in_=yd,
                                            in_offset=bass.IndirectOffsetOnAxis(m.r["slot"][:, k, i:i + 1], 0)
                                            ).then_inc(gathered[i % YG], 16)

        @block.tensor
        def _(pe):
            pe.wait_ge(m.moe1_w_in, 32)

            experts = []

            def load_experts(j):
                experts[:] = nc.values_load_multi_w_load_instructions(
                    m.r["tile_e"][0:1, bass.ds(j + (EPAD - U), U + BODY)], engines=[mybir.EngineType.PE], min_val=0,
                    max_val=E - 1, skip_runtime_bounds_check_because=IN_RANGE)[1]

            def tick(j, u):
                if there(j):
                    b = u % 2
                    pe.wait_ge(x_in[u % U], (j - u % U) * (16 // U) + 16)
                    if since(j, 2):
                        pe.wait_ge(x_copied, j - 1)
                    for k in range(KH):
                        mm = pe.transpose(ps_x[b][:, k, :], xs[:, u % U, k * P:(k + 1) * P], m.ident[:, :])
                    mm.then_inc(x_turned, 1)
                if there(j - 1):
                    b = (u - 1) % 2
                    e = experts[U + u - 1]
                    pe.wait_ge(x_copied, j)
                    if since(j - 1, 2):
                        pe.wait_ge(hid_ready, j - 2)
                    for k in range(KH):
                        mm = pe.matmul(ps_h[b][:, :], xs_t[:, b, k, :], w1[:, k, bass.ds(e, 1), :],
                                       start=(k == 0), stop=(k == KH - 1))
                    mm.then_inc(h_done, 1)
                if there(j - 2):
                    b = u % 2
                    pe.wait_ge(hid_ready, j - 1)
                    if since(j - 2, 2):
                        pe.wait_ge(g_copied, j - 3)
                    pe.transpose(ps_g[b][:, :], hid[:, b, :], m.ident[:, :]).then_inc(g_turned, 1)
                if there(j - 3):
                    b = (u - 3) % 2
                    e = experts[U + u - 3]
                    pe.wait_ge(g_copied, j - 2)
                    if since(j - 3, 2):
                        pe.wait_ge(y_copied, j - 4)
                    pe.matmul(ps_y[b][:, :], hid_t[:, b, :], w2[:, bass.ds(e, 1), :],
                              start=True, stop=True).then_inc(y_done, 1)

            rolled(pe, 3, tiles, BODY, tick, load_experts)
            pe.wait_ge(m.tail_in, 16)
            pe.wait_ge(hid_ready, tiles)
            for i in range(T):
                if i >= 2:
                    pe.wait_ge(tail_added, i - 1)
                for s in range(HS // P):
                    pe.matmul(ps_h[i % 2][:, 0:D], m.hid_s[:, s, i * P:(i + 1) * P], m.ws2[:, s, :],
                              start=(s == 0), stop=False)
                for k in range(KH):
                    mm = pe.matmul(ps_h[i % 2][:, 0:D], m.xt2[:, k, i * P:(i + 1) * P], m.wq[:, k, :],
                                   start=False, stop=(k == KH - 1))
                mm.then_inc(tail_done, 1)


BEFORE_NORMS = 13
GRAM_FIRST = 8


def stage_second(nc, m, a):
    with ExitStack() as ctx:
        l = Memory(nc, ctx)
        DP = D + 1
        xn = l.sb("xn2", [P, T, DP])
        w = l.sb("w_attn", [P, KH, 3 * D])
        wr = l.sb("w_router", [P, KH, E])
        ws1 = l.sb("ws1", [P, KH, HS])
        ws3 = l.sb("ws3", [P, KH, HS])
        bias = l.sb("bias_qkv", [P, 3 * D])
        scores = l.sb("scores2", [P, T, E])
        peak = l.sb("peak", [P, T])
        gram = l.sb("gram", [P, KH, DP])
        sums = l.sb("sums", [P, KH, P])
        prod = l.sb("prod", [P, KH, 3 * D])
        square = l.sb("square", [P, 2 * D])
        root = l.sb("root", [P, 2 * D])
        kv = l.sb("kv", [P, D])
        t1, t2 = l.sb("t1", [P, 2 * D]), l.sb("t2", [P, D])
        bq = m.bq
        gate = l.sb("gate", [P, 2, CH])
        xt, hid, wq = m.xt2, m.hid_s, m.wq
        ps_t = [l.ps(f"ps_t2{b}", [P, CH]) for b in range(2)]
        ps_g = [l.ps(f"ps_gram{b}", [P, DP]) for b in range(KH)]
        ps_l = l.ps("ps_l2", [P, T, E])
        ps_ab = [l.ps(f"ps_ab{b}", [P, CH]) for b in range(2)]
        ps_o = l.ps("ps_o2", [P, 2, D])
        wo = l.sb("wo", [P, KH, D])
        rec = l.sb("rec", [P, 2, NH])
        heads = l.sb("heads", [P, 2, NH, HD])
        heads_t = l.sb("heads_t", [P, 2, KH, P])
        ps_turn = [b[:, :].rearrange("p (g t) -> p g t", g=NG) for b in ps_ab]
        ps_back = [b[:, 0:D].rearrange("p (k t) -> p k t", k=KH) for b in ps_g]
        ps_w = ps_o[:, 0, :]
        wo_in, turned, rec_ready = l.sem("c_wo_in"), l.sem("c_turned"), l.sem("c_rec_ready")
        heads_ready, back, back_copied = l.sem("c_heads_ready"), l.sem("c_back"), l.sem("c_back_copied")
        w_done, added = l.sem("c_w_done"), l.sem("c_added")
        stat, r = m.stat, dict(m.r)
        w_in, b_in, s_in = l.sem("e_w_in"), l.sem("e_b_in"), l.sem("e_s_in")
        std_wanted, std_ready, step_sem = l.sem("e_std_wanted"), l.sem("e_std_ready"), l.sem("e_dve")
        ones_ready = l.sem("e_ones_ready")
        xn_ready, t_done, xt_ready, l_done = l.sem("e_xn_ready"), l.sem("e_t_done"), l.sem("e_xt_ready"), l.sem("e_l_done")
        logit_ready, exp_ready = l.sem("e_logit_ready"), l.sem("e_exp_ready")
        masks_ready, ranks_ready, slots_ready = l.sem("e_masks_ready"), l.sem("e_ranks_ready"), l.sem("e_slots_ready")
        dispatched = l.sem("e_dispatched")
        gram_done, gram_copied = l.sem("e_gram_done"), l.sem("e_gram_copied")
        gw_done, prod_ready, norms_done = l.sem("e_gw_done"), l.sem("e_prod_ready"), l.sem("e_norms_done")
        norms_read = l.sem("e_norms_read")
        square_ready, root_ready = l.sem("e_square_ready"), l.sem("e_root_ready")
        a_done, gate_ready, b_done, hid_ready = l.sem("e_a_done"), l.sem("e_gate_ready"), l.sem("e_b_done"), l.sem("e_hid_ready")
        ab = [ps_ab, ps_t]
        r["ps_rank"], r["ps_count"] = ps_o[:, 0, :], ps_o[:, 1, :]
        block = ctx.enter_context(nc.Block())
        units = [(c, s) for c in range(C) for s in range(HS // P)]

        @block.sync
        def _(sp):
            sp.dma_start(wo[:, :, :], a["w_o_t"].rearrange("(k p) o -> p k o", p=P)).then_inc(wo_in, 16)
            sp.dma_start(w[:, :, :], a["w_attn"].rearrange("(k p) o -> p k o", p=P)).then_inc(w_in, 16)
            sp.dma_start(wr[:, :, :], a["w_router"].rearrange("(k p) e -> p k e", p=P)).then_inc(w_in, 16)
            sp.dma_start(bias[:, :], a["b_attn"].unsqueeze(0).to_broadcast([P, 3 * D])).then_inc(b_in, 16)
            sp.dma_start(ws1[:, :, :], a["ws1"].rearrange("(k p) o -> p k o", p=P)).then_inc(s_in, 16)
            sp.dma_start(ws3[:, :, :], a["ws3"].rearrange("(k p) o -> p k o", p=P)).then_inc(s_in, 16)
            sp.dma_start(m.ws2[:, :, :], a["ws2"].rearrange("(k p) o -> p k o", p=P)).then_inc(m.tail_in, 16)
            sp.dma_start(m.w13[:, :, :, :], a["we13"].rearrange("(k p) (e h) -> p k e h", p=P, e=E)).then_inc(m.moe1_w_in, 16)
            sp.dma_start(m.we2[:, :, :], a["we2"].rearrange("e p d -> p e d")).then_inc(m.moe1_w_in, 16)

        @block.gpsimd
        def _(pool):
            pool.memset(xn[:, :, D:DP], 1.0).then_inc(ones_ready, 1)
            pool.wait_ge(m.cleared[1], 16 * -(-NT1 // CLEAR))
            for k in range(TOP1):
                pool.wait_ge(slots_ready, k + 1)
                for i in range(T):
                    pool.indirect_dma_start(out=m.xd1, out_offset=bass.IndirectOffsetOnAxis(r["slot"][:, k, i:i + 1], 0),
                                            in_=xn[:, i, 0:D], in_offset=None).then_inc(dispatched, 16)
            pool.wait_ge(dispatched, 16 * TOP1 * T)

        @block.scalar
        def _(act):
            def root_of(c):
                act.wait_ge(std_wanted, c + 1)
                act.activation(stat["std"][:, c * TC:(c + 1) * TC], stat["var"][:, c * TC:(c + 1) * TC],
                               ACT.Sqrt).then_inc(std_ready, 1)

            def copy_turned(c, tiles):
                for i in tiles:
                    i += c * TC
                    act.wait_ge(t_done, i + 1)
                    act.copy(xt[:, :, i * P:(i + 1) * P],
                             ps_t[i % 2][:, 0:D].rearrange("p (k t) -> p k t", k=KH)).then_inc(xt_ready, 1)

            for i in range(T + 1):
                if i < T:
                    act.wait_ge(back, i + 1)
                    if i >= 2:
                        act.wait_ge(w_done, i - 1)
                    act.copy(heads_t[:, i % 2, :, :], ps_back[i % 2]).then_inc(back_copied, 1)
                if i and i % TC == 0:
                    c = i // TC - 1
                    if c:
                        copy_turned(c - 1, range(2))
                    root_of(c)
                    if c:
                        copy_turned(c - 1, range(2, TC))
            copy_turned(C - 1, range(TC))
            act.wait_ge(logit_ready, 1)
            act.activation(scores[:, :, :], scores[:, :, :], ACT.Exp).then_inc(exp_ready, 1)
            act.wait_ge(gram_done, 1)
            for k in range(KH):
                act.copy(gram[:, k, :], ps_g[k][:, :]).then_inc(gram_copied, 1)
            for n in range(len(units)):
                if n == BEFORE_NORMS:
                    act.wait_ge(square_ready, 1)
                    act.activation(root[:, :], square[:, :], ACT.Sqrt).then_inc(root_ready, 1)
                act.wait_ge(a_done, n + 1)
                if n >= 2:
                    act.wait_ge(hid_ready, n - 1)
                act.activation(gate[:, n % 2, :], ab[n % 2][0][:, :], ACT.Silu).then_inc(gate_ready, 1)

        @block.vector
        def _(dve):
            step = Steps(dve, step_sem)
            def normalize(i):
                dve.wait_ge(turned, i + 1)
                if i >= 2:
                    dve.wait_ge(back, i - 1)
                    dve.wait_ge(heads_ready, i - 1)
                by_head = ps_turn[i % 2].rearrange("p g (h w) -> p (g h) w", w=32)
                dve.reciprocal(rec[:, i % 2, :], by_head[:, :, HD]).then_inc(rec_ready, 1)
                dve.wait_ge(rec_ready, i + 1)
                dve.tensor_tensor(heads[:, i % 2, :, :], by_head[:, :, 0:HD],
                                  rec[:, i % 2, :].unsqueeze(2).to_broadcast([P, NH, HD]),
                                  ALU.mult).then_inc(heads_ready, 1)

            for i in range(T + 2):
                if i < T:
                    normalize(i)
                if i >= 2:
                    dve.wait_ge(w_done, i - 1)
                    dve.tensor_tensor(m.x[:, i - 2, :], ps_w, m.x[:, i - 2, :], ALU.add).then_inc(added, 1)
                    dve.wait_ge(added, i - 1)
                    step.then(dve.bn_stats(stat["bn"][:, i - 2, :], m.x[:, i - 2, :]))
                    step.then(dve.bn_aggr(stat["mv"][:, i - 2, :], stat["bn"][:, i - 2, :]))
                    if (i - 1) % TC == 0:
                        cs = slice(i - 1 - TC, i - 1)
                        dve.tensor_scalar(stat["var"][:, cs], stat["mv"][:, cs, 1], EPS, None,
                                          ALU.add).then_inc(std_wanted, 1)
                if i >= TC + 2 and (i - 2) % TC == 0:
                    inverse_deviation(dve, step, stat, (i - 2) // TC - 1, std_wanted, std_ready)
                if i >= TC + 2 and (i - 2) % TC < 2:
                    first = (i - 2) // TC * TC - TC + (i - 2) % TC * 2
                    normalized(dve, step, m.x, xn, stat, first)
                    normalized(dve, step, m.x, xn, stat, first + 1)
                    if first % TC:
                        step.sync()
                        dve.sem_inc(xn_ready, 1)
            inverse_deviation(dve, step, stat, C - 1, std_wanted, std_ready)
            for i in range(T - TC, T):
                normalized(dve, step, m.x, xn, stat, i)
            step.sync()
            dve.sem_inc(xn_ready, 1)
            dve.wait_ge(l_done, T)
            step.then(dve.tensor_reduce(peak[:, :], ps_l[:, :, :], AX_X, ALU.max))
            dve.tensor_tensor(scores[:, :, :], ps_l[:, :, :], peak[:, :].unsqueeze(2).to_broadcast([P, T, E]),
                              ALU.subtract).then_inc(logit_ready, 1)
            dve.wait_ge(exp_ready, 1)
            step.then(dve.tensor_reduce(peak[:, :], scores[:, :, :], AX_X, ALU.add))
            step.then(dve.reciprocal(peak[:, :], peak[:, :]))
            step.then(dve.tensor_tensor(scores[:, :, :], scores[:, :, :],
                                        peak[:, :].unsqueeze(2).to_broadcast([P, T, E]), ALU.mult))
            for _ in route(dve, step, r, scores, TOP1, NT1, 0.0, TOP1 / (TOP1 + 1), masks_ready, ranks_ready, slots_ready):
                pass

            def gated(n):
                c, s = units[n]
                dve.wait_ge(gate_ready, n + 1)
                dve.wait_ge(b_done, n + 1)
                dve.tensor_tensor(hid[:, s, c * CH:(c + 1) * CH], ab[n % 2][1][:, :], gate[:, n % 2, :],
                                  ALU.mult).then_inc(hid_ready, 1)

            for n in range(BEFORE_NORMS):
                gated(n)
            dve.wait_ge(gram_copied, KH)
            for k in range(KH):
                dve.tensor_copy(sums[:, k, :], gram[:, k, D:DP].to_broadcast([P, P])).then_inc(gram_copied, 1)
            dve.wait_ge(b_in, 16)
            for k in range(KH):
                dve.wait_ge(gw_done, k + 1)
                step(dve.tensor_tensor(prod[:, k, 0:2 * D], ps_t[k][:, :], w[:, k, 0:2 * D], ALU.mult))
                step(dve.tensor_tensor(prod[:, k, 2 * D:3 * D], ps_t[k][:, D:2 * D], w[:, k, 2 * D:3 * D], ALU.mult))
            step.sync()
            dve.sem_inc(prod_ready, 1)
            bqk, bk, bv = bias[:, 0:2 * D], bias[:, D:2 * D], bias[:, 2 * D:3 * D]
            dve.wait_ge(norms_done, 1)
            step.then(dve.tensor_scalar(t1[:, :], bqk, float(S), None, ALU.mult))
            step.then(dve.scalar_tensor_tensor(t1[:, :], ps_ab[1][:, :], 2.0, t1[:, :], ALU.mult, ALU.add))
            step.then(dve.tensor_tensor(t1[:, :], t1[:, :], bqk, ALU.mult))
            dve.tensor_tensor(square[:, :], ps_ab[0][:, :], t1[:, :], ALU.add).then_inc(square_ready, 1)
            step.then(dve.scalar_tensor_tensor(kv[:, :], bv, float(S), ps_o[:, 1, :], ALU.mult, ALU.add))
            step.then(dve.tensor_tensor(kv[:, :], kv[:, :], bk, ALU.mult))
            step.then(dve.tensor_tensor(t2[:, :], ps_ab[1][:, D:2 * D], bv, ALU.mult))
            step.then(dve.tensor_tensor(kv[:, :], kv[:, :], t2[:, :], ALU.add))
            dve.tensor_tensor(kv[:, :], ps_o[:, 0, :], kv[:, :], ALU.add).then_inc(norms_read, 1)
            dve.wait_ge(norms_read, 1)
            dve.wait_ge(square_ready, 1)
            dve.wait_ge(root_ready, 1)
            step.then(dve.tensor_tensor(t2[:, :], root[:, 0:D], root[:, D:2 * D], ALU.mult))
            step.then(dve.reciprocal(t2[:, :], t2[:, :]))
            step.then(dve.tensor_tensor(t1[:, 0:D], square[:, 0:D], t2[:, :], ALU.mult))
            step.then(dve.tensor_tensor(t1[:, D:2 * D], square[:, D:2 * D], t2[:, :], ALU.mult))
            step.then(dve.tensor_tensor(t1[:, 0:D], t1[:, 0:D], t1[:, D:2 * D], ALU.mult))
            step.then(dve.tensor_scalar(t1[:, 0:D], t1[:, 0:D], -0.5, 1.5, ALU.mult, ALU.add))
            step.then(dve.tensor_tensor(t2[:, :], t2[:, :], t1[:, 0:D], ALU.mult))
            step.then(dve.tensor_tensor(kv[:, :], kv[:, :], t2[:, :], ALU.mult))
            step(dve.tensor_tensor(bq[:, :], bias[:, 0:D], kv[:, :], ALU.mult))
            step.then(dve.tensor_scalar(t2[:, :], kv[:, :], float(TOP1 + 1), None, ALU.mult))
            step(dve.tensor_tensor(wq[:, :, :], w[:, :, 0:D], t2[:, :].unsqueeze(1).to_broadcast([P, KH, D]), ALU.mult))
            step.sync()
            for n in range(BEFORE_NORMS, len(units)):
                gated(n)

        @block.tensor
        def _(pe):
            def turn_and_score(c):
                pe.wait_ge(xn_ready, c + 1)
                for i in range(c * TC, (c + 1) * TC):
                    if i >= 2:
                        pe.wait_ge(xt_ready, i - 1)
                    for k in range(KH):
                        mm = pe.transpose(ps_t[i % 2][:, k * P:(k + 1) * P], xn[:, i, k * P:(k + 1) * P], m.ident[:, :])
                    mm.then_inc(t_done, 1)
                for i in range(c * TC, (c + 1) * TC):
                    pe.wait_ge(xt_ready, i + 1)
                    for k in range(KH):
                        mm = pe.matmul(ps_l[:, i, :], xt[:, k, i * P:(i + 1) * P], wr[:, k, :],
                                       start=(k == 0), stop=(k == KH - 1))
                    mm.then_inc(l_done, 1)

            for i in range(T + 2):
                if i < T:
                    if i >= 2:
                        pe.wait_ge(heads_ready, i - 1)
                    for g in range(NG):
                        mm = pe.transpose(ps_turn[i % 2][:, g, :], m.o_t[:, g, i * P:(i + 1) * P], m.ident[:, :])
                    mm.then_inc(turned, 1)
                if 1 <= i <= T:
                    j = i - 1
                    pe.wait_ge(heads_ready, j + 1)
                    if j >= 2:
                        pe.wait_ge(back_copied, j - 1)
                    for k in range(KH):
                        mm = pe.transpose(ps_back[j % 2][:, k, :],
                                          heads[:, j % 2, k * NH // KH:(k + 1) * NH // KH, :].rearrange("p h d -> p (h d)"),
                                          m.ident[:, :])
                    mm.then_inc(back, 1)
                if i >= 2:
                    j = i - 2
                    if j == 0:
                        pe.wait_ge(wo_in, 16)
                    else:
                        pe.wait_ge(added, j)
                    pe.wait_ge(back_copied, j + 1)
                    for k in range(KH):
                        mm = pe.matmul(ps_w, heads_t[:, j % 2, k, :], wo[:, k, :],
                                       start=(k == 0), stop=(k == KH - 1))
                    mm.then_inc(w_done, 1)
                    if (j + 1) % TC == 0 and j >= TC:
                        if j < 2 * TC:
                            pe.wait_ge(w_in, 32)
                            pe.wait_ge(ones_ready, 1)
                        turn_and_score(j // TC - 1)
            turn_and_score(C - 1)
            for i in range(T):
                for k in range(KH):
                    mm = pe.matmul(ps_g[k][:, :], xn[:, i, k * P:(k + 1) * P], xn[:, i, :],
                                   start=(i == 0), stop=(i == T - 1))
                if i == GRAM_FIRST:
                    route_ranks(pe, r, masks_ready, ranks_ready)
            mm.then_inc(gram_done, 1)
            pe.wait_ge(s_in, 32)
            def shared(n):
                c, s = units[n]
                if n >= 2:
                    pe.wait_ge(gate_ready, n - 1)
                for k in range(KH):
                    mm = pe.matmul(ab[n % 2][0][:, :], ws1[:, k, s * P:(s + 1) * P], xt[:, k, c * CH:(c + 1) * CH],
                                   start=(k == 0), stop=(k == KH - 1))
                mm.then_inc(a_done, 1)
                if n >= 2:
                    pe.wait_ge(hid_ready, n - 1)
                for k in range(KH):
                    mm = pe.matmul(ab[n % 2][1][:, :], ws3[:, k, s * P:(s + 1) * P], xt[:, k, c * CH:(c + 1) * CH],
                                   start=(k == 0), stop=(k == KH - 1))
                mm.then_inc(b_done, 1)

            for n in range(BEFORE_NORMS):
                shared(n)
            pe.wait_ge(hid_ready, BEFORE_NORMS)
            pe.wait_ge(gram_copied, 2 * KH)
            for k in range(KH):
                for j in range(KH):
                    mm = pe.matmul(ps_t[k][:, :], gram[:, j, k * P:(k + 1) * P], w[:, j, 0:2 * D],
                                   start=(j == 0), stop=(j == KH - 1))
                mm.then_inc(gw_done, 1)
            for k in range(KH):
                pe.matmul(ps_ab[1][:, :], sums[:, k, :], w[:, k, 0:2 * D], start=(k == 0), stop=(k == KH - 1))
            pe.wait_ge(slots_ready, 1)
            for k in range(KH):
                pe.matmul(ps_o[:, 1, :], sums[:, k, :], w[:, k, 2 * D:3 * D], start=(k == 0), stop=(k == KH - 1))
            pe.wait_ge(prod_ready, 1)
            for k in range(KH):
                pe.matmul(ps_ab[0][:, :], m.ones_f[:, :], prod[:, k, 0:2 * D], start=(k == 0), stop=(k == KH - 1))
            for k in range(KH):
                mm = pe.matmul(ps_o[:, 0, :], m.ones_f[:, :], prod[:, k, 2 * D:3 * D],
                               start=(k == 0), stop=(k == KH - 1))
            mm.then_inc(norms_done, 1)
            shared(BEFORE_NORMS)
            pe.wait_ge(norms_read, 1)
            pe.wait_ge(square_ready, 1)
            for n in range(BEFORE_NORMS + 1, len(units)):
                shared(n)


def two_layers(nc, a, out):
    with ExitStack() as ctx:
        m = Memory(nc, ctx)
        common(nc, m)
        m.cleared = [m.sem(f"cleared{layer}") for layer in range(2)]
        m.o_t = m.sb("o_t", [P, NG, S])
        with ExitStack() as attention:
            l = Memory(nc, attention)
            m.xn = m.o_t[:, NG // 2:NG, :].rearrange("p g (i d) -> p (g i) d", d=D)
            m.v_all = l.sb("v_all", [P, T, NH, HD + 1])
            m.qs = [l.sb(f"qs{c}", [MROWS, HG, CH], BF16) for c in range(C)]
            m.ks = [l.sb(f"ks{b}", [MROWS, HG, S], BF16) for b in range(2)]
            m.w1 = l.sb("moe0_w1", [P, KH, E, HID])
            m.w2 = l.sb("moe0_w2", [P, E, D])
            m.zeros = l.sb("zeros", [P, D])
            m.zero16 = l.sb("zero16", [P, P], BF16)
            m.parts_out = [l.sem(f"parts_out{n}") for n in range(4 * C)]
            m.first_in = [l.sem(f"first_in{c}") for c in range(C)]
            m.moe0_w_in = l.sem("moe0_w_in")
            stage_project(nc, m, a)
            stage_attention(nc, m)
        m.xt2 = m.sb("xt2", [P, KH, S])
        m.hid_s = m.o_t
        m.bq = m.sb("bq", [P, D])
        m.w13 = m.sb("w13", [P, KH, E, 2 * HID])
        m.we2 = m.sb("we2", [P, E, D])
        m.ws2 = m.sb("ws2", [P, HS // P, D])
        m.wq = m.sb("wq", [P, KH, D])
        m.tail_in, m.moe1_w_in = m.sem("tail_in"), m.sem("moe1_w_in")
        stage_second(nc, m, a)
        stage_experts(nc, m, out)


def kernel(L0_attn_hidden_states, L0_attn_w_qkv, L0_attn_w_o, L0_ffn_Wg, L0_ffn_balance_bias, L0_ffn_W1, L0_ffn_W2,
           L1_attn_W, L1_attn_b, L1_ffn_w_router, L1_ffn_we1, L1_ffn_we3, L1_ffn_we2, L1_ffn_ws1, L1_ffn_ws3,
           L1_ffn_ws2):
    import numpy as np
    import concourse.bacc as bacc
    from concourse.bass_utils import run_bass_kernel_spmd

    def experts_last(w):
        return w.transpose(1, 0, 2).reshape(w.shape[1], -1)

    arrays = {
        "x": L0_attn_hidden_states, "w_qkv_t": L0_attn_w_qkv.T, "w_o_t": L0_attn_w_o.T, "wg_t": L0_ffn_Wg.T,
        "balance_bias": L0_ffn_balance_bias, "w1": experts_last(np.asarray(L0_ffn_W1)), "w2": L0_ffn_W2,
        "w_attn": L1_attn_W, "b_attn": L1_attn_b, "w_router": L1_ffn_w_router,
        "we13": experts_last(np.concatenate([np.asarray(L1_ffn_we1), np.asarray(L1_ffn_we3)], axis=2)),
        "we2": L1_ffn_we2, "ws1": L1_ffn_ws1, "ws3": L1_ffn_ws3, "ws2": L1_ffn_ws2,
    }
    arrays = {name: np.ascontiguousarray(v) for name, v in arrays.items()}
    nc = bacc.Bacc("TRN2", target_bir_lowering=False, num_devices=1)
    a = {name: nc.dram_tensor(f"in_{name}", v.shape, mybir.dt.from_np(v.dtype), kind="ExternalInput").ap()
         for name, v in arrays.items()}
    out = nc.dram_tensor("out", (1, S, D), F32, kind="ExternalOutput").ap()
    two_layers(nc, a, out)
    result = run_bass_kernel_spmd(nc, [{f"in_{name}": v for name, v in arrays.items()}], core_ids=[0])
    return result.results[0]["out"]
```
